# Optimizing a Trainium2 kernel written in Bass

```python
import numpy as np
import jax
import jax.numpy as jnp

def _softmax(x, axis=-1):
    return jax.nn.softmax(x, axis=axis)

def _gelu(x):
    return jax.nn.gelu(x, approximate=True)

def _silu(x):
    return jax.nn.silu(x)

def _sigmoid(x):
    return jax.nn.sigmoid(x)

def _layernorm(x, axis=-1, eps=1e-05):
    m = jnp.mean(x, axis=axis, keepdims=True)
    v = jnp.var(x, axis=axis, keepdims=True)
    return (x - m) / jnp.sqrt(v + eps)

def _scatter_add(tgt, idx, src, axis=0):
    return tgt.at[idx].add(src)

def _segment_sum(src, seg, n):
    return jax.ops.segment_sum(src, seg, n)
kernel_name = 'mk_cond_resid_d2_seqx_r8_a7a738'

def setup_inputs(seed: int=0):
    np.random.seed(seed)
    _w = jnp.asarray

    def _rec_inputs():
        import jax
        import jax.numpy as jnp
        _rk = jax.random.key(seed)
        x = 7.22e-05 + 1 * jax.random.normal(jax.random.fold_in(_rk, 1), (32, 128, 128), jnp.float32)
        _lenS = 128 - jax.random.randint(jax.random.fold_in(_rk, 7), (32,), 0, max(1, 128 // 4) + 1, jnp.int32)
        _lenS2 = 128 - jax.random.randint(jax.random.fold_in(_rk, 8), (32,), 0, max(1, 128 // 4) + 1, jnp.int32)
        condB_tauraws = -5.74692 + 0.777674 * jax.random.normal(jax.random.fold_in(_rk, 11), (32,), jnp.float32)
        cond_256 = -0.000235209 + 0.019331 * jax.random.normal(jax.random.fold_in(_rk, 12), (32, 32), jnp.float32)
        condB_bn2 = jnp.zeros((32,), jnp.float32)
        cond_1024 = -4.10585e-05 + 0.0199478 * jax.random.normal(jax.random.fold_in(_rk, 14), (32, 128), jnp.float32)
        itok_Sx32_0_1023 = jax.random.randint(jax.random.fold_in(_rk, 16), (128, 32), 0, 128, jnp.int32)
        condB_uprev = -0.456674 + 0.753242 * jax.random.normal(jax.random.fold_in(_rk, 18), (32,), jnp.float32)
        _validS = jnp.arange(128)[None, :] < _lenS[:, None]
        _validS2 = jnp.arange(128)[None, :] < _lenS2[:, None]
        _causal = jnp.tril(jnp.ones((128, 128), dtype=bool))
        mask_SxS_bk0 = jnp.logical_not(jnp.broadcast_to(_validS[0:1, :], (128, 128)))
        mask_Sx32_bk1 = jnp.ones((128, 32), dtype=bool)
        return (x, condB_tauraws, cond_256, condB_bn2, cond_1024, itok_Sx32_0_1023, condB_uprev, mask_SxS_bk0, mask_Sx32_bk1)
    x, condB_tauraws, cond_256, condB_bn2, cond_1024, itok_Sx32_0_1023, condB_uprev, mask_SxS_bk0, mask_Sx32_bk1 = _rec_inputs()

    def _L0_cond_setup():
        import jax, jax.numpy as jnp
        import numpy as np
        import math
        B, T, E, D = (4, 256, 128, 4)

        def _tau_init(t):
            a = 0.1 ** (1.0 / max(t - 1, 1))
            tt = -math.log(max(a, 1e-10))
            return math.log(math.exp(tt) - 1 + 1e-10)

        def causal_ema(b, tau_raw):
            alpha = jnp.exp(-jax.nn.softplus(tau_raw)).astype(b.dtype)

            def step(h, bt):
                h = alpha * h + bt
                return (h, h)
            h0 = jnp.zeros((b.shape[0], b.shape[2]), b.dtype)
            _, hs = jax.lax.scan(step, h0, jnp.swapaxes(b, 0, 1))
            return jnp.swapaxes(hs, 0, 1)
        key = jax.random.key(seed)
        ks = jax.random.split(key, 10)
        s = 0.02
        return {'x': jax.random.normal(ks[0], (B, T, E), jnp.float32), 'tau_ctx': jnp.float32(_tau_init(max(T // 2, 4))), 'tau_raws': jnp.array([_tau_init(max(T // 2 ** i, 2)) for i in range(D)], jnp.float32), 'Wg': jax.random.normal(ks[1], (E, 2 * E), jnp.float32) * s, 'bg': jnp.full((E,), -0.5, jnp.float32), 'Wn1': jax.random.normal(ks[2], (E // 4, E), jnp.float32) * s, 'bn1': jnp.zeros((E // 4,), jnp.float32), 'Wn2': jax.random.normal(ks[3], (D, E // 4), jnp.float32) * s, 'bn2': jnp.zeros((D,), jnp.float32), 'blend': jax.random.normal(ks[4], (D, E), jnp.float32) * s, 'Wsoma': jax.random.normal(ks[5], (E, E), jnp.float32) * s, 'bsoma': jnp.zeros((E,), jnp.float32), 'Wtemp': jax.random.normal(ks[6], (E, E), jnp.float32) * s, 'btemp': jnp.zeros((E,), jnp.float32), 'Wout': jax.random.normal(ks[7], (E, E), jnp.float32) * s, 'gamma': jnp.ones((E,), jnp.float32), 'beta': jnp.zeros((E,), jnp.float32)}
    _L0_cond_all = _L0_cond_setup()
    _L0_cond_in = {k: v for k, v in _L0_cond_all.items() if k in ('tau_ctx', 'Wg', 'bg', 'Wn1', 'bn1', 'Wsoma', 'bsoma', 'Wtemp', 'btemp', 'Wout', 'gamma', 'beta')}
    del _L0_cond_all

    def _L1_cond_setup():
        import jax, jax.numpy as jnp
        import numpy as np
        B, S, D, H = (4, 128, 128, 16)
        DH = D // H
        K_SPARSE = 32
        LAMBDA_MAX, ALPHA = (10.0, 5.0)
        SPARSE_THRESHOLD = 1.0
        key = jax.random.key(seed)
        ks = jax.random.split(key, 12)
        x = jax.random.normal(ks[0], (B, S, D), dtype=jnp.float32)
        prior_mask = jax.random.bernoulli(ks[1], 0.1, (S, S))
        prior_indices = jax.random.randint(ks[2], (S, K_SPARSE), 0, S)
        prior_index_mask = jax.random.bernoulli(ks[3], 0.9, (S, K_SPARSE))
        prior_index_mask = prior_index_mask.at[:, 0].set(True)
        u_prev = jax.random.normal(ks[4], (B, 1), dtype=jnp.float32)
        sc = 1.0 / np.sqrt(D)
        Wq = jax.random.normal(ks[5], (D, D), dtype=jnp.float32) * sc
        Wk = jax.random.normal(ks[6], (D, D), dtype=jnp.float32) * sc
        Wv = jax.random.normal(ks[7], (D, D), dtype=jnp.float32) * sc
        Wo = jax.random.normal(ks[8], (D, D), dtype=jnp.float32) * sc
        bq = jnp.zeros((D,), jnp.float32)
        bk = jnp.zeros((D,), jnp.float32)
        bv = jnp.zeros((D,), jnp.float32)
        bo = jnp.zeros((D,), jnp.float32)
        return {'x': x, 'prior_mask': prior_mask, 'prior_indices': prior_indices, 'prior_index_mask': prior_index_mask, 'u_prev': u_prev, 'Wq': Wq, 'bq': bq, 'Wk': Wk, 'bk': bk, 'Wv': Wv, 'bv': bv, 'Wo': Wo, 'bo': bo}
    _L1_cond_all = _L1_cond_setup()
    _L1_cond_in = {k: v for k, v in _L1_cond_all.items() if k in ('Wq', 'bq', 'Wk', 'bk', 'Wv', 'bv', 'Wo', 'bo')}
    del _L1_cond_all
    return {'x': x, 'condB_tauraws': condB_tauraws, 'cond_256': cond_256, 'condB_bn2': condB_bn2, 'cond_1024': cond_1024, 'itok_Sx32_0_1023': itok_Sx32_0_1023, 'condB_uprev': condB_uprev, 'mask_SxS_bk0': mask_SxS_bk0, 'mask_Sx32_bk1': mask_Sx32_bk1, 'L0_cond_tau_ctx': _L0_cond_in['tau_ctx'], 'L0_cond_Wg': _L0_cond_in['Wg'], 'L0_cond_bg': _L0_cond_in['bg'], 'L0_cond_Wn1': _L0_cond_in['Wn1'], 'L0_cond_bn1': _L0_cond_in['bn1'], 'L0_cond_Wsoma': _L0_cond_in['Wsoma'], 'L0_cond_bsoma': _L0_cond_in['bsoma'], 'L0_cond_Wtemp': _L0_cond_in['Wtemp'], 'L0_cond_btemp': _L0_cond_in['btemp'], 'L0_cond_Wout': _L0_cond_in['Wout'], 'L0_cond_gamma': _L0_cond_in['gamma'], 'L0_cond_beta': _L0_cond_in['beta'], 'L1_cond_Wq': _L1_cond_in['Wq'], 'L1_cond_bq': _L1_cond_in['bq'], 'L1_cond_Wk': _L1_cond_in['Wk'], 'L1_cond_bk': _L1_cond_in['bk'], 'L1_cond_Wv': _L1_cond_in['Wv'], 'L1_cond_bv': _L1_cond_in['bv'], 'L1_cond_Wo': _L1_cond_in['Wo'], 'L1_cond_bo': _L1_cond_in['bo']}

def reference(x, condB_tauraws, cond_256, condB_bn2, cond_1024, itok_Sx32_0_1023, condB_uprev, mask_SxS_bk0, mask_Sx32_bk1, L0_cond_tau_ctx, L0_cond_Wg, L0_cond_bg, L0_cond_Wn1, L0_cond_bn1, L0_cond_Wsoma, L0_cond_bsoma, L0_cond_Wtemp, L0_cond_btemp, L0_cond_Wout, L0_cond_gamma, L0_cond_beta, L1_cond_Wq, L1_cond_bq, L1_cond_Wk, L1_cond_bk, L1_cond_Wv, L1_cond_bv, L1_cond_Wo, L1_cond_bo):
    import jax
    import jax.numpy as jnp

    def _L0_cond_ref(x, tau_ctx, tau_raws, Wg, bg, Wn1, bn1, Wn2, bn2, blend, Wsoma, bsoma, Wtemp, btemp, Wout, gamma, beta):
        import jax, jax.numpy as jnp
        import numpy as np
        import math
        B, T, E, D = (4, 256, 128, 4)

        def _tau_init(t):
            a = 0.1 ** (1.0 / max(t - 1, 1))
            tt = -math.log(max(a, 1e-10))
            return math.log(math.exp(tt) - 1 + 1e-10)

        def causal_ema(b, tau_raw):
            alpha = jnp.exp(-jax.nn.softplus(tau_raw)).astype(b.dtype)

            def step(h, bt):
                h = alpha * h + bt
                return (h, h)
            h0 = jnp.zeros((b.shape[0], b.shape[2]), b.dtype)
            _, hs = jax.lax.scan(step, h0, jnp.swapaxes(b, 0, 1))
            return jnp.swapaxes(hs, 0, 1)
        ctx = causal_ema(x, tau_ctx)
        gate_in = jnp.concatenate([x, ctx], axis=-1)
        wg = jax.nn.sigmoid(jnp.einsum('btc,ec->bte', gate_in, Wg) + bg)
        gated = x * wg
        h1 = jax.nn.gelu(jnp.einsum('btc,hc->bth', x, Wn1) + bn1, approximate=False)
        mod = 0.5 + jax.nn.sigmoid(jnp.einsum('bth,dh->btd', h1, Wn2) + bn2)
        traces = jax.vmap(lambda tau, m: causal_ema(gated * m[..., None], tau))(tau_raws, jnp.moveaxis(mod, -1, 0))
        blend_w = jax.nn.softmax(blend, axis=0)
        temporal = jnp.einsum('dbtc,dc->btc', traces, blend_w)
        gate = jax.nn.sigmoid(jnp.einsum('btc,ec->bte', temporal, Wtemp) + btemp)
        soma = jax.nn.gelu(jnp.einsum('btc,ec->bte', x, Wsoma) + bsoma, approximate=False)
        out = jnp.einsum('btc,ec->bte', soma * gate, Wout)
        mu = out.mean(-1, keepdims=True)
        var = out.var(-1, keepdims=True)
        return (out - mu) / jnp.sqrt(var + 1e-05) * gamma + beta

    def _L1_cond_ref(x, prior_mask, prior_indices, prior_index_mask, u_prev, Wq, bq, Wk, bk, Wv, bv, Wo, bo):
        import jax, jax.numpy as jnp
        import numpy as np
        B, S, D, H = (4, 128, 128, 16)
        DH = D // H
        K_SPARSE = 32
        LAMBDA_MAX, ALPHA = (10.0, 5.0)
        SPARSE_THRESHOLD = 1.0
        Bb, Ss, Dd = x.shape
        scale = 1.0 / jnp.sqrt(jnp.asarray(DH, x.dtype))

        def proj(W, b):
            return (x @ W.T + b).reshape(Bb, Ss, H, DH).transpose(0, 2, 1, 3)
        Q, K, V = (proj(Wq, bq), proj(Wk, bk), proj(Wv, bv))
        lam = LAMBDA_MAX * jnp.exp(-ALPHA * u_prev.reshape(Bb))
        use_sparse = lam >= SPARSE_THRESHOLD
        scores = jnp.einsum('bhqd,bhkd->bhqk', Q, K) * scale
        prior_bias = jnp.where(prior_mask[:Ss, :Ss], 0.0, -1.0).astype(x.dtype)
        bias = lam[:, None, None, None] * prior_bias[None, None]
        dense_out = jnp.einsum('bhqk,bhkd->bhqd', jax.nn.softmax(scores + bias, axis=-1), V)
        idx = prior_indices[:Ss]
        Kg = K[:, :, idx]
        Vg = V[:, :, idx]
        s_scores = jnp.einsum('bhsd,bhskd->bhsk', Q, Kg) * scale
        s_scores = jnp.where(prior_index_mask[:Ss][None, None], s_scores, jnp.asarray(-jnp.inf, x.dtype))
        sparse_out = jnp.einsum('bhsk,bhskd->bhsd', jax.nn.softmax(s_scores, axis=-1), Vg)
        out = jnp.where(use_sparse[:, None, None, None], sparse_out, dense_out)
        out = out.transpose(0, 2, 1, 3).reshape(Bb, Ss, Dd)
        return out @ Wo.T + bo
    x = x + _L0_cond_ref(x, L0_cond_tau_ctx, condB_tauraws, L0_cond_Wg, L0_cond_bg, L0_cond_Wn1, L0_cond_bn1, cond_256, condB_bn2, cond_1024, L0_cond_Wsoma, L0_cond_bsoma, L0_cond_Wtemp, L0_cond_btemp, L0_cond_Wout, L0_cond_gamma, L0_cond_beta)
    x = x + _L1_cond_ref(x, mask_SxS_bk0, itok_Sx32_0_1023, mask_Sx32_bk1, condB_uprev[:, None], L1_cond_Wq, L1_cond_bq, L1_cond_Wk, L1_cond_bk, L1_cond_Wv, L1_cond_bv, L1_cond_Wo, L1_cond_bo)
    return x

_drawn_inputs = setup_inputs


def setup_inputs(seed=0):
    import zlib

    import numpy as np

    out = dict(_drawn_inputs(seed))
    spreads = {'condB_bn2': (0.0, 2.0),
     'L0_cond_bg': (-0.5, 0.6),
     'L0_cond_bn1': (0.0, 2.0),
     'L0_cond_bsoma': (0.0, 0.1),
     'L0_cond_btemp': (0.0, 0.1),
     'L0_cond_gamma': (1.0, 0.2),
     'L0_cond_beta': (0.0, 0.1),
     'L1_cond_bq': (0.0, 0.1),
     'L1_cond_bk': (0.0, 2.0),
     'L1_cond_bv': (0.0, 0.1),
     'L1_cond_bo': (0.0, 0.1)}
    factors = {'condB_tauraws': 8.0, 'cond_256': 34.605, 'cond_1024': 64.0, 'L0_cond_Wn1': 43.026}
    for name, (base, spread) in spreads.items():
        noise = np.random.default_rng([zlib.crc32(name.encode()), seed]).standard_normal(out[name].shape)
        drawn = base * np.exp(spread * noise) if base else spread * noise
        out[name] = jnp.asarray(drawn.astype(out[name].dtype))
    for name, factor in factors.items():
        out[name] = (out[name] * factor).astype(out[name].dtype)
    return out
```

```python
from contextlib import ExitStack

import numpy as np

import concourse.bass as bass
from concourse import mybir

F32 = mybir.dt.float32
BF16 = mybir.dt.bfloat16
I32 = mybir.dt.int32
U8 = mybir.dt.uint8
ALU = mybir.AluOpType
ACT = mybir.ActivationFunctionType
AX_X = mybir.AxisListType.X

P = 128
B = 32
GB = 4
G = B // GB
W = GB * P
D = 32
Q = 8
NCH = P // Q
NJ = NCH * D // P
H = 16
DH = P // H
K_SPARSE = 32
TERMS_Q = (0, 1, 0, 2, 1, 0)
TERMS_K = (0, 0, 1, 0, 1, 2)
NT = len(TERMS_Q)
KR = NT * DH
SLOT = 64
NU = H // 2
NZ = H // 4
BIG = 1.0e30
SCALE = float(1.0 / np.sqrt(np.float32(DH)))

WCOLS = ["wg_x", "wg_ctx", "wsoma", "wtemp", "wout", "wq", "wk", "wv", "wo"]
C_ID, C_LT, C_LTM, C_K = 0, P, 2 * P, 3 * P
C_A = 4 * P
C_AM = C_A + NCH * D
C_P = C_AM + NCH * D
C_PM = C_P + D
C_T = C_PM + D
C_END = C_T + Q


VEC_STEPS = ["neg_abs_tau", "neg_relu_tau", "ones0", "ones1", "log_decay", "idx_f", "mask_f", "idx_plus", "idx_masked",
             "decay_arg", "blend_max", "blend_negmax", "blend_sum", "blend_recip", "blend_4", "half_bw", "w_lag", "lt",
             "decay_p", "decay_a", "gate_biases", "mod_bias", "w_out", "q_bias", "k_bias", "not_prior", "lam",
             "use", "not_use", "dense_lam", "cnt_start"] + [f"cnt{j}" for j in range(K_SPARSE)] + [
             "cnt_one", "cnt_none", "neg_lc"]
ACT_STEPS = ["exp_tau", "softplus", "exp_u", "exp_blend", "lt", "decay_p", "apow", "decay_a", "ln_cnt"]


def vec(name):
    return VEC_STEPS.index(name) + 1


def scal(name):
    return ACT_STEPS.index(name) + 1


def build(nc, x, w, wn1, wn2, cols, small, tau4, rows, taus, taux, uprev, bn2, blend, consts,
          idx, idx_mask, prior_mask, out):
    with ExitStack() as ctx:
        def sb(name, shape, dt=F32):
            return ctx.enter_context(nc.sbuf_tensor(name, shape, dt))

        def sem(name):
            return ctx.enter_context(nc.semaphore(name))

        w_sb = sb("w_sb", [P, len(WCOLS), P])
        wt = {n: w_sb[:, k, :] for k, n in enumerate(WCOLS)}
        wn1_sb = sb("wn1_sb", [P, D])
        wn2_sb = sb("wn2_sb", [D + 1, P])
        cols_sb = sb("cols_sb", [P, 5])
        small_sb = sb("small_sb", [D, 2])
        rows_sb = sb("rows_sb", [P, 4, P])
        c_sb = sb("c_sb", [P, C_END])
        ident = c_sb[:, C_ID:C_ID + P]
        lt = sb("lt", [P, P])
        decay_a = sb("decay_a", [P, NCH, D])
        decay_p = sb("decay_p", [P, D])
        apow = sb("apow", [P, Q])
        half_bw = sb("half_bw", [P, P])
        w_lag = sb("w_lag", [D, Q, P])
        neg_lc = sb("neg_lc", [P, P])
        not_prior = sb("not_prior", [P, P])
        use_b = sb("use_b", [P, B])
        dense_lam = sb("dense_lam", [P, B])
        hb = sb("hb", [P, 5])
        hs = sb("hs", [D, 1])
        x1b_all = sb("x1b_all", [P, B, P])
        v_all = sb("v_all", [P, B, P])
        q_parts = sb("q_parts", [P, 3, B * P], BF16)
        k_parts = sb("k_parts", [P, 3, B * P], BF16)

        ARENA = 19 * W * 2
        arena = sb("arena", [P, ARENA])
        at = [0]

        def take(n):
            at[0] += n
            assert at[0] <= ARENA, at[0]
            return arena[:, at[0] - n:at[0]]

        xn, xT, th, ctxT, thd, bh = [], [], [], [], [], []
        somaT, h1T, modT, gT, gn, thn, modn, mod_a, acc, prod = [], [], [], [], [], [], [], [], [], []
        for u in range(2):
            xn.append(take(W))
            four = take(4 * W)
            bh.append(four.rearrange("p (j n) -> p j n", j=NJ))
            xT.append(four[:, 0:W])
            th.append(four[:, W:2 * W])
            ctxT.append(four[:, 2 * W:3 * W])
            thd.append(four[:, 3 * W:4 * W])
            somaT.append(take(W))
            h1T.append(take(W))
            modT.append(take(W))
            gT.append(take(W))
            gn.append(take(W))
            thn.append(take(P))
            modn.append(take(P))
            mod_a.append(take(4 * W))
            acc.append(take(W))
            prod.append([take(W), take(W)])
        crn, temporalT, tg, sg, ln, x1g = gn, [p[1] for p in prod], modT, gT, acc, somaT
        x1T = [m[:, 0:W] for m in mod_a]
        qk_f = [[m[:, W:2 * W], m[:, 2 * W:3 * W]] for m in mod_a]
        rest = [m[:, 3 * W:4 * W] for m in mod_a]
        stats = sb("stats", [P, 2, GB, 6])
        moments = sb("moments", [P, 2, GB, 2])
        vareps = sb("vareps", [P, 2, GB])
        rstd = sb("rstd", [P, 2, GB])
        minus_half = sb("minus_half", [P, GB])

        at[0] = 0
        stack = [[take(NU * W // 2).bitcast(BF16).rearrange("p (n t) -> p n t", n=NU) for _ in range(2)]
                 for _ in range(2)]
        neg_t = [take(W) for _ in range(3)]
        prob = [take(W) for _ in range(4)]
        probT = [take(W) for _ in range(3)]
        oT = [take(W) for _ in range(2)]
        vx = [take(H * D).rearrange("p (h e) -> p h e", h=H) for _ in range(2)]
        nbias = [take(P) for _ in range(2)]
        dtmp = take(P)
        attn = [take(P) for _ in range(2)]
        attnT = [take(P) for _ in range(2)]
        yout = [take(W).rearrange("p (b c) -> p b c", b=GB) for _ in range(2)]
        neg_max = sb("neg_max", [P, 2, H])
        rden = sb("rden", [P, 2, H])

        pro = arena[:, ARENA - 8 * W:ARENA]
        idx_i = pro[:, 0:K_SPARSE].bitcast(I32)
        idx_f = pro[:, 32:64]
        im_f = pro[:, 64:96]
        idx_m = pro[:, 96:128]
        cnt = [pro[:, 128:256], pro[:, 256:384]]
        lncnt = pro[:, 384:512]
        cnt0 = pro[:, 512:640]
        taus_sb = pro[:, 640:704]
        sp_a = pro[:, 704:768]
        sp_b = pro[:, 768:832]
        sp_c = pro[:, 832:896]
        sp_d = pro[:, 2436:2500]
        lna = pro[:, 896:960]
        up = pro[:, 960:992]
        lam = pro[:, 992:1024]
        not_use = pro[:, 1024:1056]
        bl = pro[:, 1056:1088]
        bl_e = pro[:, 1088:1120]
        bl_m = pro[:, 1120:1121]
        bl_s = pro[:, 1121:1122]
        bl_r = pro[:, 1122:1123]
        bl_4 = pro[:, 1124:1252]
        arg_a = pro[:, 1252:1252 + NCH * D]
        exp_lt = pro[:, 1764:1892]
        exp_a = pro[:, 1892:2404]
        exp_p = pro[:, 2404:2436]
        u8s = sb("u8s", [P, P + K_SPARSE], U8)

        ps = [ctx.enter_context(nc.psum_tensor(f"ps{u}", [P, 4, W], F32)) for u in range(2)]

        def bank(u, k):
            return ps[u][:, k, :]

        loaded = sem("loaded")
        x_loaded = [sem("x_loaded0"), sem("x_loaded1")]
        x_free = sem("x_free")
        dv = sem("dv")
        ac = sem("ac")
        blend_t = sem("blend_t")
        names_a = ("xT_ps xT_ready ctx_ps ctx_ready wg_ps h1_ps soma_ps gate_tanh h1_ready soma_ready modT_ps modn_ps "
                   "modT_tanh modn_tanh gated_ready modT_ready modn_ready mod_a_ready gn_ps gn_ready lag_ps prod_ready "
                   "lag_added state_ps bh_ready cross_ps cross_ready crossT_ps temporal_ready temp_ps temp_tanh "
                   "mixed_ready out_ps stats_ready moments_ready vareps_ready rstd_ready ln_ready xb_ready scaled_ready x1_ready "
                   "x1b_ready x1T_ps x1T_ready qkv_ps qk_f_ready part1_ready rest1_ready part2_ready rest2_ready "
                   "part3_ready v_stored tail_read").split()
        s = {n: sem(n) for n in names_a}
        names_b = ("logits_begun aggr_begun half_set a_done stack_loaded0 stack_loaded1 score_ps negt_ready prob_ready probT_ps probT_ready pv_ps oT_ready "
                   "on_ps rden_ready attn_ready attnT_ps attnT_ready y_ps y_ready y_stored0 y_stored1 v_copied bias_a bias_ready vx_zeroed "
                   "vx_free nbias_free").split()
        s.update({n: sem(n) for n in names_b})

        block = ctx.enter_context(nc.Block())
        n_loads = 16

        def grp(i, u, k=1, c=0):
            return i * (2 * k) + (u * k + c)

        x_v = x.rearrange("b t c -> t b c")
        out_v = out.rearrange("b t c -> t b c")

        NB2 = 2 * GB

        @block.sync
        def _(sp):
            for dst, src in ((cols_sb[:], cols), (c_sb[:], consts), (w_sb[:], w), (wn1_sb[:], wn1),
                             (wn2_sb[0:D, :], wn2), (wn2_sb[D:D + 1, :], bn2), (small_sb[:], small),
                             (taus_sb[:, 0:D], taus.broadcast_to([P, D])),
                             (taus_sb[:, D:D + 1], tau4), (taus_sb[:, D + 1:D + 2], taux.broadcast_to([P, 1])),
                             (up, uprev.broadcast_to([P, B])), (bl, blend), (idx_i, idx),
                             (u8s[:, 0:P], prior_mask), (u8s[:, P:P + K_SPARSE], idx_mask),
                             (rows_sb[:].rearrange("p a n -> p (a n)"), rows.broadcast_to([P, 4 * P]))):
                sp.dma_start(dst, src).then_inc(loaded, 16)
            with sp.Fori(0, G // 2) as i:
                for u in range(2):
                    sp.wait_ge(x_free, i * 2 + 1)
                    sp.dma_start(xn[u].rearrange("p (b c) -> p b c", b=GB),
                                 x_v[:, bass.ds(i * (2 * GB) + u * GB, GB), :]).then_inc(x_loaded[u], 16)
            sp.wait_ge(s["a_done"], 4)

            def load_stack(i, u):
                for which, (parts, terms) in enumerate(((q_parts, TERMS_Q), (k_parts, TERMS_K))):
                    for n, part in enumerate(terms):
                        for slot in range(2):
                            r0 = slot * SLOT + n * DH
                            dst = stack[u][which][r0:r0 + DH, :, :]
                            src = parts[slot * SLOT:(slot + 1) * SLOT, part, bass.ds(i * (2 * W) + u * W, W)]
                            sp.dma_start(dst, src).then_inc(s[f"stack_loaded{u}"], 16)

            def store(i, u):
                sp.wait_ge(s["y_ready"], i * NB2 + GB * (u + 1))
                sp.dma_start(out_v[:, bass.ds(i * NB2 + u * GB, GB), :], yout[u]).then_inc(s[f"y_stored{u}"], 16)

            load_stack(0, 0)
            load_stack(0, 1)
            with sp.Fori(0, G // 2 - 1) as i:
                for u in range(2):
                    sp.wait_ge(s["score_ps"], i * (NZ * NB2) + NZ * GB * (u + 1))
                    load_stack(i + 1, u)
                    store(i, u)
            for u in range(2):
                store(G // 2 - 1, u)
            sp.wait_ge(s["y_stored0"], 16 * G // 2)
            sp.wait_ge(s["y_stored1"], 16 * G // 2)

        @block.tensor
        def _(pe):
            pe.wait_ge(loaded, 16 * n_loads)
            pe.wait_ge(dv, vec("blend_4"))
            pe.transpose(bank(0, 0)[:, 0:P], bl_4, ident).then_inc(blend_t, 1)
            pe.wait_ge(dv, vec("w_out"))
            with pe.Fori(0, G // 2) as i:
                pe.wait_ge(s["tail_read"], i * 4 + 1)
                pe.wait_ge(s["v_stored"], i * 2 + 1)
                for u in range(2):
                    pe.wait_ge(x_loaded[u], i * 16 + 16)
                    for b in range(GB):
                        cs = slice(b * P, b * P + P)
                        mm = pe.transpose(bank(u, 0)[:, cs], xn[u][:, cs], ident)
                    mm.then_inc(s["xT_ps"], 1)
                    for b in range(GB):
                        cs = slice(b * P, b * P + P)
                        mm = pe.matmul(bank(u, 1)[:, cs], xn[u][:, cs], lt[:], start=True, stop=True)
                    mm.then_inc(s["ctx_ps"], 1)
                for u in range(2):
                    pe.wait_ge(s["xT_ready"], grp(i, u, 1, 1))
                    pe.matmul(bank(u, 3)[0:D, :], wn1_sb[:], xT[u], start=True, stop=True).then_inc(s["h1_ps"], 1)
                    pe.matmul(bank(u, 0), wt["wsoma"], xT[u], start=True, stop=True).then_inc(s["soma_ps"], 1)
                    pe.matmul(bank(u, 2), wt["wg_x"], xT[u], start=True, stop=False)
                    pe.wait_ge(s["ctx_ready"], grp(i, u, 1, 1))
                    pe.matmul(bank(u, 2), wt["wg_ctx"], ctxT[u], start=False, stop=True).then_inc(s["wg_ps"], 1)
                for u in range(2):
                    pe.wait_ge(s["h1_ready"], grp(i, u, 1, 1))
                    pe.matmul(bank(u, 1), wn2_sb[0:D, :], h1T[u][0:D, :], start=True, stop=True)\
                        .then_inc(s["modT_ps"], 1)
                    for b in range(GB):
                        mm = pe.matmul(bank(u, 3)[:, b * D:b * D + D], h1T[u][0:D + 1, b * P:b * P + P],
                                       wn2_sb[:, 0:D], start=True, stop=True)
                    mm.then_inc(s["modn_ps"], 1)
                for u in range(2):
                    pe.wait_ge(s["gated_ready"], grp(i, u, 1, 1))
                    for b in range(GB):
                        cs = slice(b * P, b * P + P)
                        mm = pe.transpose(bank(u, 2)[:, cs], gT[u][:, cs], ident)
                    mm.then_inc(s["gn_ps"], 1)
                    pe.wait_ge(s["modT_ready"], grp(i, u, 1, 1))
                    pe.wait_ge(s["soma_ready"], grp(i, u, 1, 1))
                    for lag in range(Q):
                        if lag >= 2:
                            pe.wait_ge(s["prod_ready"], grp(i, u, Q, lag - 1))
                        pe.matmul(bank(u, lag % 2), w_lag[:, lag, :], modT[u][0:D, :], start=True, stop=True)\
                            .then_inc(s["lag_ps"], 1)
                for u in range(2):
                    pe.wait_ge(s["gn_ready"], grp(i, u, 1, 1))
                    pe.wait_ge(s["modn_tanh"], grp(i, u, 1, 1))
                    for j in range(NJ):
                        if j >= 2:
                            pe.wait_ge(s["bh_ready"], grp(i, u, NJ, j - 1))
                        for b in range(GB):
                            if j == 0:
                                pe.wait_ge(s["mod_a_ready"], grp(i, u, GB, b + 1))
                            cs = slice(b * P, b * P + P)
                            mm = pe.matmul(bank(u, 2 + j % 2)[:, cs],
                                           mod_a[u][:, b * W + j * P:b * W + j * P + P], gn[u][:, cs],
                                           start=True, stop=True)
                        mm.then_inc(s["state_ps"], 1)
                for u in range(2):
                    pe.wait_ge(s["prod_ready"], grp(i, u, Q, Q))
                    pe.wait_ge(s["bh_ready"], grp(i, u, NJ, NJ))
                    for j in range(NJ):
                        mm = pe.matmul(bank(u, 0)[32 * j:32 * j + 32, :], decay_p[:], bh[u][:, j, :],
                                       start=True, stop=True)
                    mm.then_inc(s["cross_ps"], 1)
                for u in range(2):
                    pe.wait_ge(s["cross_ready"], grp(i, u, 1, 1))
                    for b in range(GB):
                        cs = slice(b * P, b * P + P)
                        mm = pe.transpose(bank(u, 1)[:, cs], crn[u][:, cs], ident)
                    mm.then_inc(s["crossT_ps"], 1)
                for u in range(2):
                    pe.wait_ge(s["temporal_ready"], grp(i, u, 1, 1))
                    pe.matmul(bank(u, 2), wt["wtemp"], temporalT[u], start=True, stop=True).then_inc(s["temp_ps"], 1)
                for u in range(2):
                    pe.wait_ge(s["mixed_ready"], grp(i, u, 1, 1))
                    for b in range(GB):
                        cs = slice(b * P, b * P + P)
                        mm = pe.matmul(bank(u, 3)[:, cs], sg[u][:, cs], wt["wout"], start=True, stop=True)
                    mm.then_inc(s["out_ps"], 1)
                for u in range(2):
                    pe.wait_ge(s["x1_ready"], grp(i, u, 1, 1))
                    for b in range(GB):
                        cs = slice(b * P, b * P + P)
                        mm = pe.transpose(bank(u, 0)[:, cs], x1g[u][:, cs], ident)
                    mm.then_inc(s["x1T_ps"], 1)
                for u in range(2):
                    pe.wait_ge(s["x1T_ready"], grp(i, u, 1, 1))
                    pe.matmul(bank(u, 1), wt["wq"], x1T[u], start=True, stop=True).then_inc(s["qkv_ps"], 1)
                    pe.matmul(bank(u, 2), wt["wk"], x1T[u], start=True, stop=True).then_inc(s["qkv_ps"], 1)
                    for b in range(GB):
                        cs = slice(b * P, b * P + P)
                        mm = pe.matmul(bank(u, 3)[:, cs], x1T[u][:, cs], wt["wv"], start=True, stop=True)
                    mm.then_inc(s["qkv_ps"], 1)
            pe.wait_ge(s["tail_read"], 2 * G + 1)
            pe.wait_ge(s["v_stored"], G + 1)
            pe.sem_inc(s["a_done"], 1)
            pe.wait_ge(s["a_done"], 4)

            def scores(i, n, z):
                u, b = n // GB % 2, n % GB
                if z == 0 and b == 0:
                    pe.wait_ge(s[f"stack_loaded{u}"], i * (16 * 4 * NT) + 16 * 4 * NT * (1 + n // NB2))
                c = NZ * n + z
                if isinstance(i, int) and NZ * NB2 * i + c < 2:
                    pass
                else:
                    pe.wait_ge(s["negt_ready"], i * (4 * NZ * NB2) + 4 * (c - 1))
                for k in range(4):
                    r0, tile = SLOT * (z % 2), 4 * (z // 2) + k
                    mm = pe.matmul(ps[0][:, c % 2, k * P:k * P + P],
                                   stack[u][0][r0:r0 + KR, tile, b * P:b * P + P],
                                   stack[u][1][r0:r0 + KR, tile, b * P:b * P + P], start=True, stop=True)
                mm.then_inc(s["score_ps"], 1)

            def turn(i, n, z):
                c = NZ * n + z
                pe.wait_ge(s["prob_ready"], i * (4 * NZ * NB2) + 4 * (c + 1))
                if not (isinstance(i, int) and NZ * NB2 * i + c < 2):
                    pe.wait_ge(s["probT_ready"], i * (NZ * NB2) + (c - 1))
                for k in range(4):
                    mm = pe.transpose(ps[0][:, 2 + c % 2, k * P:k * P + P], prob[c % 4][:, k * P:k * P + P], ident)
                mm.then_inc(s["probT_ps"], 1)

            def values(i, n, z):
                c = NZ * n + z
                pe.wait_ge(s["probT_ready"], i * (NZ * NB2) + (c + 1))
                if z == 0:
                    pe.wait_ge(s["v_copied"], i * NB2 + (n + 1))
                    if not (isinstance(i, int) and NB2 * i + n < 1):
                        pe.wait_ge(s["oT_ready"], i * NB2 + n)
                for k in range(4):
                    mm = pe.matmul(ps[1][32 * k:32 * k + 32, 0, z * P:z * P + P], vx[n % 2][:, 4 * z + k, :],
                                   probT[c % 3][:, k * P:k * P + P], start=True, stop=True)
                mm.then_inc(s["pv_ps"], 1)

            def turn_o(i, n):
                pe.wait_ge(s["oT_ready"], i * NB2 + (n + 1))
                if not (isinstance(i, int) and NB2 * i + n < 1):
                    pe.wait_ge(s["attn_ready"], i * NB2 + n)
                for z in range(NZ):
                    mm = pe.transpose(ps[1][:, 1, z * P:z * P + P], oT[n % 2][:, z * P:z * P + P], ident)
                mm.then_inc(s["on_ps"], 1)

            def turn_attn(i, n):
                pe.wait_ge(s["attn_ready"], i * NB2 + (n + 1))
                if not (isinstance(i, int) and NB2 * i + n < 1):
                    pe.wait_ge(s["attnT_ready"], i * NB2 + n)
                pe.transpose(ps[1][:, 2, 0:P], attn[n % 2], ident).then_inc(s["attnT_ps"], 1)

            def project(i, n):
                pe.wait_ge(s["attnT_ready"], i * NB2 + (n + 1))
                if not (isinstance(i, int) and NB2 * i + n < 1):
                    pe.wait_ge(s["y_ready"], i * NB2 + n)
                pe.matmul(ps[1][:, 3, 0:P], attnT[n % 2], wt["wo"], start=True, stop=True).then_inc(s["y_ps"], 1)

            def step(i, n, last=False, first=False):
                for z in range(NZ):
                    if not last:
                        scores(i, n + 1, z)
                    turn(i, n, z)
                    if not first and z < 3:
                        (turn_o, turn_attn, project)[z](i, n - 1)
                    if z >= 1:
                        values(i, n, z - 1)
                values(i, n, NZ - 1)

            for z in range(NZ):
                scores(0, 0, z)
            for n in range(2):
                step(0, n, first=(n == 0))
            with pe.Fori(0, B // NB2 - 1) as i:
                for n in range(2, 2 + NB2):
                    step(i, n)
            for n in range(2, NB2):
                step(B // NB2 - 1, n, last=(n == NB2 - 1))
            turn_o(B // NB2 - 1, NB2 - 1)
            turn_attn(B // NB2 - 1, NB2 - 1)
            project(B // NB2 - 1, NB2 - 1)

        @block.scalar
        def _(act):
            act.wait_ge(loaded, 16 * n_loads)
            act.wait_ge(dv, vec("neg_abs_tau"))
            act.activation(sp_b[:, 0:D + 2], sp_a[:, 0:D + 2], ACT.Exp).then_inc(ac, 1)
            act.wait_ge(ac, scal("exp_tau"))
            act.activation(sp_c[:, 0:D + 2], sp_b[:, 0:D + 2], ACT.Ln, bias=1.0).then_inc(ac, 1)
            act.activation(lam, up, ACT.Exp, scale=-5.0).then_inc(ac, 1)
            act.wait_ge(dv, vec("blend_negmax"))
            act.activation(bl_e, bl, ACT.Exp, bias=bl_m).then_inc(ac, 1)
            act.activation(exp_lt, c_sb[:, C_LT:C_LT + P], ACT.Exp, scale=lna[:, D + 1:D + 2]).then_inc(ac, 1)
            act.activation(exp_p, c_sb[:, C_P:C_P + D], ACT.Exp, scale=lna[:, D:D + 1]).then_inc(ac, 1)
            act.activation(apow[:], c_sb[:, C_T:C_T + Q], ACT.Exp, scale=lna[:, D:D + 1]).then_inc(ac, 1)
            act.activation(exp_a, arg_a, ACT.Exp).then_inc(ac, 1)
            act.wait_ge(dv, vec("cnt_one"))
            act.activation(lncnt, cnt0, ACT.Ln).then_inc(ac, 1)
            act.wait_ge(dv, vec("k_bias"))
            act.sem_inc(s["tail_read"], 1)
            with act.Fori(0, G // 2) as i:
                for u in range(2):
                    act.wait_ge(s["xT_ps"], grp(i, u, 1, 1))
                    act.activation(xT[u], bank(u, 0), ACT.Copy).then_inc(s["xT_ready"], 1)
                for u in range(2):
                    act.wait_ge(s["h1_ps"], grp(i, u, 1, 1))
                    act.activation(h1T[u][0:D, :], bank(u, 3)[0:D, :], ACT.Gelu, bias=small_sb[:, 0:1])\
                        .then_inc(s["h1_ready"], 1)
                    act.wait_ge(s["wg_ps"], grp(i, u, 1, 1))
                    act.activation(th[u], bank(u, 2), ACT.Tanh, bias=hb[:, 0:1], scale=0.5)\
                        .then_inc(s["gate_tanh"], 1)
                    act.wait_ge(s["soma_ps"], grp(i, u, 1, 1))
                    act.activation(somaT[u], bank(u, 0), ACT.Gelu, bias=cols_sb[:, 1:2]).then_inc(s["soma_ready"], 1)
                for u in range(2):
                    act.wait_ge(s["modT_ps"], grp(i, u, 1, 1))
                    act.activation(thd[u][0:D, :], bank(u, 1)[0:D, :], ACT.Tanh, bias=hs[:, 0:1], scale=0.5)\
                        .then_inc(s["modT_tanh"], 1)
                    act.wait_ge(s["modn_ps"], grp(i, u, 1, 1))
                    act.activation(thn[u], bank(u, 3)[:, 0:P], ACT.Tanh, scale=0.5).then_inc(s["modn_tanh"], 1)
                for u in range(2):
                    act.wait_ge(s["gn_ps"], grp(i, u, 1, 1))
                    act.activation(gn[u], bank(u, 2), ACT.Copy).then_inc(s["gn_ready"], 1)
                for u in range(2):
                    act.wait_ge(s["cross_ps"], grp(i, u, 1, 1))
                    act.activation(crn[u], bank(u, 0), ACT.Copy).then_inc(s["cross_ready"], 1)
                for u in range(2):
                    act.wait_ge(s["temp_ps"], grp(i, u, 1, 1))
                    act.activation(tg[u], bank(u, 2), ACT.Tanh, bias=hb[:, 1:2], scale=0.5).then_inc(s["temp_tanh"], 1)
                for u in range(2):
                    act.wait_ge(s["x1T_ps"], grp(i, u, 1, 1))
                    act.activation(x1T[u], bank(u, 0), ACT.Copy).then_inc(s["x1T_ready"], 1)
                for u in range(2):
                    for w_, parts in enumerate((q_parts, k_parts)):
                        c = 2 * u + w_
                        act.wait_ge(s["qkv_ps"], grp(i, u, 3, w_ + 1))
                        act.activation(qk_f[u][w_], bank(u, 1 + w_), ACT.Identity, bias=hb[:, 3 + w_:4 + w_],
                                       scale=(-SCALE if w_ == 0 else 1.0)).then_inc(s["qk_f_ready"], 1)
                        act.wait_ge(s["qk_f_ready"], i * 4 + (c + 1))
                        act.activation(parts[:, 0, bass.ds(i * (2 * W) + u * W, W)], qk_f[u][w_], ACT.Copy)\
                            .then_inc(s["tail_read"], 1)
            act.wait_ge(s["tail_read"], 2 * G + 1)
            act.sem_inc(s["a_done"], 1)
            act.wait_ge(s["a_done"], 4)

            def exps(i, n, z):
                c = NZ * n + z
                for k in range(4):
                    act.wait_ge(s["negt_ready"], i * (4 * NZ * NB2) + (4 * c + k + 1))
                    if k == 0 and not (isinstance(i, int) and NZ * NB2 * i + c < 4):
                        act.wait_ge(s["probT_ps"], i * (NZ * NB2) + (c - 3))
                    act.activation(prob[c % 4][:, k * P:k * P + P], neg_t[c % 3][:, k * P:k * P + P], ACT.Exp,
                                   bias=neg_max[:, n % 2, 4 * z + k:4 * z + k + 1], scale=-1.0)\
                        .then_inc(s["prob_ready"], 1)

            def move(i, n, z):
                c = NZ * n + z
                act.wait_ge(s["probT_ps"], i * (NZ * NB2) + (c + 1))
                if not (isinstance(i, int) and NZ * NB2 * i + c < 3):
                    act.wait_ge(s["pv_ps"], i * (NZ * NB2) + (c - 2))
                act.activation(probT[c % 3], ps[0][:, 2 + c % 2, :], ACT.Copy).then_inc(s["probT_ready"], 1)

            def move_o(i, n):
                act.wait_ge(s["pv_ps"], i * (NZ * NB2) + NZ * (n + 1))
                act.activation(oT[n % 2], ps[1][:, 0, :], ACT.Copy).then_inc(s["oT_ready"], 1)

            def move_attn(i, n):
                act.wait_ge(s["attnT_ps"], i * NB2 + (n + 1))
                act.activation(attnT[n % 2], ps[1][:, 2, 0:P], ACT.Copy).then_inc(s["attnT_ready"], 1)

            def step(i, n, last=False, first=False):
                for z in range(NZ):
                    move(i, n, z)
                    if not first and z == 2:
                        move_attn(i, n - 1)
                    if not last:
                        exps(i, n + 1, z)
                move_o(i, n)

            for z in range(NZ):
                exps(0, 0, z)
            for n in range(2):
                step(0, n, first=(n == 0))
            with act.Fori(0, B // NB2 - 1) as i:
                for n in range(2, 2 + NB2):
                    step(i, n)
            for n in range(2, NB2):
                step(B // NB2 - 1, n, last=(n == NB2 - 1))
            move_attn(B // NB2 - 1, NB2 - 1)

        @block.vector
        def _(dve):
            count = [0]

            def pro(name, ins):
                count[0] += 1
                assert VEC_STEPS[count[0] - 1] == name, name
                ins.then_inc(dv, 1)
                dve.wait_ge(dv, count[0])

            nt = D + 2
            dve.wait_ge(loaded, 16 * n_loads)
            pro("neg_abs_tau", dve.scalar_tensor_tensor(sp_a[:, 0:nt], taus_sb[:, 0:nt], -1.0, taus_sb[:, 0:nt],
                                                        ALU.mult, ALU.min))
            pro("neg_relu_tau", dve.tensor_scalar(sp_d[:, 0:nt], taus_sb[:, 0:nt], 0.0, -1.0, ALU.max, ALU.mult))
            pro("ones0", dve.memset(h1T[0][D:D + 1, :], 1.0))
            pro("ones1", dve.memset(h1T[1][D:D + 1, :], 1.0))
            dve.wait_ge(ac, scal("softplus"))
            pro("log_decay", dve.tensor_tensor(lna[:, 0:nt], sp_d[:, 0:nt], sp_c[:, 0:nt], ALU.subtract))
            pro("idx_f", dve.tensor_copy(idx_f, idx_i))
            pro("mask_f", dve.tensor_copy(im_f, u8s[:, P:P + K_SPARSE]))
            pro("idx_plus", dve.scalar_tensor_tensor(idx_m, idx_f, 1.0, im_f, ALU.add, ALU.mult))
            pro("idx_masked", dve.tensor_scalar(idx_m, idx_m, -1.0, None, ALU.add))
            pro("decay_arg", dve.tensor_tensor(arg_a.rearrange("p (k d) -> p k d", d=D),
                                               c_sb[:, C_A:C_A + NCH * D].rearrange("p (k d) -> p k d", d=D),
                                               lna[:, 0:D].unsqueeze(1).broadcast_to([P, NCH, D]), ALU.mult))
            pro("blend_max", dve.tensor_reduce(bl_s, bl, AX_X, ALU.max))
            pro("blend_negmax", dve.tensor_scalar(bl_m, bl_s, -1.0, None, ALU.mult))
            dve.wait_ge(ac, scal("exp_blend"))
            pro("blend_sum", dve.tensor_reduce(bl_s, bl_e, AX_X, ALU.add))
            pro("blend_recip", dve.reciprocal(bl_r, bl_s))
            pro("blend_4", dve.tensor_scalar(bl_4.rearrange("p (k d) -> p k d", d=D),
                                             bl_e.unsqueeze(1).broadcast_to([P, 4, D]), bl_r, 0.5,
                                             ALU.mult, ALU.mult))
            dve.wait_ge(blend_t, 1)
            pro("half_bw", dve.tensor_copy(half_bw[:], bank(0, 0)[:, 0:P]))
            dve.wait_ge(ac, scal("decay_a"))
            pro("w_lag", dve.tensor_tensor(w_lag[:], half_bw[0:D, :].unsqueeze(1).broadcast_to([D, Q, P]),
                                           apow[0:D, :].unsqueeze(2).broadcast_to([D, Q, P]), ALU.mult))
            pro("lt", dve.tensor_tensor(lt[:], exp_lt, c_sb[:, C_LTM:C_LTM + P], ALU.mult))
            pro("decay_p", dve.tensor_tensor(decay_p[:], exp_p, c_sb[:, C_PM:C_PM + D], ALU.mult))
            pro("decay_a", dve.tensor_tensor(decay_a[:].rearrange("p k d -> p (k d)"), exp_a,
                                             c_sb[:, C_AM:C_AM + NCH * D], ALU.mult))
            pro("gate_biases", dve.tensor_scalar(hb[:, 0:2], cols_sb[:, 0:3:2], 0.5, None, ALU.mult))
            pro("mod_bias", dve.tensor_scalar(hs[:], small_sb[:, 1:2], 0.5, None, ALU.mult))
            pro("w_out", dve.tensor_scalar(wt["wout"], wt["wout"], 0.5, None, ALU.mult))
            pro("q_bias", dve.tensor_scalar(hb[:, 3:4], cols_sb[:, 3:4], -SCALE, None, ALU.mult))
            pro("k_bias", dve.tensor_copy(hb[:, 4:5], cols_sb[:, 4:5]))
            pro("not_prior", dve.tensor_scalar(not_prior[:], u8s[:, 0:P], -1.0, 1.0, ALU.mult, ALU.add))
            pro("lam", dve.tensor_scalar(lam, lam, 10.0, None, ALU.mult))
            pro("use", dve.tensor_scalar(use_b[:], lam, 1.0, None, ALU.is_ge))
            pro("not_use", dve.tensor_scalar(not_use, use_b[:], -1.0, 1.0, ALU.mult, ALU.add))
            pro("dense_lam", dve.tensor_tensor(dense_lam[:], not_use, lam, ALU.mult))
            pro("cnt_start", dve.memset(cnt[0], 0.0))
            for j in range(K_SPARSE):
                pro(f"cnt{j}", dve.scalar_tensor_tensor(cnt[(j + 1) % 2], c_sb[:, C_K:C_K + P], idx_m[:, j:j + 1],
                                                        cnt[j % 2], ALU.is_equal, ALU.add))
            pro("cnt_one", dve.tensor_scalar(cnt0, cnt[0], 1.0, None, ALU.max))
            pro("cnt_none", dve.tensor_scalar(cnt[1], cnt[0], 0.0, BIG, ALU.is_equal, ALU.mult))
            dve.wait_ge(ac, scal("ln_cnt"))
            pro("neg_lc", dve.tensor_tensor(neg_lc[:], cnt[1], lncnt, ALU.subtract))
            dve.sem_inc(s["v_stored"], 1)

            def chunks(ap, a, b):
                return ap.rearrange("p (n q) -> p n q", q=Q)[:, :, a:b]

            def packed(ap, lag):
                return ap[:, 0:(W // Q) * (Q - lag)].rearrange("p (n q) -> p n q", q=Q - lag)

            with dve.Fori(0, G // 2) as i:
                for u in range(2):
                    dve.wait_ge(s["ctx_ps"], grp(i, u, 1, 1))
                    dve.tensor_copy(ctxT[u], bank(u, 1)).then_inc(s["ctx_ready"], 1)
                for u in range(2):
                    dve.wait_ge(s["gate_tanh"], grp(i, u, 1, 1))
                    dve.scalar_tensor_tensor(gT[u], th[u], 1.0, xT[u], ALU.add, ALU.mult)\
                        .then_inc(s["gated_ready"], 1)
                for u in range(2):
                    dve.wait_ge(s["modT_tanh"], grp(i, u, 1, 1))
                    dve.tensor_scalar(modT[u][0:D, :], thd[u][0:D, :], 0.5, 1.0, ALU.mult, ALU.add)\
                        .then_inc(s["modT_ready"], 1)
                    dve.wait_ge(s["modn_tanh"], grp(i, u, 1, 1))
                    dve.tensor_scalar(modn[u], thn[u], 0.5, 1.0, ALU.mult, ALU.add).then_inc(s["modn_ready"], 1)
                for u in range(2):
                    for lag in range(Q):
                        dve.wait_ge(s["lag_ps"], grp(i, u, Q, lag + 1))
                        if lag == 0:
                            dve.tensor_tensor(acc[u], bank(u, 0), gT[u], ALU.mult).then_inc(s["prod_ready"], 1)
                            continue
                        if lag >= 3:
                            dve.wait_ge(s["lag_added"], grp(i, u, Q - 1, lag - 2))
                        dve.tensor_tensor(packed(prod[u][lag % 2], lag), chunks(bank(u, lag % 2), 0, Q - lag),
                                          chunks(gT[u], 0, Q - lag), ALU.mult).then_inc(s["prod_ready"], 1)
                for u in range(2):
                    for j in range(NJ):
                        dve.wait_ge(s["state_ps"], grp(i, u, NJ, j + 1))
                        dve.tensor_tensor(bh[u][:, j, :].rearrange("p (b c) -> p b c", b=GB),
                                          bank(u, 2 + j % 2).rearrange("p (b c) -> p b c", b=GB),
                                          half_bw[:].unsqueeze(1).broadcast_to([P, GB, P]), ALU.mult)\
                            .then_inc(s["bh_ready"], 1)
                for u in range(2):
                    dve.wait_ge(s["crossT_ps"], grp(i, u, 1, 1))
                    dve.wait_ge(s["lag_added"], grp(i, u, Q - 1, Q - 1))
                    dve.tensor_tensor(temporalT[u], bank(u, 1), acc[u], ALU.add).then_inc(s["temporal_ready"], 1)
                for u in range(2):
                    dve.wait_ge(s["temp_tanh"], grp(i, u, 1, 1))
                    dve.scalar_tensor_tensor(sg[u], tg[u], 1.0, somaT[u], ALU.add, ALU.mult)\
                        .then_inc(s["mixed_ready"], 1)
                for u in range(2):
                    dve.wait_ge(s["out_ps"], grp(i, u, 1, 1))
                    for b in range(GB):
                        dve.bn_stats(stats[:, u, b, :], bank(u, 3)[:, b * P:b * P + P]).then_inc(s["stats_ready"], 1)
                    for b in range(GB):
                        dve.wait_ge(s["stats_ready"], grp(i, u, GB, b + 1))
                        dve.sem_inc(s["aggr_begun"], 1)
                        dve.bn_aggr(moments[:, u, b, :], stats[:, u, b, :]).then_inc(s["moments_ready"], 1)
                    dve.wait_ge(s["moments_ready"], grp(i, u, GB, GB))
                    dve.tensor_scalar(vareps[:, u, :], moments[:, u, :, 1], 1e-5, None, ALU.add)\
                        .then_inc(s["vareps_ready"], 1)
                    dve.wait_ge(s["rstd_ready"], grp(i, u, 1, 1))
                    for b in range(GB):
                        cs = slice(b * P, b * P + P)
                        dve.tensor_scalar(ln[u][:, cs], bank(u, 3)[:, cs], moments[:, u, b, 0:1],
                                          rstd[:, u, b:b + 1], ALU.subtract, ALU.mult).then_inc(s["ln_ready"], 1)
                for u in range(2):
                    for w_, parts in enumerate((q_parts, k_parts)):
                        c = 2 * u + w_
                        col = bass.ds(i * (2 * W) + u * W, W)
                        dve.wait_ge(s["tail_read"], i * 4 + (c + 2))
                        if w_ == 1:
                            dve.wait_ge(s["part3_ready"], i * 4 + c)
                        dve.tensor_tensor(rest[u], qk_f[u][w_], parts[:, 0, col], ALU.subtract)\
                            .then_inc(s["rest1_ready"], 1)
                        dve.wait_ge(s["rest1_ready"], i * 4 + (c + 1))
                        dve.tensor_copy(parts[:, 1, col], rest[u]).then_inc(s["part2_ready"], 1)
                        dve.wait_ge(s["part2_ready"], i * 4 + (c + 1))
                        dve.tensor_tensor(parts[:, 2, col], rest[u], parts[:, 1, col], ALU.subtract)\
                            .then_inc(s["part3_ready"], 1)
                    dve.wait_ge(s["qkv_ps"], grp(i, u, 3, 3))
                    dve.tensor_tensor(v_all[:, bass.ds(i * (2 * GB) + u * GB, GB), :],
                                      bank(u, 3).rearrange("p (b c) -> p b c", b=GB),
                                      rows_sb[:, 3, :].unsqueeze(1).broadcast_to([P, GB, P]), ALU.add)\
                        .then_inc(s["v_stored"], 1)
            dve.wait_ge(s["v_stored"], G + 1)
            dve.sem_inc(s["a_done"], 1)
            dve.wait_ge(s["a_done"], 4)

            def logits(i, n, z):
                c = NZ * n + z
                if z == 0:
                    dve.wait_ge(s["bias_ready"], i * NB2 + (n + 1))
                if not (isinstance(i, int) and NZ * NB2 * i + c < 3):
                    dve.wait_ge(s["prob_ready"], i * (4 * NZ * NB2) + 4 * (c - 2))
                dve.wait_ge(s["score_ps"], i * (NZ * NB2) + (c + 1))
                dve.sem_inc(s["logits_begun"], 1)
                for k in range(4):
                    cs = slice(k * P, k * P + P)
                    h = 4 * z + k
                    dve.tensor_tensor_reduce(out=neg_t[c % 3][:, cs], in0=ps[0][:, c % 2, cs], in1=nbias[n % 2],
                                             scale=1.0, scalar=3.0e38, op0=ALU.add, op1=ALU.min,
                                             accum_out=neg_max[:, n % 2, h:h + 1]).then_inc(s["negt_ready"], 1)

            def normalise(i, n):
                dve.wait_ge(s["on_ps"], i * NB2 + (n + 1))
                o = ps[1][:, 1, :].rearrange("p (h e) -> p h e", e=D)
                dve.reciprocal(rden[:, n % 2, :], o[:, :, DH]).then_inc(s["rden_ready"], 1)
                dve.wait_ge(s["rden_ready"], i * NB2 + (n + 1))
                dve.tensor_tensor(attn[n % 2].rearrange("p (h e) -> p h e", e=DH), o[:, :, 0:DH],
                                  rden[:, n % 2, :].unsqueeze(2).broadcast_to([P, H, DH]), ALU.mult)\
                    .then_inc(s["attn_ready"], 1)

            def result(i, n):
                dve.wait_ge(s["y_ps"], i * NB2 + (n + 1))
                u, b = n // GB % 2, n % GB
                if b == 0 and not (isinstance(i, int) and NB2 * i + n < NB2):
                    dve.wait_ge(s[f"y_stored{u}"], i * 16 + 16 * (n // NB2))
                dve.tensor_tensor(yout[u][:, b, :], ps[1][:, 3, 0:P], x1b_all[:, i * NB2 + n, :]
                                  if isinstance(i, int) else x1b_all[:, bass.ds(i * NB2 + n, 1), :]
                                  .rearrange("p a c -> p (a c)"), ALU.add).then_inc(s["y_ready"], 1)

            def step(i, n, last=False, first=False):
                for z in range(NZ):
                    if not last:
                        logits(i, n + 1, z)
                    if not first and z == 1:
                        normalise(i, n - 1)
                    if not first and z == 3:
                        result(i, n - 1)

            for z in range(NZ):
                logits(0, 0, z)
            for n in range(2):
                step(0, n, first=(n == 0))
            with dve.Fori(0, B // NB2 - 1) as i:
                for n in range(2, 2 + NB2):
                    step(i, n)
            for n in range(2, NB2):
                step(B // NB2 - 1, n, last=(n == NB2 - 1))
            normalise(B // NB2 - 1, NB2 - 1)
            result(B // NB2 - 1, NB2 - 1)

        @block.gpsimd
        def _(pool):
            pool.sem_inc(x_free, 1)
            pool.memset(minus_half[:], -0.5).then_inc(s["half_set"], 1)
            pool.wait_ge(s["half_set"], 1)
            pool.wait_ge(loaded, 16 * n_loads)
            pool.wait_ge(dv, vec("decay_a"))
            with pool.Fori(0, G // 2) as i:
                for u in range(2):
                    pool.wait_ge(x_loaded[u], i * 16 + 16)
                    pool.wait_ge(s["ctx_ps"], grp(i, u, 1, 1))
                    x4 = xn[u].rearrange("p (b c) -> p b c", b=GB)
                    pool.tensor_tensor(x4, x4, rows_sb[:, 1, :].unsqueeze(1).broadcast_to([P, GB, P]), ALU.add)\
                        .then_inc(s["xb_ready"], 1)
                for u in range(2):
                    pool.wait_ge(s["modn_ready"], grp(i, u, 1, 1))
                    for b in range(GB):
                        pool.tensor_tensor(mod_a[u][:, b * W:b * W + W].rearrange("p (k d) -> p k d", d=D),
                                           decay_a[:],
                                           modn[u][:, b * D:b * D + D].unsqueeze(1).broadcast_to([P, NCH, D]),
                                           ALU.mult).then_inc(s["mod_a_ready"], 1)
                    for lag in range(1, Q):
                        pool.wait_ge(s["prod_ready"], grp(i, u, Q, lag + 1))
                        if lag >= 2:
                            pool.wait_ge(s["lag_added"], grp(i, u, Q - 1, lag - 1))
                        a = acc[u].rearrange("p (n q) -> p n q", q=Q)[:, :, lag:Q]
                        pr = prod[u][lag % 2][:, 0:(W // Q) * (Q - lag)].rearrange("p (n q) -> p n q", q=Q - lag)
                        pool.tensor_tensor(a, a, pr, ALU.add).then_inc(s["lag_added"], 1)
                for u in range(2):
                    pool.wait_ge(s["vareps_ready"], grp(i, u, 1, 1))
                    pool.tensor_tensor(rstd[:, u, :], vareps[:, u, :], minus_half[:], ALU.pow)\
                        .then_inc(s["rstd_ready"], 1)
                for u in range(2):
                    pool.wait_ge(s["ln_ready"], grp(i, u, GB, GB))
                    ln4 = ln[u].rearrange("p (b c) -> p b c", b=GB)
                    pool.tensor_tensor(ln4, ln4, rows_sb[:, 0, :].unsqueeze(1).broadcast_to([P, GB, P]), ALU.mult)\
                        .then_inc(s["scaled_ready"], 1)
                    pool.wait_ge(s["scaled_ready"], grp(i, u, 1, 1))
                    pool.wait_ge(s["xb_ready"], grp(i, u, 1, 1))
                    pool.tensor_tensor(x1g[u], ln[u], xn[u], ALU.add).then_inc(s["x1_ready"], 1)
                for u in range(2):
                    pool.wait_ge(s["x1_ready"], grp(i, u, 1, 1))
                    pool.tensor_tensor(x1b_all[:, bass.ds(i * (2 * GB) + u * GB, GB), :],
                                       x1g[u].rearrange("p (b c) -> p b c", b=GB),
                                       rows_sb[:, 2, :].unsqueeze(1).broadcast_to([P, GB, P]), ALU.add)\
                        .then_inc(x_free, 1)
            pool.wait_ge(x_free, G + 1)
            pool.sem_inc(s["a_done"], 1)
            pool.wait_ge(s["a_done"], 4)
            for n in range(2):
                pool.memset(vx[n], 0.0).then_inc(s["vx_zeroed"], 1)
            for n in range(2):
                pool.wait_ge(s["vx_zeroed"], n + 1)
                pool.memset(vx[n][:, :, DH:DH + 1], 1.0).then_inc(s["vx_zeroed"], 1)
            pool.wait_ge(s["vx_zeroed"], 4)

            def row_of(ap, i, n):
                return ap[:, i * NB2 + n:i * NB2 + n + 1] if isinstance(i, int) else ap[:, bass.ds(i * NB2 + n, 1)]

            def prepare(i, n):
                first = isinstance(i, int) and NB2 * i + n < 2
                if not first:
                    pool.wait_ge(s["negt_ready"], i * (4 * NZ * NB2) + 4 * NZ * (n - 1))
                pool.tensor_tensor(nbias[n % 2], neg_lc[:], row_of(use_b, i, n).broadcast_to([P, P]), ALU.mult)\
                    .then_inc(s["bias_a"], 1)
                pool.tensor_tensor(dtmp, not_prior[:], row_of(dense_lam, i, n).broadcast_to([P, P]), ALU.mult)\
                    .then_inc(s["bias_a"], 1)
                pool.wait_ge(s["bias_a"], i * (2 * NB2) + 2 * (n + 1))
                pool.tensor_tensor(nbias[n % 2], nbias[n % 2], dtmp, ALU.add).then_inc(s["bias_ready"], 1)
                pool.wait_ge(s["bias_ready"], i * NB2 + (n + 1))
                if not first:
                    pool.wait_ge(s["pv_ps"], i * (NZ * NB2) + NZ * (n - 1))
                v = v_all[:, i * NB2 + n, :] if isinstance(i, int) else \
                    v_all[:, bass.ds(i * NB2 + n, 1), :].rearrange("p a c -> p (a c)")
                pool.tensor_copy(vx[n % 2][:, :, 0:DH], v.rearrange("p (h e) -> p h e", e=DH))\
                    .then_inc(s["v_copied"], 1)

            for n in range(2):
                prepare(0, n)
            with pool.Fori(0, B // NB2 - 1) as i:
                for n in range(2, 2 + NB2):
                    prepare(i, n)
            for n in range(2, NB2):
                prepare(B // NB2 - 1, n)


_ORDER = ["x", "w", "wn1", "wn2", "cols", "small", "tau4", "rows", "taus", "taux", "uprev", "bn2", "blend", "consts",
          "idx", "idx_mask", "prior_mask"]


def shape_constants():
    c = np.zeros((P, C_END), np.float32)
    r = np.arange(P)
    c[:, C_ID:C_ID + P] = np.eye(P)
    lag = r[None, :] - r[:, None]
    c[:, C_LT:C_LT + P] = np.maximum(lag, 0)
    c[:, C_LTM:C_LTM + P] = lag >= 0
    c[:, C_K:C_K + P] = r[None, :]
    to_start = np.repeat(np.arange(NCH) * Q, D)[None, :] - r[:, None]
    c[:, C_A:C_A + NCH * D] = np.maximum(to_start, 0)
    c[:, C_AM:C_AM + NCH * D] = to_start > 0
    inside = np.arange(D)[None, :] - (r // D * Q)[:, None]
    c[:, C_P:C_P + D] = np.clip(inside, 0, Q)
    c[:, C_PM:C_PM + D] = (inside >= 0) & (inside < Q)
    c[:, C_T:C_T + Q] = np.arange(Q)[None, :]
    return c


def kernel(x, condB_tauraws, cond_256, condB_bn2, cond_1024, itok_Sx32_0_1023, condB_uprev, mask_SxS_bk0,
           mask_Sx32_bk1, L0_cond_tau_ctx, L0_cond_Wg, L0_cond_bg, L0_cond_Wn1, L0_cond_bn1, L0_cond_Wsoma,
           L0_cond_bsoma, L0_cond_Wtemp, L0_cond_btemp, L0_cond_Wout, L0_cond_gamma, L0_cond_beta, L1_cond_Wq,
           L1_cond_bq, L1_cond_Wk, L1_cond_bk, L1_cond_Wv, L1_cond_bv, L1_cond_Wo, L1_cond_bo):
    import concourse.bacc as bacc
    from concourse.bass_utils import run_bass_kernel_spmd

    def arr(a):
        return np.asarray(a)

    order = np.arange(P).reshape(NZ // 2, 2, 4, DH).transpose(1, 3, 0, 2).reshape(P)
    wg = arr(L0_cond_Wg).T
    weights = [wg[0:P], wg[P:2 * P], arr(L0_cond_Wsoma).T, arr(L0_cond_Wtemp).T, arr(L0_cond_Wout).T,
               arr(L1_cond_Wq)[order].T, arr(L1_cond_Wk)[order].T, arr(L1_cond_Wv).T, arr(L1_cond_Wo).T]
    taus = arr(condB_tauraws)
    arrays = {
        "x": arr(x),
        "w": np.stack(weights, axis=1),
        "wn1": arr(L0_cond_Wn1).T,
        "wn2": np.tile(arr(cond_256).T, (1, P // D)),
        "cols": np.stack([arr(L0_cond_bg), arr(L0_cond_bsoma), arr(L0_cond_btemp), arr(L1_cond_bq)[order],
                          arr(L1_cond_bk)[order]], axis=1),
        "small": np.stack([arr(L0_cond_bn1), arr(condB_bn2)], axis=1),
        "tau4": np.tile(taus, P // D)[:, None],
        "rows": np.concatenate([arr(L0_cond_gamma), arr(L0_cond_beta), arr(L1_cond_bo), arr(L1_cond_bv)])[None, :],
        "taus": taus[None, :],
        "taux": arr(L0_cond_tau_ctx).reshape(1, 1),
        "uprev": arr(condB_uprev)[None, :],
        "bn2": np.tile(arr(condB_bn2), P // D)[None, :],
        "blend": arr(cond_1024).T,
        "consts": shape_constants(),
        "idx": arr(itok_Sx32_0_1023),
        "idx_mask": arr(mask_Sx32_bk1),
        "prior_mask": arr(mask_SxS_bk0),
    }
    nc = bacc.Bacc("TRN2", target_bir_lowering=False, num_devices=1)
    ins, args = {}, []
    for name in _ORDER:
        a = np.ascontiguousarray(arrays[name])
        ins[f"in_{name}"] = a
        args.append(nc.dram_tensor(f"in_{name}", a.shape, mybir.dt.from_np(a.dtype), kind="ExternalInput").ap())
    out = nc.dram_tensor("out", (B, P, P), F32, kind="ExternalOutput").ap()
    build(nc, *args, out)
    return run_bass_kernel_spmd(nc, [ins], core_ids=[0]).results[0]["out"]
```

```python
from contextlib import ExitStack

import numpy as np

import concourse.bass as bass
from concourse import mybir

F32 = mybir.dt.float32
BF16 = mybir.dt.bfloat16
I32 = mybir.dt.int32
U8 = mybir.dt.uint8
ALU = mybir.AluOpType
ACT = mybir.ActivationFunctionType
AX_X = mybir.AxisListType.X

P = 128
B = 32
GB = 4
G = B // GB
W = GB * P
D = 32
Q = 8
NCH = P // Q
NJ = NCH * D // P
H = 16
DH = P // H
K_SPARSE = 32
TERMS_Q = (0, 1, 0, 2, 1, 0)
TERMS_K = (0, 0, 1, 0, 1, 2)
NT = len(TERMS_Q)
KR = NT * DH
SLOT = 64
NU = H // 2
NZ = H // 4
BIG = 1.0e30
NT_RING = 8
SHIFTED_BY_POOL = (0, 1, 3)
MOVED_BY_DVE = (1,)
SCALE = float(1.0 / np.sqrt(np.float32(DH)))

WCOLS = ["wg_x", "wg_ctx", "wsoma", "wtemp", "wout", "wq", "wk", "wv", "wo"]
COLS = ["bg", "bsoma", "btemp", "bq", "bk", "bmod", "bn1", "tau4"]
C_WN1 = len(COLS)
C_BLEND = C_WN1 + D
C_COLS = C_BLEND + D
R_TAU = 4 * P
R_U = R_TAU + D + 1
R_END = R_U + B
C_LT, C_LTM = 0, P
C_A = 2 * P
C_AM = C_A + NCH * D
C_P = C_AM + NCH * D
C_PM = C_P + D
C_T = C_PM + D
C_K = C_T + Q
C_END = C_K + P

VEC_STEPS = ["neg_abs_tau", "neg_relu_tau", "gate_biases", "mod_bias", "q_bias", "k_bias", "ones0", "ones1",
             "key_no",
             "log_decay", "lt", "blend_max", "blend_negmax", "decay_arg", "blend_sum", "blend_recip", "blend_4",
             "half_bw", "decay_p", "decay_a", "w_lag", "w_rest", "w_a1", "w_a3", "w_mid", "w_b2", "w_out",
             "idx_f", "mask_f", "idx_plus", "idx_masked", "not_prior", "lam", "use", "not_use", "dense_lam",
             "cnt_start"] + [f"cnt{j}" for j in range(K_SPARSE)] + ["cnt_one", "cnt_none"]
ACT_STEPS = ["exp_tau", "softplus", "lt", "exp_blend", "decay_p", "apow", "decay_a", "exp_u", "w_a", "w_b3"]


def vec(name):
    return VEC_STEPS.index(name) + 1


def scal(name):
    return ACT_STEPS.index(name) + 1


def build(nc, x, w, wn2, cols, rows, consts, ident_in, idx, masks, out):
    with ExitStack() as ctx:
        def sb(name, shape, dt=F32):
            return ctx.enter_context(nc.sbuf_tensor(name, shape, dt))

        def sem(name):
            return ctx.enter_context(nc.semaphore(name))

        ident_sb = sb("ident_sb", [P, P])
        ident = ident_sb[:]
        w_sb = sb("w_sb", [P, len(WCOLS), P])
        wt = {n: w_sb[:, k, :] for k, n in enumerate(WCOLS)}
        wn2_sb = sb("wn2_sb", [D + 1, P])
        cols_sb = sb("cols_sb", [P, C_COLS])
        col = {n: cols_sb[:, k:k + 1] for k, n in enumerate(COLS)}
        wn1 = cols_sb[:, C_WN1:C_WN1 + D]
        bl = cols_sb[:, C_BLEND:C_BLEND + D]
        rows_sb = sb("rows_sb", [P, R_END])
        gamma, beta, bo, bv = [rows_sb[:, k * P:k * P + P] for k in range(4)]
        lt = sb("lt", [P, P])
        decay_a = sb("decay_a", [P, NCH, D])
        decay_p = sb("decay_p", [P, D])
        half_bw = sb("half_bw", [P, P])
        lag_a = sb("lag_a", [P, Q, P], BF16)
        lag_b = sb("lag_b", [P, Q, P], BF16)
        mod_pa = [sb(f"mod_pa{u}", [P, W], BF16) for u in range(2)]
        mod_pb = [sb(f"mod_pb{u}", [P, W], BF16) for u in range(2)]
        neg_lc = sb("neg_lc", [P, P])
        not_prior = sb("not_prior", [P, P])
        cnt = [sb(f"cnt{k}", [P, P]) for k in range(2)]
        cnt1 = sb("count_min1", [P, P])
        lncnt = sb("lncnt", [P, P])
        use_b = sb("use_b", [P, B])
        dense_lam = sb("dense_lam", [P, B])
        hb = sb("hb", [P, 5])
        idx_i = sb("idx_i", [P, K_SPARSE], I32)
        masks_sb = sb("masks_sb", [P, P + K_SPARSE], U8)
        idx_m = sb("idx_m", [P, K_SPARSE])
        key_no = sb("key_no", [P, P])
        lam, not_use = sb("lam", [P, B])[:], sb("not_use", [P, B])[:]
        idx_f, im_f = sb("idx_f", [P, K_SPARSE])[:], sb("im_f", [P, K_SPARSE])[:]
        x1b_all = sb("x1b_all", [P, B, P])
        v_all = sb("v_all", [P, B, P])
        q_parts = sb("q_parts", [P, 3, B * P], BF16)
        k_parts = sb("k_parts", [P, 3, B * P], BF16)
        stats = sb("stats", [P, 2, GB, 6])
        moments = sb("moments", [P, 2, GB, 2])
        vareps = sb("vareps", [P, 2, GB])
        rstd = sb("rstd", [P, 2, GB])
        minus_half = sb("minus_half", [P, GB])
        neg_max = sb("neg_max", [P, 2, H])
        rden = sb("rden", [P, 2, H])

        ARENA = 20 * W * 2 + 4 * W
        arena = sb("arena", [P, ARENA])
        at = [0]

        def take(n):
            at[0] += n
            assert at[0] <= ARENA, at[0]
            return arena[:, at[0] - n:at[0]]

        xT, th, ctxT, thd, bh = [], [], [], [], []
        somaT, h1T, modT, gT, gn, thn, modn, mod_a, prod = [], [], [], [], [], [], [], [], []
        for u in range(2):
            four = take(4 * W)
            bh.append(four.rearrange("p (j n) -> p j n", j=NJ))
            xT.append(four[:, 0:W])
            th.append(four[:, W:2 * W])
            ctxT.append(four[:, 2 * W:3 * W])
            thd.append(four[:, 3 * W:4 * W])
            mod_a.append(take(4 * W))
            somaT.append(take(W))
            h1T.append(take(W))
            modT.append(take(W))
            gT.append(take(W))
            gn.append(take(W))
            thn.append(take(P))
            modn.append(take(P))
            prod.append([take(W), take(W)])
        xn = [take(W) for _ in range(2)]
        xb = [take(W) for _ in range(2)]
        acc = [take(W) for _ in range(2)]
        x1g = [take(W) for _ in range(2)]
        x1T = take(W)
        qk_f = [take(W), take(W)]
        rest = take(W)
        crn, temporalT, tg, sg, ln = gn, [p[1] for p in prod], modT, gT, acc
        mod_rest = [p[0] for p in prod]

        at[0] = 0
        stack = [[take(NU * W // 2).bitcast(BF16).rearrange("p (n t) -> p n t", n=NU) for _ in range(2)]
                 for _ in range(2)]
        neg_t = [take(W) for _ in range(NT_RING)]
        prob = [take(W) for _ in range(4)]
        probT = [take(W) for _ in range(2)]
        oT = [take(W) for _ in range(2)]
        vx = [take(H * D).rearrange("p (h e) -> p h e", h=H) for _ in range(2)]
        nbias = [take(P) for _ in range(2)]
        dtmp = take(P)
        attn = [take(P) for _ in range(2)]
        attnT = [take(P) for _ in range(2)]
        yout = [take(W).rearrange("p (b c) -> p b c", b=GB) for _ in range(2)]

        c_sb = mod_a[1][:, 0:C_END]
        assert C_END <= 4 * W
        pr = bh[1].rearrange("p j n -> p (j n)")
        nt = D + 2
        sp_a, sp_b, sp_c, sp_d, lna = [pr[:, 64 * k:64 * k + nt] for k in range(5)]
        bl_e, bl_m, bl_s, bl_r, bl_4 = pr[:, 320:352], pr[:, 352:353], pr[:, 353:354], pr[:, 354:355], pr[:, 384:512]
        exp_lt, exp_p, apow = pr[:, 640:768], pr[:, 768:800], pr[:, 800:808]
        arg_a = pr[:, 1024:1536]
        exp_a = pr[:, 1536:2048]
        tau34 = sb("tau34", [P, nt])
        w_lag = mod_a[0][:, 0:Q * P].rearrange("p (q c) -> p q c", q=Q)
        w_rest = mod_a[0][:, Q * P:2 * Q * P].rearrange("p (q c) -> p q c", q=Q)
        w_mid = sb("w_mid", [P, Q, P], BF16)

        ps = [ctx.enter_context(nc.psum_tensor(f"ps{u}", [P, 4, W], F32)) for u in range(2)]

        def bank(u, k):
            return ps[u][:, k, :]

        names = (
            "small_loaded const_loaded x_loaded0 x_loaded1 w_loaded idx_loaded vec_step act_step blend_turned "
            "half_set xT_ps xT_ready ctx_ps ctx_ready wg_ps h1_ps soma_ps gate_tanh h1_ready soma_ready modT_ps "
            "modn_ps modT_tanh modn_tanh gated_ready modT_ready modn_ready mod_part1 mod_rest_ready mod_part2 "
            "mod_part3 mod_part1b mod_a_ready gn_ps gn_ready lag_ps prod_ready lag_added state_ps bh_ready "
            "cross_ps cross_ready crossT_ps temporal_ready temp_ps temp_tanh mixed_ready out_ps aggr_begun "
            "stats_ready moments_ready vareps_ready rstd_ready ln_ready xb_ready scaled_ready x1_ready x1b_ready "
            "x1T_ps x1T_ready q_ps k_ps v_ps qk_f_ready part1_ready rest1_ready part2_ready part3_ready v_stored "
            "a_done stack_loaded0 stack_loaded1 logits_begun score_ps negt_ready shifted prob_ready probT_ps "
            "probT_act probT_dve pv_ps oT_ready on_ps rden_ready attn_ready attnT_ps attnT_ready y_ps y_ready "
            "y_stored0 y_stored1 lncnt_ready neg_lc_ready v_copied bias_a bias_ready vx_zeroed ")
        s = {n: sem(n) for n in names.split()}
        block = ctx.enter_context(nc.Block())

        def at_start(i, m, before):
            return isinstance(i, int) and 2 * i + m < before

        def grp(i, m, k=1, c=0):
            return i * (2 * k) + (m * k + c)

        def group_cols(i, m):
            return bass.ds(i * (2 * W) + m * W, W)

        def group_rows(i, m):
            return bass.ds(i * (2 * GB) + m * GB, GB)

        def by_row(ap):
            return ap.rearrange("p (b c) -> p b c", b=GB)

        def each_row(ap):
            return ap.unsqueeze(1).broadcast_to([P, GB, P])

        def pipeline(eng, front, step, end):
            front(0, 0)
            step(0, 0)
            with eng.Fori(0, G // 2 - 1) as i:
                step(i, 1)
                step(i, 2)
            end()

        x_v = x.rearrange("b t c -> t b c")
        out_v = out.rearrange("b t c -> t b c")
        LAST = G // 2 - 1
        NB2 = 2 * GB

        PEELED = 4

        def row_no(i, n):
            return NB2 * i + n if isinstance(i, int) else PEELED

        def over_rows(eng, step):
            for n in range(PEELED):
                step(0, n)
            with eng.Fori(0, B // NB2 - 1) as i:
                for n in range(PEELED, PEELED + NB2):
                    step(i, n)
            for n in range(PEELED, NB2):
                step(B // NB2 - 1, n)

        EXPS = [1 if z in SHIFTED_BY_POOL else 4 for z in range(NZ)]

        def exps_of(i, c):
            return i * (sum(EXPS) * NB2) + (sum(EXPS) * (c // NZ) + sum(EXPS[:c % NZ]))

        def shifts_of(i, c):
            n = len(SHIFTED_BY_POOL)
            return i * (n * NB2) + (n * (c // NZ) + sum(z in SHIFTED_BY_POOL for z in range(c % NZ)))

        def probT_moved(eng, i, c):
            by_dve = c % NZ in MOVED_BY_DVE
            n = len(MOVED_BY_DVE) if by_dve else NZ - len(MOVED_BY_DVE)
            eng.wait_ge(s["probT_dve" if by_dve else "probT_act"],
                        i * (n * NB2) + (n * (c // NZ) + sum((z in MOVED_BY_DVE) == by_dve for z in range(c % NZ + 1))))

        @block.sync
        def _(sp):
            for dst, src, done in ((rows_sb[:], rows.broadcast_to([P, R_END]), "small_loaded"),
                                   (cols_sb[:], cols, "small_loaded"), (ident, ident_in, "small_loaded"),
                                   (by_row(xn[0]), x_v[:, 0:GB, :], "x_loaded0"), (c_sb, consts, "const_loaded"),
                                   (w_sb[:], w, "w_loaded"), (wn2_sb[:], wn2, "w_loaded"),
                                   (by_row(xn[1]), x_v[:, GB:2 * GB, :], "x_loaded1"),
                                   (idx_i[:], idx, "idx_loaded"), (masks_sb[:], masks, "idx_loaded")):
                sp.dma_start(dst, src).then_inc(s[done], 16)

            def load_x(i, m):
                sp.wait_ge(s["ctx_ps"], grp(i, m, 1, -1))
                sp.wait_ge(s["xb_ready"], grp(i, m, 1, -1))
                sp.dma_start(by_row(xn[m % 2]), x_v[:, group_rows(i, m), :]).then_inc(s[f"x_loaded{m % 2}"], 16)

            with sp.Fori(0, G // 2 - 1) as i:
                for m in (2, 3):
                    load_x(i, m)

            def load_stack(i, u):
                for which, (parts, terms) in enumerate(((q_parts, TERMS_Q), (k_parts, TERMS_K))):
                    for n, part in enumerate(terms):
                        for slot in range(2):
                            r0 = slot * SLOT + n * DH
                            dst = stack[u][which][r0:r0 + DH, :, :]
                            src = parts[slot * SLOT:(slot + 1) * SLOT, part, group_cols(i, u)]
                            sp.dma_start(dst, src).then_inc(s[f"stack_loaded{u}"], 16)

            def store(i, u):
                sp.wait_ge(s["y_ready"], i * NB2 + GB * (u + 1))
                sp.dma_start(out_v[:, group_rows(i, u), :], yout[u]).then_inc(s[f"y_stored{u}"], 16)

            sp.wait_ge(s["out_ps"], G - 1)
            load_stack(0, 0)
            sp.wait_ge(s["a_done"], 4)
            load_stack(0, 1)
            with sp.Fori(0, G // 2 - 1) as i:
                for u in range(2):
                    sp.wait_ge(s["score_ps"], i * (NZ * NB2) + NZ * GB * (u + 1))
                    load_stack(i + 1, u)
                    store(i, u)
            for u in range(2):
                store(G // 2 - 1, u)
            sp.wait_ge(s["y_stored0"], 16 * G // 2)
            sp.wait_ge(s["y_stored1"], 16 * G // 2)

        @block.tensor
        def _(pe):
            pe.wait_ge(s["small_loaded"], 48)
            pe.wait_ge(s["vec_step"], vec("blend_4"))
            pe.transpose(bank(1, 0)[:, 0:P], bl_4, ident).then_inc(s["blend_turned"], 1)

            def four(out_bank, lhs, rhs, done):
                for b in range(GB):
                    cs = slice(b * P, b * P + P)
                    mm = pe.matmul(out_bank[:, cs], lhs(cs), rhs(cs), start=True, stop=True)
                mm.then_inc(s[done], 1)

            def turned(out_bank, src, done):
                for b in range(GB):
                    cs = slice(b * P, b * P + P)
                    mm = pe.transpose(out_bank[:, cs], src[:, cs], ident)
                mm.then_inc(s[done], 1)

            def f_inputs(i, m):
                u = m % 2
                pe.wait_ge(s[f"x_loaded{u}"], i * 16 + 16 * (m // 2 + 1))
                if not at_start(i, m, 2):
                    pe.wait_ge(s["temporal_ready"], grp(i, m, 1, -1))
                turned(bank(u, 0), xn[u], "xT_ps")
                if at_start(i, m, 1):
                    pe.wait_ge(s["vec_step"], vec("lt"))
                four(bank(u, 1), lambda cs: xn[u][:, cs], lambda cs: lt[:], "ctx_ps")

            def f_dense(i, m):
                u = m % 2
                if at_start(i, m, 1):
                    pe.wait_ge(s["w_loaded"], 32)
                pe.wait_ge(s["xT_ready"], grp(i, m, 1, 1))
                pe.matmul(bank(u, 0), wt["wsoma"], xT[u], start=True, stop=True).then_inc(s["soma_ps"], 1)
                pe.matmul(bank(u, 2), wt["wg_x"], xT[u], start=True, stop=False)
                pe.wait_ge(s["ctx_ready"], grp(i, m, 1, 1))
                pe.matmul(bank(u, 2), wt["wg_ctx"], ctxT[u], start=False, stop=True).then_inc(s["wg_ps"], 1)
                if not at_start(i, m, 2):
                    pe.wait_ge(s["ln_ready"], grp(i, m, GB, -GB))
                pe.matmul(bank(u, 3)[0:D, :], wn1, xT[u], start=True, stop=True).then_inc(s["h1_ps"], 1)

            def f_modulation(i, m):
                u = m % 2
                pe.wait_ge(s["h1_ready"], grp(i, m, 1, 1))
                pe.matmul(bank(u, 1), wn2_sb[0:D, :], h1T[u][0:D, :], start=True, stop=True).then_inc(s["modT_ps"], 1)
                for b in range(GB):
                    mm = pe.matmul(bank(u, 3)[:, b * D:b * D + D], h1T[u][0:D + 1, b * P:b * P + P],
                                   wn2_sb[:, 0:D], start=True, stop=True)
                mm.then_inc(s["modn_ps"], 1)

            def f_gated(i, m):
                u = m % 2
                pe.wait_ge(s["gated_ready"], grp(i, m, 1, 1))
                turned(bank(u, 2), gT[u], "gn_ps")

            def f_lags(i, m, lags):
                u = m % 2
                for lag in lags:
                    if lag == 0:
                        pe.wait_ge(s["soma_ready"], grp(i, m, 1, 1))
                        pe.wait_ge(s["mod_part3"], grp(i, m, 1, 1))
                        pe.wait_ge(s["mod_part1b"], grp(i, m, 1, 1))
                        if at_start(i, m, 1):
                            pe.wait_ge(s["vec_step"], vec("w_b2"))
                            pe.wait_ge(s["act_step"], scal("w_b3"))
                    if lag >= 2:
                        pe.wait_ge(s["prod_ready"], grp(i, m, Q, lag - 1))
                    pe.matmul(bank(u, lag % 2), lag_a[:, lag, :], mod_pa[u][:], start=True, stop=False)
                    pe.matmul(bank(u, lag % 2), lag_b[:, lag, :], mod_pb[u][:], start=False, stop=True)\
                        .then_inc(s["lag_ps"], 1)

            def b_states(i, m, blocks):
                u = m % 2
                for j in blocks:
                    if j == 0:
                        pe.wait_ge(s["gn_ready"], grp(i, m, 1, 1))
                    if j == 0 and not at_start(i, m, 2):
                        pe.wait_ge(s["v_stored"], grp(i, m, 1, -1))
                        pe.wait_ge(s["qk_f_ready"], grp(i, m, 2, -2))
                    if j == 1:
                        pe.wait_ge(s["modn_tanh"], grp(i, m, 1, 1))
                    if j >= 2:
                        pe.wait_ge(s["bh_ready"], grp(i, m, NJ, j - 1))
                    for b in range(GB):
                        if j == 0:
                            pe.wait_ge(s["mod_a_ready"], grp(i, m, GB, b + 1))
                        cs = slice(b * P, b * P + P)
                        mm = pe.matmul(bank(u, 2 + j % 2)[:, cs], mod_a[u][:, b * W + j * P:b * W + j * P + P],
                                       gn[u][:, cs], start=True, stop=True)
                    mm.then_inc(s["state_ps"], 1)

            def b_cross(i, m):
                u = m % 2
                pe.wait_ge(s["prod_ready"], grp(i, m, Q, Q))
                pe.wait_ge(s["bh_ready"], grp(i, m, NJ, NJ))
                for j in range(NJ):
                    mm = pe.matmul(bank(u, 0)[32 * j:32 * j + 32, :], decay_p[:], bh[u][:, j, :],
                                   start=True, stop=True)
                mm.then_inc(s["cross_ps"], 1)

            def b_crossT(i, m):
                u = m % 2
                pe.wait_ge(s["cross_ready"], grp(i, m, 1, 1))
                turned(bank(u, 1), crn[u], "crossT_ps")

            def b_gate(i, m):
                u = m % 2
                pe.wait_ge(s["temporal_ready"], grp(i, m, 1, 1))
                pe.matmul(bank(u, 2), wt["wtemp"], temporalT[u], start=True, stop=True).then_inc(s["temp_ps"], 1)

            def b_out(i, m):
                u = m % 2
                if at_start(i, m, 1):
                    pe.wait_ge(s["vec_step"], vec("w_out"))
                pe.wait_ge(s["mixed_ready"], grp(i, m, 1, 1))
                four(bank(u, 3), lambda cs: sg[u][:, cs], lambda cs: wt["wout"], "out_ps")

            def c_x1T(i, m):
                u = m % 2
                pe.wait_ge(s["x1_ready"], grp(i, m, 1, 1))
                pe.wait_ge(s["modn_tanh"], (G if isinstance(i, int) and 2 * i + m > G - 3 else grp(i, m, 1, 3)))
                pe.wait_ge(s["ln_ready"], grp(i, m, GB, GB))
                turned(bank(u, 3), x1g[u], "x1T_ps")

            def c_qk(i, m):
                u = m % 2
                pe.wait_ge(s["gn_ready"], (G if isinstance(i, int) and 2 * i + m > G - 3 else grp(i, m, 1, 3)))
                pe.wait_ge(s["temp_tanh"], grp(i, m, 1, 1))
                pe.wait_ge(s["x1T_ready"], grp(i, m, 1, 1))
                pe.matmul(bank(u, 2), wt["wq"], x1T, start=True, stop=True).then_inc(s["q_ps"], 1)
                pe.matmul(bank(u, 3), wt["wk"], x1T, start=True, stop=True).then_inc(s["k_ps"], 1)

            def c_v(i, m):
                u = m % 2
                pe.wait_ge(s["qk_f_ready"], grp(i, m, 2, 1))
                four(bank(u, 2), lambda cs: x1T[:, cs], lambda cs: wt["wv"], "v_ps")

            def front(i, m):
                f_inputs(i, m)
                f_dense(i, m)
                f_modulation(i, m)
                f_gated(i, m)
                f_lags(i, m, range(Q))

            def step(i, m):
                f_inputs(i, m + 1)
                b_states(i, m, range(0, 2))
                f_dense(i, m + 1)
                b_states(i, m, range(2, NJ))
                f_modulation(i, m + 1)
                b_cross(i, m)
                if not at_start(i, m, 1):
                    c_x1T(i, m - 1)
                f_gated(i, m + 1)
                b_crossT(i, m)
                if not at_start(i, m, 1):
                    c_qk(i, m - 1)
                f_lags(i, m + 1, range(0, 2))
                b_gate(i, m)
                f_lags(i, m + 1, range(2, 4))
                if not at_start(i, m, 1):
                    c_v(i, m - 1)
                f_lags(i, m + 1, range(4, 6))
                b_out(i, m)
                f_lags(i, m + 1, range(6, Q))

            def end():
                b_states(LAST, 1, range(NJ))
                c_x1T(LAST, 0)
                b_cross(LAST, 1)
                c_qk(LAST, 0)
                b_crossT(LAST, 1)
                c_v(LAST, 0)
                b_gate(LAST, 1)
                b_out(LAST, 1)
                c_x1T(LAST, 1)
                c_qk(LAST, 1)
                c_v(LAST, 1)

            pipeline(pe, front, step, end)
            pe.wait_ge(s["v_stored"], G)
            pe.sem_inc(s["a_done"], 1)
            pe.wait_ge(s["a_done"], 4)

            def scores(i, n, z):
                u, b = n // GB % 2, n % GB
                if z == 0 and b == 0:
                    pe.wait_ge(s[f"stack_loaded{u}"], i * (16 * 4 * NT) + 16 * 4 * NT * (1 + n // NB2))
                c = NZ * n + z
                if isinstance(i, int) and NZ * NB2 * i + c < 2:
                    pass
                else:
                    pe.wait_ge(s["negt_ready"], i * (4 * NZ * NB2) + 4 * (c - 1))
                for k in range(4):
                    r0, tile = SLOT * (z % 2), 4 * (z // 2) + k
                    mm = pe.matmul(ps[0][:, c % 2, k * P:k * P + P],
                                   stack[u][0][r0:r0 + KR, tile, b * P:b * P + P],
                                   stack[u][1][r0:r0 + KR, tile, b * P:b * P + P], start=True, stop=True)
                mm.then_inc(s["score_ps"], 1)

            def turn(i, n, z):
                c = NZ * n + z
                pe.wait_ge(s["prob_ready"], exps_of(i, c + 1))
                if not (isinstance(i, int) and NZ * NB2 * i + c < 2):
                    probT_moved(pe, i, c - 2)
                for k in range(4):
                    mm = pe.transpose(ps[0][:, 2 + c % 2, k * P:k * P + P], prob[c % 4][:, k * P:k * P + P], ident)
                mm.then_inc(s["probT_ps"], 1)

            def values(i, n, z):
                c = NZ * n + z
                probT_moved(pe, i, c)
                if z == 0:
                    pe.wait_ge(s["v_copied"], i * NB2 + (n + 1))
                    if row_no(i, n) >= 2:
                        pe.wait_ge(s["oT_ready"], i * NB2 + (n - 1))
                for k in range(4):
                    mm = pe.matmul(ps[1][32 * k:32 * k + 32, n % 2, z * P:z * P + P], vx[n % 2][:, 4 * z + k, :],
                                   probT[c % 2][:, k * P:k * P + P], start=True, stop=True)
                mm.then_inc(s["pv_ps"], 1)

            def turn_o(i, n):
                pe.wait_ge(s["oT_ready"], i * NB2 + (n + 1))
                if not (isinstance(i, int) and NB2 * i + n < 1):
                    pe.wait_ge(s["attn_ready"], i * NB2 + n)
                for z in range(NZ):
                    mm = pe.transpose(ps[1][:, 2, z * P:z * P + P], oT[n % 2][:, z * P:z * P + P], ident)
                mm.then_inc(s["on_ps"], 1)

            def turn_attn(i, n):
                pe.wait_ge(s["attn_ready"], i * NB2 + (n + 1))
                if row_no(i, n) >= 1:
                    pe.wait_ge(s["attnT_ready"], i * NB2 + n)
                    pe.wait_ge(s["y_ready"], i * NB2 + n)
                pe.transpose(ps[1][:, 3, 0:P], attn[n % 2], ident).then_inc(s["attnT_ps"], 1)

            def project(i, n):
                pe.wait_ge(s["attnT_ready"], i * NB2 + (n + 1))
                pe.matmul(ps[1][:, 3, P:2 * P], attnT[n % 2], wt["wo"], start=True, stop=True).then_inc(s["y_ps"], 1)

            def step(i, n):
                for z in range(NZ):
                    turn(i, n, z)
                    row, quad = n + 1 + (z + 1) // NZ, (z + 1) % NZ
                    if row_no(i, row) < B:
                        scores(i, row, quad)
                    if z >= 1:
                        values(i, n, z - 1)
                    elif row_no(i, n) >= 1:
                        values(i, n - 1, NZ - 1)
                    if z == 1 and row_no(i, n) >= 1:
                        turn_o(i, n - 1)
                    if z == 1 and row_no(i, n) >= 2:
                        project(i, n - 2)
                    if z == 3 and row_no(i, n) >= 1:
                        turn_attn(i, n - 1)

            for c in range(NZ + 1):
                scores(0, c // NZ, c % NZ)
            over_rows(pe, step)
            values(B // NB2 - 1, NB2 - 1, NZ - 1)
            project(B // NB2 - 1, NB2 - 2)
            turn_o(B // NB2 - 1, NB2 - 1)
            turn_attn(B // NB2 - 1, NB2 - 1)
            project(B // NB2 - 1, NB2 - 1)

        @block.scalar
        def _(act):
            act.wait_ge(s["small_loaded"], 48)
            act.wait_ge(s["vec_step"], vec("neg_abs_tau"))
            act.activation(sp_b, sp_a, ACT.Exp).then_inc(s["act_step"], 1)
            act.wait_ge(s["act_step"], scal("exp_tau"))
            act.activation(sp_c, sp_b, ACT.Ln, bias=1.0).then_inc(s["act_step"], 1)
            act.wait_ge(s["const_loaded"], 16)
            act.wait_ge(s["vec_step"], vec("log_decay"))
            act.activation(exp_lt, c_sb[:, C_LT:C_LT + P], ACT.Exp, scale=lna[:, D + 1:D + 2])\
                .then_inc(s["act_step"], 1)
            act.wait_ge(s["vec_step"], vec("blend_negmax"))
            act.activation(bl_e, bl, ACT.Exp, bias=bl_m).then_inc(s["act_step"], 1)
            act.activation(exp_p, c_sb[:, C_P:C_P + D], ACT.Exp, scale=lna[:, D:D + 1]).then_inc(s["act_step"], 1)
            act.activation(apow, c_sb[:, C_T:C_T + Q], ACT.Exp, scale=lna[:, D:D + 1]).then_inc(s["act_step"], 1)
            act.wait_ge(s["vec_step"], vec("decay_arg"))
            act.activation(exp_a, arg_a, ACT.Exp).then_inc(s["act_step"], 1)
            act.activation(lam, rows_sb[:, R_U:R_U + B], ACT.Exp, scale=-5.0).then_inc(s["act_step"], 1)

            def f_inputs(i, m):
                u = m % 2
                act.wait_ge(s["xT_ps"], grp(i, m, 1, 1))
                act.activation(xT[u], bank(u, 0), ACT.Copy).then_inc(s["xT_ready"], 1)
                act.wait_ge(s["ctx_ps"], grp(i, m, 1, 1))
                act.activation(ctxT[u], bank(u, 1), ACT.Copy).then_inc(s["ctx_ready"], 1)

            def f_dense(i, m):
                u = m % 2
                act.wait_ge(s["soma_ps"], grp(i, m, 1, 1))
                act.activation(somaT[u], bank(u, 0), ACT.Gelu, bias=col["bsoma"]).then_inc(s["soma_ready"], 1)
                if at_start(i, m, 1):
                    act.wait_ge(s["vec_step"], vec("mod_bias"))
                act.wait_ge(s["wg_ps"], grp(i, m, 1, 1))
                act.activation(th[u], bank(u, 2), ACT.Tanh, bias=hb[:, 0:1], scale=0.5).then_inc(s["gate_tanh"], 1)
                act.wait_ge(s["h1_ps"], grp(i, m, 1, 1))
                act.activation(h1T[u][0:D, :], bank(u, 3)[0:D, :], ACT.Gelu, bias=col["bn1"][0:D, :])\
                    .then_inc(s["h1_ready"], 1)

            def f_modulation(i, m):
                u = m % 2
                act.wait_ge(s["modT_ps"], grp(i, m, 1, 1))
                act.activation(thd[u], bank(u, 1), ACT.Tanh, bias=hb[:, 2:3], scale=0.5).then_inc(s["modT_tanh"], 1)
                act.wait_ge(s["modn_ps"], grp(i, m, 1, 1))
                act.activation(thn[u], bank(u, 3)[:, 0:P], ACT.Tanh, scale=0.5).then_inc(s["modn_tanh"], 1)
                act.wait_ge(s["modT_ready"], grp(i, m, 1, 1))
                act.activation(mod_pb[u][64:96, :], modT[u][64:96, :], ACT.Copy).then_inc(s["mod_part1b"], 1)

            def f_gated(i, m):
                u = m % 2
                act.wait_ge(s["gn_ps"], grp(i, m, 1, 1))
                act.activation(gn[u], bank(u, 2), ACT.Copy).then_inc(s["gn_ready"], 1)

            def b_cross(i, m):
                u = m % 2
                act.wait_ge(s["cross_ps"], grp(i, m, 1, 1))
                act.activation(crn[u], bank(u, 0), ACT.Copy).then_inc(s["cross_ready"], 1)

            def b_gate(i, m):
                u = m % 2
                act.wait_ge(s["temp_ps"], grp(i, m, 1, 1))
                act.activation(tg[u], bank(u, 2), ACT.Tanh, bias=hb[:, 1:2], scale=0.5).then_inc(s["temp_tanh"], 1)

            def c_x1T(i, m):
                u = m % 2
                act.wait_ge(s["x1T_ps"], grp(i, m, 1, 1))
                if not at_start(i, m, 1):
                    act.wait_ge(s["v_ps"], grp(i, m, 1, 0))
                act.activation(x1T, bank(u, 3), ACT.Copy).then_inc(s["x1T_ready"], 1)

            def c_qk(i, m):
                u = m % 2
                if not at_start(i, m, 1):
                    act.wait_ge(s["rest1_ready"], grp(i, m, 2, 0))
                act.wait_ge(s["q_ps"], grp(i, m, 1, 1))
                act.activation(qk_f[0], bank(u, 2), ACT.Identity, bias=hb[:, 3:4], scale=-SCALE)\
                    .then_inc(s["qk_f_ready"], 1)
                act.wait_ge(s["k_ps"], grp(i, m, 1, 1))
                act.activation(qk_f[1], bank(u, 3), ACT.Identity, bias=hb[:, 4:5]).then_inc(s["qk_f_ready"], 1)
                for n, parts in enumerate((q_parts, k_parts)):
                    act.wait_ge(s["qk_f_ready"], grp(i, m, 2, n + 1))
                    act.activation(parts[:, 0, group_cols(i, m)], qk_f[n], ACT.Copy).then_inc(s["part1_ready"], 1)

            def front(i, m):
                f_inputs(i, m)
                f_dense(i, m)
                act.wait_ge(s["vec_step"], vec("w_lag"))
                act.activation(lag_a[:], w_lag, ACT.Copy).then_inc(s["act_step"], 1)
                act.activation(lag_b[96:128], w_lag[96:128], ACT.Copy).then_inc(s["act_step"], 1)
                f_modulation(i, m)
                f_gated(i, m)

            def step(i, m):
                f_inputs(i, m + 1)
                f_dense(i, m + 1)
                f_modulation(i, m + 1)
                b_cross(i, m)
                if not at_start(i, m, 1):
                    c_x1T(i, m - 1)
                f_gated(i, m + 1)
                if not at_start(i, m, 1):
                    c_qk(i, m - 1)
                b_gate(i, m)

            def end():
                c_x1T(LAST, 0)
                b_cross(LAST, 1)
                c_qk(LAST, 0)
                b_gate(LAST, 1)
                c_x1T(LAST, 1)
                c_qk(LAST, 1)

            pipeline(act, front, step, end)
            act.wait_ge(s["vec_step"], vec("cnt_one"))
            act.activation(lncnt[:], cnt1[:], ACT.Ln).then_inc(s["lncnt_ready"], 1)
            act.wait_ge(s["part1_ready"], 2 * G)
            act.sem_inc(s["a_done"], 1)
            act.wait_ge(s["a_done"], 4)

            def exps(i, n, z):
                c = NZ * n + z
                if not (isinstance(i, int) and NZ * NB2 * i + c < 4):
                    act.wait_ge(s["probT_ps"], i * (NZ * NB2) + (c - 3))
                if z in SHIFTED_BY_POOL:
                    act.wait_ge(s["shifted"], shifts_of(i, c + 1))
                    act.activation(prob[c % 4], neg_t[c % NT_RING], ACT.Exp, scale=-1.0).then_inc(s["prob_ready"], 1)
                    return
                for k in range(4):
                    act.wait_ge(s["negt_ready"], i * (4 * NZ * NB2) + (4 * c + k + 1))
                    act.activation(prob[c % 4][:, k * P:k * P + P], neg_t[c % NT_RING][:, k * P:k * P + P], ACT.Exp,
                                   bias=neg_max[:, n % 2, 4 * z + k:4 * z + k + 1], scale=-1.0)\
                        .then_inc(s["prob_ready"], 1)

            def move(i, n, z):
                c = NZ * n + z
                act.wait_ge(s["probT_ps"], i * (NZ * NB2) + (c + 1))
                if not (isinstance(i, int) and NZ * NB2 * i + c < 2):
                    act.wait_ge(s["pv_ps"], i * (NZ * NB2) + (c - 1))
                act.activation(probT[c % 2], ps[0][:, 2 + c % 2, :], ACT.Copy).then_inc(s["probT_act"], 1)

            def move_o(i, n):
                act.wait_ge(s["pv_ps"], i * (NZ * NB2) + NZ * (n + 1))
                act.activation(oT[n % 2], ps[1][:, n % 2, :], ACT.Copy).then_inc(s["oT_ready"], 1)

            def move_attn(i, n):
                act.wait_ge(s["attnT_ps"], i * NB2 + (n + 1))
                act.activation(attnT[n % 2], ps[1][:, 3, 0:P], ACT.Copy).then_inc(s["attnT_ready"], 1)

            def step(i, n):
                for z in range(NZ):
                    if z not in MOVED_BY_DVE:
                        move(i, n, z)
                    if z == 0 and row_no(i, n) >= 1:
                        move_o(i, n - 1)
                    if z == 0 and row_no(i, n) >= 2:
                        move_attn(i, n - 2)
                    row, quad = n + (z + 3) // NZ, (z + 3) % NZ
                    if row_no(i, row) < B:
                        exps(i, row, quad)

            for z in range(3):
                exps(0, 0, z)
            over_rows(act, step)
            move_o(B // NB2 - 1, NB2 - 1)
            move_attn(B // NB2 - 1, NB2 - 2)
            move_attn(B // NB2 - 1, NB2 - 1)

        @block.vector
        def _(dve):
            count = [0]

            def pro(name, ins):
                count[0] += 1
                assert VEC_STEPS[count[0] - 1] == name, name
                ins.then_inc(s["vec_step"], 1)
                dve.wait_ge(s["vec_step"], count[0])

            for n in range(2):
                dve.memset(mod_pb[n][0:64, :], 0.0).then_inc(s["half_set"], 1)
            dve.memset(lag_b[0:64], 0.0).then_inc(s["half_set"], 1)
            dve.wait_ge(s["small_loaded"], 48)
            dve.tensor_copy(tau34[:, 0:D], rows_sb[:, R_TAU:R_TAU + D]).then_inc(s["half_set"], 1)
            dve.tensor_copy(tau34[:, D:D + 1], col["tau4"]).then_inc(s["half_set"], 1)
            dve.tensor_copy(tau34[:, D + 1:D + 2], rows_sb[:, R_TAU + D:R_TAU + D + 1]).then_inc(s["half_set"], 1)
            dve.wait_ge(s["half_set"], 6)
            pro("neg_abs_tau", dve.scalar_tensor_tensor(sp_a, tau34[:], -1.0, tau34[:], ALU.mult, ALU.min))
            pro("neg_relu_tau", dve.tensor_scalar(sp_d, tau34[:], 0.0, -1.0, ALU.max, ALU.mult))
            pro("gate_biases", dve.tensor_scalar(hb[:, 0:2], cols_sb[:, 0:3:2], 0.5, None, ALU.mult))
            pro("mod_bias", dve.tensor_scalar(hb[:, 2:3], col["bmod"], 0.5, None, ALU.mult))
            pro("q_bias", dve.tensor_scalar(hb[:, 3:4], col["bq"], -SCALE, None, ALU.mult))
            pro("k_bias", dve.tensor_copy(hb[:, 4:5], col["bk"]))
            pro("ones0", dve.memset(h1T[0][D:D + 1, :], 1.0))
            pro("ones1", dve.memset(h1T[1][D:D + 1, :], 1.0))
            dve.wait_ge(s["const_loaded"], 16)
            pro("key_no", dve.tensor_copy(key_no[:], c_sb[:, C_K:C_K + P]))
            dve.wait_ge(s["act_step"], scal("softplus"))
            pro("log_decay", dve.tensor_tensor(lna, sp_d, sp_c, ALU.subtract))
            dve.wait_ge(s["act_step"], scal("lt"))
            pro("lt", dve.tensor_tensor(lt[:], exp_lt, c_sb[:, C_LTM:C_LTM + P], ALU.mult))
            pro("blend_max", dve.tensor_reduce(bl_s, bl, AX_X, ALU.max))
            pro("blend_negmax", dve.tensor_scalar(bl_m, bl_s, -1.0, None, ALU.mult))
            pro("decay_arg", dve.tensor_tensor(arg_a.rearrange("p (k d) -> p k d", d=D),
                                               c_sb[:, C_A:C_A + NCH * D].rearrange("p (k d) -> p k d", d=D),
                                               lna[:, 0:D].unsqueeze(1).broadcast_to([P, NCH, D]), ALU.mult))
            dve.wait_ge(s["act_step"], scal("exp_blend"))
            pro("blend_sum", dve.tensor_reduce(bl_s, bl_e, AX_X, ALU.add))
            pro("blend_recip", dve.reciprocal(bl_r, bl_s))
            pro("blend_4", dve.tensor_scalar(bl_4.rearrange("p (k d) -> p k d", d=D),
                                             bl_e.unsqueeze(1).broadcast_to([P, 4, D]), bl_r, 0.5,
                                             ALU.mult, ALU.mult))
            dve.wait_ge(s["blend_turned"], 1)
            pro("half_bw", dve.tensor_copy(half_bw[:], bank(1, 0)[:, 0:P]))
            dve.wait_ge(s["act_step"], scal("decay_a"))
            pro("decay_p", dve.tensor_tensor(decay_p[:], exp_p, c_sb[:, C_PM:C_PM + D], ALU.mult))
            pro("decay_a", dve.tensor_tensor(decay_a[:].rearrange("p k d -> p (k d)"), exp_a,
                                             c_sb[:, C_AM:C_AM + NCH * D], ALU.mult))
            pro("w_lag", dve.tensor_tensor(w_lag, half_bw[:].unsqueeze(1).broadcast_to([P, Q, P]),
                                           apow.unsqueeze(2).broadcast_to([P, Q, P]), ALU.mult))
            dve.wait_ge(s["act_step"], scal("w_a"))
            pro("w_rest", dve.tensor_tensor(w_rest, w_lag, lag_a[:], ALU.subtract))
            pro("w_a1", dve.tensor_copy(lag_a[32:64], w_rest[32:64]))
            pro("w_a3", dve.tensor_copy(lag_a[96:128], w_rest[96:128]))
            pro("w_mid", dve.tensor_copy(w_mid[64:96], w_rest[64:96]))
            pro("w_b2", dve.tensor_tensor(lag_b[64:96], w_rest[64:96], w_mid[64:96], ALU.subtract))

            def late_tables():
                pro("w_out", dve.tensor_scalar(wt["wout"], wt["wout"], 0.5, None, ALU.mult))
                dve.wait_ge(s["idx_loaded"], 32)
                pro("idx_f", dve.tensor_copy(idx_f, idx_i[:]))
                pro("mask_f", dve.tensor_copy(im_f, masks_sb[:, P:P + K_SPARSE]))
                pro("idx_plus", dve.scalar_tensor_tensor(idx_m[:], idx_f, 1.0, im_f, ALU.add, ALU.mult))
                pro("idx_masked", dve.tensor_scalar(idx_m[:], idx_m[:], -1.0, None, ALU.add))
                pro("not_prior", dve.tensor_scalar(not_prior[:], masks_sb[:, 0:P], -1.0, 1.0, ALU.mult, ALU.add))
                dve.wait_ge(s["act_step"], scal("exp_u"))
                pro("lam", dve.tensor_scalar(lam, lam, 10.0, None, ALU.mult))
                pro("use", dve.tensor_scalar(use_b[:], lam, 1.0, None, ALU.is_ge))
                pro("not_use", dve.tensor_scalar(not_use, use_b[:], -1.0, 1.0, ALU.mult, ALU.add))
                pro("dense_lam", dve.tensor_tensor(dense_lam[:], not_use, lam, ALU.mult))
                pro("cnt_start", dve.memset(cnt[0][:], 0.0))
                for j in range(K_SPARSE):
                    pro(f"cnt{j}", dve.scalar_tensor_tensor(cnt[(j + 1) % 2][:], key_no[:],
                                                            idx_m[:, j:j + 1], cnt[j % 2][:],
                                                            ALU.is_equal, ALU.add))
                pro("cnt_one", dve.tensor_scalar(cnt1[:], cnt[0][:], 1.0, None, ALU.max))
                pro("cnt_none", dve.tensor_scalar(cnt[1][:], cnt[0][:], 0.0, BIG, ALU.is_equal, ALU.mult))

            def chunks(ap, a, b):
                return ap.rearrange("p (n q) -> p n q", q=Q)[:, :, a:b]

            def packed(ap, lag):
                return ap[:, 0:(W // Q) * (Q - lag)].rearrange("p (n q) -> p n q", q=Q - lag)

            def f_gated(i, m):
                u = m % 2
                dve.wait_ge(s["xT_ready"], grp(i, m, 1, 1))
                dve.wait_ge(s["gate_tanh"], grp(i, m, 1, 1))
                dve.scalar_tensor_tensor(gT[u], th[u], 1.0, xT[u], ALU.add, ALU.mult).then_inc(s["gated_ready"], 1)

            def f_modulation(i, m):
                u = m % 2
                dve.wait_ge(s["modT_tanh"], grp(i, m, 1, 1))
                dve.tensor_scalar(modT[u], thd[u], 0.5, 1.0, ALU.mult, ALU.add).then_inc(s["modT_ready"], 1)
                dve.tensor_scalar(mod_pa[u][:], thd[u], 0.5, 1.0, ALU.mult, ALU.add).then_inc(s["mod_part1"], 1)
                dve.wait_ge(s["modn_tanh"], grp(i, m, 1, 1))
                dve.tensor_scalar(modn[u], thn[u], 0.5, 1.0, ALU.mult, ALU.add).then_inc(s["modn_ready"], 1)
                dve.wait_ge(s["modT_ready"], grp(i, m, 1, 1))
                dve.wait_ge(s["mod_part1"], grp(i, m, 1, 1))
                dve.tensor_tensor(mod_rest[u], modT[u], mod_pa[u][:], ALU.subtract).then_inc(s["mod_rest_ready"], 1)
                dve.wait_ge(s["mod_rest_ready"], grp(i, m, 1, 1))
                dve.tensor_copy(mod_pa[u][64:128, :], mod_rest[u][64:128, :]).then_inc(s["mod_part2"], 1)
                dve.wait_ge(s["mod_part2"], grp(i, m, 1, 1))
                dve.tensor_tensor(mod_pb[u][96:128, :], mod_rest[u][96:128, :], mod_pa[u][96:128, :],
                                  ALU.subtract).then_inc(s["mod_part3"], 1)

            def f_lags(i, m, lags):
                u = m % 2
                for lag in lags:
                    dve.wait_ge(s["lag_ps"], grp(i, m, Q, lag + 1))
                    if lag == 0:
                        if not at_start(i, m, 2):
                            dve.wait_ge(s["x1_ready"], grp(i, m, 1, -1))
                        dve.tensor_tensor(acc[u], bank(u, 0), gT[u], ALU.mult).then_inc(s["prod_ready"], 1)
                        continue
                    if lag >= 3:
                        dve.wait_ge(s["lag_added"], grp(i, m, Q - 1, lag - 2))
                    dve.tensor_tensor(packed(prod[u][lag % 2], lag), chunks(bank(u, lag % 2), 0, Q - lag),
                                      chunks(gT[u], 0, Q - lag), ALU.mult).then_inc(s["prod_ready"], 1)

            def b_states(i, m, blocks):
                u = m % 2
                for j in blocks:
                    dve.wait_ge(s["state_ps"], grp(i, m, NJ, j + 1))
                    dve.tensor_tensor(by_row(bh[u][:, j, :]), by_row(bank(u, 2 + j % 2)), each_row(half_bw[:]),
                                      ALU.mult).then_inc(s["bh_ready"], 1)

            def b_temporal(i, m):
                u = m % 2
                dve.wait_ge(s["lag_added"], grp(i, m, Q - 1, Q - 1))
                dve.wait_ge(s["crossT_ps"], grp(i, m, 1, 1))
                dve.tensor_tensor(temporalT[u], bank(u, 1), acc[u], ALU.add).then_inc(s["temporal_ready"], 1)

            def b_mixed(i, m):
                u = m % 2
                dve.wait_ge(s["temp_tanh"], grp(i, m, 1, 1))
                dve.scalar_tensor_tensor(sg[u], tg[u], 1.0, somaT[u], ALU.add, ALU.mult)\
                    .then_inc(s["mixed_ready"], 1)

            def c_moments(i, m):
                u = m % 2
                dve.wait_ge(s["out_ps"], grp(i, m, 1, 1))
                for b in range(GB):
                    dve.bn_stats(stats[:, u, b, :], bank(u, 3)[:, b * P:b * P + P]).then_inc(s["stats_ready"], 1)
                dve.wait_ge(s["stats_ready"], grp(i, m, GB, GB))
                dve.sem_inc(s["aggr_begun"], 1)
                for b in range(GB):
                    dve.bn_aggr(moments[:, u, b, :], stats[:, u, b, :]).then_inc(s["moments_ready"], 1)
                dve.wait_ge(s["moments_ready"], grp(i, m, GB, GB))
                dve.tensor_scalar(vareps[:, u, :], moments[:, u, :, 1], 1e-5, None, ALU.add)\
                    .then_inc(s["vareps_ready"], 1)

            def c_norm(i, m):
                u = m % 2
                dve.wait_ge(s["rstd_ready"], grp(i, m, 1, 1))
                for b in range(GB):
                    cs = slice(b * P, b * P + P)
                    dve.tensor_scalar(ln[u][:, cs], bank(u, 3)[:, cs], moments[:, u, b, 0:1], rstd[:, u, b:b + 1],
                                      ALU.subtract, ALU.mult).then_inc(s["ln_ready"], 1)

            def c_split(i, m, which):
                col_ = group_cols(i, m)
                for n, parts in ((which, (q_parts, k_parts)[which]),):
                    dve.wait_ge(s["part1_ready"], grp(i, m, 2, n + 1))
                    if not (n == 0 and at_start(i, m, 1)):
                        dve.wait_ge(s["part3_ready"], grp(i, m, 2, n))
                    dve.tensor_tensor(rest, qk_f[n], parts[:, 0, col_], ALU.subtract).then_inc(s["rest1_ready"], 1)
                    dve.wait_ge(s["rest1_ready"], grp(i, m, 2, n + 1))
                    dve.tensor_copy(parts[:, 1, col_], rest).then_inc(s["part2_ready"], 1)
                    dve.wait_ge(s["part2_ready"], grp(i, m, 2, n + 1))
                    dve.tensor_tensor(parts[:, 2, col_], rest, parts[:, 1, col_], ALU.subtract)\
                        .then_inc(s["part3_ready"], 1)

            def c_values(i, m):
                u = m % 2
                dve.wait_ge(s["v_ps"], grp(i, m, 1, 1))
                dve.tensor_tensor(v_all[:, group_rows(i, m), :], by_row(bank(u, 2)), each_row(bv), ALU.add)\
                    .then_inc(s["v_stored"], 1)

            def front(i, m):
                f_gated(i, m)
                f_modulation(i, m)
                f_lags(i, m, range(Q))
                late_tables()

            def step(i, m):
                if not at_start(i, m, 1):
                    c_moments(i, m - 1)
                b_states(i, m, range(0, 1))
                if not at_start(i, m, 1):
                    c_norm(i, m - 1)
                b_states(i, m, range(1, 2))
                f_gated(i, m + 1)
                b_states(i, m, range(2, NJ))
                f_modulation(i, m + 1)
                b_temporal(i, m)
                f_lags(i, m + 1, range(0, 4))
                b_mixed(i, m)
                if not at_start(i, m, 1):
                    c_values(i, m - 1)
                f_lags(i, m + 1, range(4, 5))
                if not at_start(i, m, 1):
                    c_split(i, m - 1, 0)
                f_lags(i, m + 1, range(5, 6))
                if not at_start(i, m, 1):
                    c_split(i, m - 1, 1)
                f_lags(i, m + 1, range(6, Q))

            def end():
                c_moments(LAST, 0)
                b_states(LAST, 1, range(0, 1))
                c_norm(LAST, 0)
                b_states(LAST, 1, range(1, NJ))
                b_temporal(LAST, 1)
                c_values(LAST, 0)
                b_mixed(LAST, 1)
                c_split(LAST, 0, 0)
                c_moments(LAST, 1)
                c_norm(LAST, 1)
                c_split(LAST, 0, 1)
                c_values(LAST, 1)
                for which in range(2):
                    c_split(LAST, 1, which)

            pipeline(dve, front, step, end)
            dve.wait_ge(s["lncnt_ready"], 1)
            dve.tensor_tensor(neg_lc[:], cnt[1][:], lncnt[:], ALU.subtract).then_inc(s["neg_lc_ready"], 1)
            dve.wait_ge(s["part3_ready"], 2 * G)
            dve.sem_inc(s["a_done"], 1)
            dve.wait_ge(s["a_done"], 4)

            def logits(i, n, z):
                c = NZ * n + z
                if z == 0:
                    dve.wait_ge(s["bias_ready"], i * NB2 + (n + 1))
                if not (isinstance(i, int) and NZ * NB2 * i + c < NT_RING):
                    dve.wait_ge(s["prob_ready"], exps_of(i, c - NT_RING + 1))
                dve.wait_ge(s["score_ps"], i * (NZ * NB2) + (c + 1))
                dve.sem_inc(s["logits_begun"], 1)
                for k in range(4):
                    cs = slice(k * P, k * P + P)
                    h = 4 * z + k
                    dve.tensor_tensor_reduce(out=neg_t[c % NT_RING][:, cs], in0=ps[0][:, c % 2, cs], in1=nbias[n % 2],
                                             scale=1.0, scalar=3.0e38, op0=ALU.add, op1=ALU.min,
                                             accum_out=neg_max[:, n % 2, h:h + 1]).then_inc(s["negt_ready"], 1)

            def move(i, n, z):
                c = NZ * n + z
                if not (isinstance(i, int) and NZ * NB2 * i + c < 2):
                    dve.wait_ge(s["pv_ps"], i * (NZ * NB2) + (c - 1))
                dve.wait_ge(s["probT_ps"], i * (NZ * NB2) + (c + 1))
                dve.tensor_copy(probT[c % 2], ps[0][:, 2 + c % 2, :]).then_inc(s["probT_dve"], 1)

            def normalise(i, n):
                dve.wait_ge(s["on_ps"], i * NB2 + (n + 1))
                o = ps[1][:, 2, :].rearrange("p (h e) -> p h e", e=D)
                dve.reciprocal(rden[:, n % 2, :], o[:, :, DH]).then_inc(s["rden_ready"], 1)
                dve.wait_ge(s["rden_ready"], i * NB2 + (n + 1))
                dve.tensor_tensor(attn[n % 2].rearrange("p (h e) -> p h e", e=DH), o[:, :, 0:DH],
                                  rden[:, n % 2, :].unsqueeze(2).broadcast_to([P, H, DH]), ALU.mult)\
                    .then_inc(s["attn_ready"], 1)

            def result(i, n):
                dve.wait_ge(s["y_ps"], i * NB2 + (n + 1))
                u, b = n // GB % 2, n % GB
                if b == 0 and not (isinstance(i, int) and NB2 * i + n < NB2):
                    dve.wait_ge(s[f"y_stored{u}"], i * 16 + 16 * (n // NB2))
                dve.tensor_tensor(yout[u][:, b, :], ps[1][:, 3, P:2 * P], x1b_all[:, i * NB2 + n, :]
                                  if isinstance(i, int) else x1b_all[:, bass.ds(i * NB2 + n, 1), :]
                                  .rearrange("p a c -> p (a c)"), ALU.add).then_inc(s["y_ready"], 1)

            def step(i, n):
                for z in range(NZ):
                    if row_no(i, n + 1) < B:
                        logits(i, n + 1, z)
                    if z in MOVED_BY_DVE:
                        move(i, n, z)
                    if z == 2 and row_no(i, n) >= 2:
                        result(i, n - 2)
                    if z == 2 and row_no(i, n) >= 1:
                        normalise(i, n - 1)

            for z in range(NZ):
                logits(0, 0, z)
            over_rows(dve, step)
            result(B // NB2 - 1, NB2 - 2)
            normalise(B // NB2 - 1, NB2 - 1)
            result(B // NB2 - 1, NB2 - 1)

        @block.gpsimd
        def _(pool):
            pool.memset(minus_half[:], -0.5).then_inc(s["x1b_ready"], 1)
            pool.wait_ge(s["x1b_ready"], 1)
            pool.wait_ge(s["small_loaded"], 48)

            def f_inputs(i, m):
                u = m % 2
                if not at_start(i, m, 2):
                    pool.wait_ge(s["x1_ready"], grp(i, m, 1, -1))
                pool.wait_ge(s[f"x_loaded{u}"], i * 16 + 16 * (m // 2 + 1))
                pool.tensor_tensor(by_row(xb[u]), by_row(xn[u]), each_row(beta), ALU.add).then_inc(s["xb_ready"], 1)

            def f_decayed(i, m):
                u = m % 2
                pool.wait_ge(s["modn_ready"], grp(i, m, 1, 1))
                if at_start(i, m, 1):
                    pool.wait_ge(s["vec_step"], vec("w_b2"))
                for b in range(GB):
                    pool.tensor_tensor(mod_a[u][:, b * W:b * W + W].rearrange("p (k d) -> p k d", d=D), decay_a[:],
                                       modn[u][:, b * D:b * D + D].unsqueeze(1).broadcast_to([P, NCH, D]),
                                       ALU.mult).then_inc(s["mod_a_ready"], 1)

            def f_lags(i, m):
                u = m % 2
                for lag in range(1, Q):
                    pool.wait_ge(s["prod_ready"], grp(i, m, Q, lag + 1))
                    if lag >= 2:
                        pool.wait_ge(s["lag_added"], grp(i, m, Q - 1, lag - 1))
                    a = acc[u].rearrange("p (n q) -> p n q", q=Q)[:, :, lag:Q]
                    pr_ = prod[u][lag % 2][:, 0:(W // Q) * (Q - lag)].rearrange("p (n q) -> p n q", q=Q - lag)
                    pool.tensor_tensor(a, a, pr_, ALU.add).then_inc(s["lag_added"], 1)

            def c_rstd(i, m):
                u = m % 2
                pool.wait_ge(s["vareps_ready"], grp(i, m, 1, 1))
                pool.tensor_tensor(rstd[:, u, :], vareps[:, u, :], minus_half[:], ALU.pow).then_inc(s["rstd_ready"], 1)

            def c_residual(i, m):
                u = m % 2
                pool.wait_ge(s["ln_ready"], grp(i, m, GB, GB))
                pool.tensor_tensor(by_row(ln[u]), by_row(ln[u]), each_row(gamma), ALU.mult)\
                    .then_inc(s["scaled_ready"], 1)
                pool.wait_ge(s["scaled_ready"], grp(i, m, 1, 1))
                pool.wait_ge(s["xb_ready"], grp(i, m, 1, 1))
                pool.tensor_tensor(x1g[u], ln[u], xb[u], ALU.add).then_inc(s["x1_ready"], 1)

            def c_keep(i, m):
                u = m % 2
                pool.wait_ge(s["x1_ready"], grp(i, m, 1, 1))
                pool.tensor_tensor(x1b_all[:, group_rows(i, m), :], by_row(x1g[u]), each_row(bo), ALU.add)\
                    .then_inc(s["x1b_ready"], 1)

            def front(i, m):
                f_inputs(i, m)
                f_decayed(i, m)
                f_lags(i, m)

            def step(i, m):
                if not at_start(i, m, 1):
                    c_rstd(i, m - 1)
                    c_residual(i, m - 1)
                f_inputs(i, m + 1)
                if not at_start(i, m, 1):
                    c_keep(i, m - 1)
                f_decayed(i, m + 1)
                f_lags(i, m + 1)

            def end():
                for m in range(2):
                    c_rstd(LAST, m)
                    c_residual(LAST, m)
                    c_keep(LAST, m)

            pipeline(pool, front, step, end)
            pool.wait_ge(s["x1b_ready"], G + 1)
            pool.sem_inc(s["a_done"], 1)
            pool.wait_ge(s["a_done"], 4)

            for n in range(2):
                pool.memset(vx[n], 0.0).then_inc(s["vx_zeroed"], 1)
            for n in range(2):
                pool.wait_ge(s["vx_zeroed"], n + 1)
                pool.memset(vx[n][:, :, DH:DH + 1], 1.0).then_inc(s["vx_zeroed"], 1)
            pool.wait_ge(s["vx_zeroed"], 4)

            def row_of(ap, i, n):
                return ap[:, i * NB2 + n:i * NB2 + n + 1] if isinstance(i, int) else ap[:, bass.ds(i * NB2 + n, 1)]

            def prepare_bias(i, n):
                first = isinstance(i, int) and NB2 * i + n < 2
                if not first:
                    pool.wait_ge(s["negt_ready"], i * (4 * NZ * NB2) + 4 * NZ * (n - 1))
                if isinstance(i, int) and NB2 * i + n == 0:
                    pool.wait_ge(s["neg_lc_ready"], 1)
                else:
                    pool.wait_ge(s["bias_ready"], i * NB2 + n)
                pool.tensor_tensor(nbias[n % 2], neg_lc[:], row_of(use_b, i, n).broadcast_to([P, P]), ALU.mult)\
                    .then_inc(s["bias_a"], 1)
                pool.tensor_tensor(dtmp, not_prior[:], row_of(dense_lam, i, n).broadcast_to([P, P]), ALU.mult)\
                    .then_inc(s["bias_a"], 1)
                pool.wait_ge(s["bias_a"], i * (2 * NB2) + 2 * (n + 1))
                pool.tensor_tensor(nbias[n % 2], nbias[n % 2], dtmp, ALU.add).then_inc(s["bias_ready"], 1)

            def prepare_values(i, n):
                if not (isinstance(i, int) and NB2 * i + n < 2):
                    pool.wait_ge(s["pv_ps"], i * (NZ * NB2) + NZ * (n - 1))
                v = v_all[:, i * NB2 + n, :] if isinstance(i, int) else \
                    v_all[:, bass.ds(i * NB2 + n, 1), :].rearrange("p a c -> p (a c)")
                pool.tensor_copy(vx[n % 2][:, :, 0:DH], v.rearrange("p (h e) -> p h e", e=DH))\
                    .then_inc(s["v_copied"], 1)

            def shift(i, n, z):
                c = NZ * n + z
                pool.wait_ge(s["negt_ready"], i * (4 * NZ * NB2) + 4 * (c + 1))
                t4 = neg_t[c % NT_RING].rearrange("p (h k) -> p h k", h=4)
                pool.tensor_tensor(t4, t4, neg_max[:, n % 2, 4 * z:4 * z + 4].unsqueeze(2).broadcast_to([P, 4, P]),
                                   ALU.subtract).then_inc(s["shifted"], 1)

            def step(i, n):
                for z in SHIFTED_BY_POOL:
                    if row_no(i, n + 1) < B:
                        shift(i, n + 1, z)
                    if z == SHIFTED_BY_POOL[0] and row_no(i, n + 2) < B:
                        prepare_bias(i, n + 2)
                if row_no(i, n + 2) < B:
                    prepare_values(i, n + 2)

            for n in range(2):
                prepare_bias(0, n)
                prepare_values(0, n)
            for z in SHIFTED_BY_POOL:
                shift(0, 0, z)
            over_rows(pool, step)


_ORDER = ["x", "w", "wn2", "cols", "rows", "consts", "ident", "idx", "masks"]


def shape_constants():
    c = np.zeros((P, C_END), np.float32)
    r = np.arange(P)
    lag = r[None, :] - r[:, None]
    c[:, C_LT:C_LT + P] = np.maximum(lag, 0)
    c[:, C_LTM:C_LTM + P] = lag >= 0
    to_start = np.repeat(np.arange(NCH) * Q, D)[None, :] - r[:, None]
    c[:, C_A:C_A + NCH * D] = np.maximum(to_start, 0)
    c[:, C_AM:C_AM + NCH * D] = to_start > 0
    inside = np.arange(D)[None, :] - (r // D * Q)[:, None]
    c[:, C_P:C_P + D] = np.clip(inside, 0, Q)
    c[:, C_PM:C_PM + D] = (inside >= 0) & (inside < Q)
    c[:, C_T:C_T + Q] = np.arange(Q)[None, :]
    c[:, C_K:C_K + P] = r[None, :]
    return c


def kernel(x, condB_tauraws, cond_256, condB_bn2, cond_1024, itok_Sx32_0_1023, condB_uprev, mask_SxS_bk0,
           mask_Sx32_bk1, L0_cond_tau_ctx, L0_cond_Wg, L0_cond_bg, L0_cond_Wn1, L0_cond_bn1, L0_cond_Wsoma,
           L0_cond_bsoma, L0_cond_Wtemp, L0_cond_btemp, L0_cond_Wout, L0_cond_gamma, L0_cond_beta, L1_cond_Wq,
           L1_cond_bq, L1_cond_Wk, L1_cond_bk, L1_cond_Wv, L1_cond_bv, L1_cond_Wo, L1_cond_bo):
    import concourse.bacc as bacc
    from concourse.bass_utils import run_bass_kernel_spmd

    def arr(a):
        return np.asarray(a)

    order = np.arange(P).reshape(NZ // 2, 2, 4, DH).transpose(1, 3, 0, 2).reshape(P)
    wg = arr(L0_cond_Wg).T
    weights = [wg[0:P], wg[P:2 * P], arr(L0_cond_Wsoma).T, arr(L0_cond_Wtemp).T, arr(L0_cond_Wout).T,
               arr(L1_cond_Wq)[order].T, arr(L1_cond_Wk)[order].T, arr(L1_cond_Wv).T, arr(L1_cond_Wo).T]
    taus = arr(condB_tauraws)
    four = P // D
    bn2 = np.tile(arr(condB_bn2), four)
    columns = {"bg": L0_cond_bg, "bsoma": L0_cond_bsoma, "btemp": L0_cond_btemp, "bq": arr(L1_cond_bq)[order],
               "bk": arr(L1_cond_bk)[order], "bmod": bn2, "bn1": np.tile(arr(L0_cond_bn1), four),
               "tau4": np.tile(taus, four)}
    arrays = {
        "x": arr(x),
        "w": np.stack(weights, axis=1),
        "wn2": np.concatenate([np.tile(arr(cond_256).T, (1, four)), bn2[None, :]]),
        "cols": np.concatenate([np.stack([arr(columns[n]) for n in COLS], axis=1), arr(L0_cond_Wn1).T,
                                arr(cond_1024).T], axis=1),
        "rows": np.concatenate([arr(L0_cond_gamma), arr(L0_cond_beta), arr(L1_cond_bo), arr(L1_cond_bv), taus,
                                arr(L0_cond_tau_ctx).reshape(1), arr(condB_uprev)])[None, :],
        "consts": shape_constants(),
        "ident": np.eye(P, dtype=np.float32),
        "idx": arr(itok_Sx32_0_1023),
        "masks": np.concatenate([arr(mask_SxS_bk0), arr(mask_Sx32_bk1)], axis=1),
    }
    nc = bacc.Bacc("TRN2", target_bir_lowering=False, num_devices=1)
    ins, args = {}, []
    for name in _ORDER:
        a = np.ascontiguousarray(arrays[name])
        ins[f"in_{name}"] = a
        args.append(nc.dram_tensor(f"in_{name}", a.shape, mybir.dt.from_np(a.dtype), kind="ExternalInput").ap())
    out = nc.dram_tensor("out", (B, P, P), F32, kind="ExternalOutput").ap()
    build(nc, *args, out)
    return run_bass_kernel_spmd(nc, [ins], core_ids=[0]).results[0]["out"]
```

```python
from contextlib import ExitStack

import numpy as np

import concourse.bass as bass
from concourse import mybir

F32 = mybir.dt.float32
BF16 = mybir.dt.bfloat16
I32 = mybir.dt.int32
U8 = mybir.dt.uint8
ALU = mybir.AluOpType
ACT = mybir.ActivationFunctionType
AX_X = mybir.AxisListType.X

P = 128
B = 32
GB = 4
G = B // GB
W = GB * P
D = 32
Q = 8
NCH = P // Q
NJ = NCH * D // P
H = 16
DH = P // H
K_SPARSE = 32
TERMS_Q = (0, 1, 0, 2, 1, 0)
TERMS_K = (0, 0, 1, 0, 1, 2)
NT = len(TERMS_Q)
KR = NT * DH
SLOT = 64
NU = H // 2
NZ = H // 4
BIG = 1.0e30
BIAS_AT = 1
NT_RING = 8
SCALE = float(1.0 / np.sqrt(np.float32(DH)))

WCOLS = ["wg_x", "wg_ctx", "wsoma", "wtemp", "wout", "wq", "wk", "wv", "wo"]
COLS = ["bg", "bsoma", "btemp", "bq", "bk", "bmod", "bn1", "tau4"]
C_WN1 = len(COLS)
C_BLEND = C_WN1 + D
C_COLS = C_BLEND + D
R_TAU = 4 * P
R_U = R_TAU + D + 1
R_END = R_U + B
C_LT, C_LTM = 0, P
C_A = 2 * P
C_AM = C_A + NCH * D
C_P = C_AM + NCH * D
C_PM = C_P + D
C_T = C_PM + D
C_K = C_T + Q
C_END = C_K + P

VEC_STEPS = (["neg_abs_tau", "neg_relu_tau", "gate_biases", "mod_bias", "q_bias", "k_bias"]
             + [f"wn2_row{b}" for b in range(GB)]
             + ["log_decay", "lt", "blend_max", "blend_negmax", "decay_arg", "blend_sum", "blend_recip", "blend_4",
                "half_bw", "decay_p", "decay_a", "w_lag", "w_a", "w_rest", "w_mid", "w_b2", "key_no", "w_out",
                "ident_b", "idx_f", "mask_f", "idx_plus", "idx_masked"]
             + [f"hot{j}" for j in range(K_SPARSE)]
             + ["not_prior", "lam", "use", "not_use", "dense_lam", "cnt_one", "cnt_none"])
ACT_STEPS = ["exp_tau", "softplus", "lt", "exp_blend", "decay_p", "apow", "decay_a", "exp_u", "w_b3", "w_a1", "w_a3"]


def vec(name):
    return VEC_STEPS.index(name) + 1


def scal(name):
    return ACT_STEPS.index(name) + 1


def build(nc, x, w, wn2, cols, rows, consts, ident_in, idx, masks, out):
    with ExitStack() as ctx:
        def sb(name, shape, dt=F32):
            return ctx.enter_context(nc.sbuf_tensor(name, shape, dt))

        def sem(name):
            return ctx.enter_context(nc.semaphore(name))

        ident_sb = sb("ident_sb", [P, P])
        ident = ident_sb[:]
        w_sb = sb("w_sb", [P, len(WCOLS), P])
        wt = {n: w_sb[:, k, :] for k, n in enumerate(WCOLS)}
        wn2_sb = sb("wn2_sb", [P, P])
        wn2_row = sb("wn2_row", [P, GB, P])
        cols_sb = sb("cols_sb", [P, C_COLS])
        col = {n: cols_sb[:, k:k + 1] for k, n in enumerate(COLS)}
        wn1 = cols_sb[:, C_WN1:C_WN1 + D]
        bl = cols_sb[:, C_BLEND:C_BLEND + D]
        rows_sb = sb("rows_sb", [P, R_END])
        gamma, beta, bo, bv = [rows_sb[:, k * P:k * P + P] for k in range(4)]
        lt = sb("lt", [P, P])
        decay_a = sb("decay_a", [P, NCH, D])
        decay_p = sb("decay_p", [P, D])
        half_bw = sb("half_bw", [P, P])
        lag_a = sb("lag_a", [P, Q, P], BF16)
        lag_b = sb("lag_b", [P, Q, P], BF16)
        mod_pa = [sb(f"mod_pa{u}", [P, W], BF16) for u in range(2)]
        mod_pb = [sb(f"mod_pb{u}", [P, W], BF16) for u in range(2)]
        neg_lc = sb("neg_lc", [P, P])
        not_prior = sb("not_prior", [P, P])
        count_none = sb("count_none", [P, P])
        cnt1 = sb("count_min1", [P, P])
        lncnt = sb("lncnt", [P, P])
        use_b = sb("use_b", [P, B])
        dense_lam = sb("dense_lam", [P, B])
        hb = sb("hb", [P, 5])
        idx_i = sb("idx_i", [P, K_SPARSE], I32)
        masks_sb = sb("masks_sb", [P, P + K_SPARSE], U8)
        idx_m = sb("idx_m", [P, K_SPARSE])
        ident_b = sb("ident_b", [P, P], BF16)
        key_no = sb("key_no", [P, P])
        table_probe = sb("table_probe", [P, 1])
        lam, not_use = sb("lam", [P, B])[:], sb("not_use", [P, B])[:]
        idx_f, im_f = sb("idx_f", [P, K_SPARSE])[:], sb("im_f", [P, K_SPARSE])[:]
        x1b_all = sb("x1b_all", [P, B, P])
        v_all = sb("v_all", [P, B, P])
        q_parts = sb("q_parts", [P, 3, B * P], BF16)
        k_parts = sb("k_parts", [P, 3, B * P], BF16)
        stats = sb("stats", [P, 2, GB, 6])
        moments = sb("moments", [P, 2, GB, 2])
        vareps = sb("vareps", [P, 2, GB])
        rstd = sb("rstd", [P, 2, GB])
        minus_half = sb("minus_half", [P, GB])
        neg_max = sb("neg_max", [P, 2, H])
        rden = sb("rden", [P, 2, H])

        ARENA = 47 * W
        arena = sb("arena", [P, ARENA])
        at = [0]

        def take(n):
            at[0] += n
            assert at[0] <= ARENA, at[0]
            return arena[:, at[0] - n:at[0]]

        xT, th, ctxT, thd, bh = [], [], [], [], []
        somaT, h1T, modT, gT, gn, modn, mod_a, prod = [], [], [], [], [], [], [], []
        for u in range(2):
            four = take(4 * W)
            bh.append(four.rearrange("p (j n) -> p j n", j=NJ))
            xT.append(four[:, 0:W])
            th.append(four[:, W:2 * W])
            ctxT.append(four[:, 2 * W:3 * W])
            thd.append(four[:, 3 * W:4 * W])
            mod_a.append(take(4 * W))
        for u in range(2):
            somaT.append(take(W))
            h1T.append(take(P))
            modT.append(take(W))
            gT.append(take(W))
            gn.append(take(W))
            prod.append([take(W), take(W)])
            modn.append(take(P))
            weights_at = at[0] - 5 * W - P
        xn = [take(W) for _ in range(2)]
        xb, acc, x1g = [[take(W)] for _ in range(3)]
        take(2 * W)
        last_at = at[0]
        for bufs in (xb, acc, x1g):
            bufs.append(take(W))
        one_hot = arena[:, at[0]:at[0] + K_SPARSE * P // 2].bitcast(BF16).rearrange("p (j k) -> p j k", k=P)
        x1T = take(W)
        qk_f = [take(W), take(W)]
        rest = take(W)
        crn, temporalT, tg, sg, ln = gn, [p[1] for p in prod], modT, gT, acc
        mod_rest = [p[0] for p in prod]
        vx = [take(H * D).rearrange("p (h e) -> p h e", h=H) for _ in range(2)]
        nbias = [take(P) for _ in range(2)]
        dtmp = take(P)
        attn = [take(P) for _ in range(2)]
        attnT = [take(P) for _ in range(2)]

        at[0] = 0

        def take_stack():
            return [take(NU * W // 2).bitcast(BF16).rearrange("p (n t) -> p n t", n=NU) for _ in range(2)]

        stack = [take_stack()]
        prob = [take(W) for _ in range(4)]
        probT = [take(W) for _ in range(4)]
        neg_t = [take(W) for _ in range(NT_RING)]
        yout = [take(W).rearrange("p (b c) -> p b c", b=GB) for _ in range(2)]
        oT = [take(W) for _ in range(2)]
        stack.append(take_stack())
        assert at[0] <= last_at

        c_sb = mod_a[1][:, 0:C_END]
        assert C_END <= 4 * W
        pr = bh[1].rearrange("p j n -> p (j n)")
        nt = D + 2
        sp_a, sp_b, sp_c, sp_d, lna = [pr[:, 64 * k:64 * k + nt] for k in range(5)]
        bl_e, bl_m, bl_s, bl_r, bl_4 = pr[:, 320:352], pr[:, 352:353], pr[:, 353:354], pr[:, 354:355], pr[:, 384:512]
        exp_lt, exp_p, apow = pr[:, 640:768], pr[:, 768:800], pr[:, 800:808]
        arg_a = pr[:, 1024:1536]
        exp_a = pr[:, 1536:2048]
        tau34 = sb("tau34", [P, nt])
        weights = arena[:, weights_at:weights_at + 2 * Q * P]
        w_lag = weights[:, 0:Q * P].rearrange("p (q c) -> p q c", q=Q)
        w_rest = weights[:, Q * P:2 * Q * P].rearrange("p (q c) -> p q c", q=Q)
        w_mid = sb("w_mid", [P, Q, P], BF16)

        ps = [ctx.enter_context(nc.psum_tensor(f"ps{u}", [P, 4, W], F32)) for u in range(2)]

        def bank(u, k):
            return ps[u][:, k, :]

        names = (
            "small_loaded wn2_loaded const_loaded x_loaded0 x_loaded1 w_loaded idx_loaded vec_step act_step "
            "blend_turned "
            "half_set xT_ps xT_ready ctx_ps ctx_ready wg_ps h1_ps soma_ps gate_tanh h1_ready soma_ready modT_ps "
            "modn_begun modn_ps modT_tanh gated_ready modT_ready modn_ready mod_part1 mod_rest_ready mod_part2 "
            "mod_part3 mod_part1b mod_a_ready gn_ps gn_ready lag_ps prod_ready lag_added state_ps bh_ready "
            "cross_ps cross_ready crossT_ps temporal_ready temp_ps temp_tanh mixed_ready out_ps aggr_begun "
            "stats_ready moments_ready vareps_ready rstd_ready centred xb_ready x1_ready x1b_ready "
            "x1T_ps x1T_ready q_ps k_ps v_ps qk_f_ready part1_ready rest1_ready part2_ready part3_ready v_stored "
            "counts_ps table_loaded stack_loaded0 stack_loaded1 logits_begun score_ps negt_ready shifted "
            "prob_ready probT_ps "
            "probT_ready pv_ps oT_ready on_ps rden_ready attn_ready attnT_ps attnT_ready y_ps y_ready "
            "y_stored0 y_stored1 lncnt_ready neg_lc_ready v_copied bias_a bias_ready vx_zeroed ")
        s = {n: sem(n) for n in names.split()}
        block = ctx.enter_context(nc.Block())

        def at_start(i, m, before):
            return isinstance(i, int) and 2 * i + m < before

        def grp(i, m, k=1, c=0):
            return i * (2 * k) + (m * k + c)

        def group_cols(i, m):
            return bass.ds(i * (2 * W) + m * W, W)

        def group_rows(i, m):
            return bass.ds(i * (2 * GB) + m * GB, GB)

        def by_row(ap):
            return ap.rearrange("p (b c) -> p b c", b=GB)

        def each_row(ap):
            return ap.unsqueeze(1).broadcast_to([P, GB, P])

        def pipeline(eng, front, step, end):
            front(0, 0)
            for m in range(3):
                step(0, m)
            with eng.Fori(1, G // 2 - 1) as i:
                step(i, 1)
                step(i, 2)
            end()

        x_v = x.rearrange("b t c -> t b c")
        out_v = out.rearrange("b t c -> t b c")
        LAST = G // 2 - 1
        NB2 = 2 * GB

        PEELED = 4

        def row_no(i, n):
            return NB2 * i + n if isinstance(i, int) else PEELED

        def over_rows(eng, step):
            for n in range(PEELED):
                step(0, n)
            with eng.Fori(0, B // NB2 - 1) as i:
                for n in range(PEELED, PEELED + NB2):
                    step(i, n)
            for n in range(PEELED, NB2):
                step(B // NB2 - 1, n)

        def quads(i, c):
            return i * (NZ * NB2) + c

        @block.sync
        def _(sp):
            for dst, src, done in ((rows_sb[:], rows.broadcast_to([P, R_END]), "small_loaded"),
                                   (cols_sb[:], cols, "small_loaded"), (ident, ident_in, "small_loaded"),
                                   (by_row(xn[0]), x_v[:, 0:GB, :], "x_loaded0"), (wn2_sb[:], wn2, "wn2_loaded"),
                                   (c_sb, consts, "const_loaded"),
                                   (w_sb[:], w, "w_loaded"),
                                   (by_row(xn[1]), x_v[:, GB:2 * GB, :], "x_loaded1"),
                                   (idx_i[:], idx, "idx_loaded"), (masks_sb[:], masks, "idx_loaded")):
                sp.dma_start(dst, src).then_inc(s[done], 16)
            for u in range(2):
                sp.sem_inc(s[f"y_stored{u}"], 16)

            def load_x(i, m):
                sp.wait_ge(s["ctx_ps"], grp(i, m, 1, -1))
                sp.wait_ge(s["xb_ready"], grp(i, m, 1, -1))
                sp.dma_start(by_row(xn[m % 2]), x_v[:, group_rows(i, m), :]).then_inc(s[f"x_loaded{m % 2}"], 16)

            with sp.Fori(0, G // 2 - 1) as i:
                for m in (2, 3):
                    load_x(i, m)

            def load_stack(i, u):
                for which, (parts, terms) in enumerate(((q_parts, TERMS_Q), (k_parts, TERMS_K))):
                    for n, part in enumerate(terms):
                        for slot in range(2):
                            r0 = slot * SLOT + n * DH
                            dst = stack[u][which][r0:r0 + DH, :, :]
                            src = parts[slot * SLOT:(slot + 1) * SLOT, part, group_cols(i, u)]
                            sp.dma_start(dst, src).then_inc(s[f"stack_loaded{u}"], 16)

            def store(i, u):
                sp.wait_ge(s["y_ready"], i * NB2 + GB * (u + 1))
                sp.dma_start(out_v[:, group_rows(i, u), :], yout[u]).then_inc(s[f"y_stored{u}"], 16)

            sp.wait_ge(s["cross_ps"], G - 1)
            load_stack(0, 0)
            sp.wait_ge(s["out_ps"], G)
            sp.wait_ge(s["ctx_ps"], G)
            sp.wait_ge(s["xb_ready"], G)
            sp.wait_ge(s["x1b_ready"], G)
            load_stack(0, 1)

            def reload(i, u):
                sp.wait_ge(s["score_ps"], i * (NZ * NB2) + NZ * GB * (u + 1))
                load_stack(i + 1, u)
                store(i, u)

            sp.wait_ge(s["part3_ready"], 2 * (G - 2))
            with sp.Fori(0, G // 2 - 2) as i:
                for u in range(2):
                    reload(i, u)
            sp.wait_ge(s["part3_ready"], 2 * G)
            for u in range(2):
                reload(G // 2 - 2, u)
            for u in range(2):
                store(G // 2 - 1, u)
            sp.wait_ge(s["y_stored0"], 16 + 16 * G // 2)
            sp.wait_ge(s["y_stored1"], 16 + 16 * G // 2)

        @block.tensor
        def _(pe):
            pe.wait_ge(s["small_loaded"], 48)

            def four(out_bank, lhs, rhs, done):
                for b in range(GB):
                    cs = slice(b * P, b * P + P)
                    mm = pe.matmul(out_bank[:, cs], lhs(cs), rhs(cs), start=True, stop=True)
                mm.then_inc(s[done], 1)

            def turned(out_bank, src, done):
                for b in range(GB):
                    cs = slice(b * P, b * P + P)
                    mm = pe.transpose(out_bank[:, cs], src[:, cs], ident)
                mm.then_inc(s[done], 1)

            def f_x(i, m):
                u = m % 2
                pe.wait_ge(s[f"x_loaded{u}"], i * 16 + 16 * (m // 2 + 1))
                if not at_start(i, m, 2):
                    pe.wait_ge(s["temporal_ready"], grp(i, m, 1, -1))
                turned(bank(u, 0), xn[u], "xT_ps")

            def f_context(i, m):
                u = m % 2
                if at_start(i, m, 1):
                    pe.wait_ge(s["vec_step"], vec("lt"))
                four(bank(u, 1), lambda cs: xn[u][:, cs], lambda cs: lt[:], "ctx_ps")

            def f_soma(i, m):
                u = m % 2
                if at_start(i, m, 1):
                    pe.wait_ge(s["w_loaded"], 16)
                pe.wait_ge(s["xT_ready"], grp(i, m, 1, 1))
                pe.matmul(bank(u, 0), wt["wsoma"], xT[u], start=True, stop=True).then_inc(s["soma_ps"], 1)

            def f_gate(i, m):
                u = m % 2
                pe.matmul(bank(u, 2), wt["wg_x"], xT[u], start=True, stop=False)
                pe.wait_ge(s["ctx_ready"], grp(i, m, 1, 1))
                pe.matmul(bank(u, 2), wt["wg_ctx"], ctxT[u], start=False, stop=True).then_inc(s["wg_ps"], 1)

            def f_hidden(i, m):
                u = m % 2
                if not at_start(i, m, 2):
                    pe.wait_ge(s["centred"], grp(i, m, GB, -GB))
                for b in range(GB):
                    mm = pe.matmul(bank(u, 3)[b * D:b * D + D, 0:P], wn1, xT[u][:, b * P:b * P + P],
                                   start=True, stop=True)
                mm.then_inc(s["h1_ps"], 1)

            def f_modulation(i, m):
                u = m % 2
                pe.wait_ge(s["h1_ready"], grp(i, m, 1, 1))
                if at_start(i, m, 1):
                    pe.wait_ge(s["vec_step"], vec(f"wn2_row{GB - 1}"))
                for b in range(GB):
                    mm = pe.matmul(bank(u, 1)[:, b * P:b * P + P], wn2_row[:, b, :], h1T[u], start=True, stop=True)
                mm.then_inc(s["modT_ps"], 1)

            def f_modulation_n(i, m):
                u = m % 2
                pe.wait_ge(s["modT_ready"], grp(i, m, 1, 1))
                pe.sem_inc(s["modn_begun"], 1)
                for b in range(GB):
                    mm = pe.transpose(bank(u, 1)[:, b * D:b * D + D], modT[u][0:D, b * P:b * P + P], ident[0:D, 0:D])
                mm.then_inc(s["modn_ps"], 1)

            def f_gated(i, m):
                u = m % 2
                pe.wait_ge(s["gated_ready"], grp(i, m, 1, 1))
                turned(bank(u, 2), gT[u], "gn_ps")

            def f_lags(i, m, lags):
                u = m % 2
                for lag in lags:
                    if lag == 0:
                        pe.wait_ge(s["soma_ready"], grp(i, m, 1, 1))
                        pe.wait_ge(s["mod_part3"], grp(i, m, 1, 1))
                        pe.wait_ge(s["mod_part1b"], grp(i, m, 1, 1))
                        if at_start(i, m, 1):
                            pe.wait_ge(s["vec_step"], vec("w_b2"))
                            pe.wait_ge(s["act_step"], scal("w_a3"))
                    if lag == 1:
                        pe.wait_ge(s["modn_ready"], grp(i, m, 1, 1))
                    if lag >= 2:
                        pe.wait_ge(s["prod_ready"], grp(i, m, Q, lag - 1))
                    pe.matmul(bank(u, lag % 2), lag_a[:, lag, :], mod_pa[u][:], start=True, stop=False)
                    pe.matmul(bank(u, lag % 2), lag_b[:, lag, :], mod_pb[u][:], start=False, stop=True)\
                        .then_inc(s["lag_ps"], 1)

            def b_states(i, m, blocks):
                u = m % 2
                for j in blocks:
                    if j == 0:
                        pe.wait_ge(s["gn_ready"], grp(i, m, 1, 1))
                    if j == 0 and not at_start(i, m, 2):
                        pe.wait_ge(s["v_stored"], grp(i, m, 1, -1))
                        pe.wait_ge(s["qk_f_ready"], grp(i, m, 2, -2))
                    if j == 1 and at_start(i, m, 2) and not at_start(i, m, 1):
                        pe.wait_ge(s["vec_step"], vec("cnt_none"))
                    if j >= 2:
                        pe.wait_ge(s["bh_ready"], grp(i, m, NJ, j - 1))
                    for b in range(GB):
                        if j == 0:
                            pe.wait_ge(s["mod_a_ready"], grp(i, m, GB, b + 1))
                        cs = slice(b * P, b * P + P)
                        mm = pe.matmul(bank(u, 2 + j % 2)[:, cs], mod_a[u][:, b * W + j * P:b * W + j * P + P],
                                       gn[u][:, cs], start=True, stop=True)
                    mm.then_inc(s["state_ps"], 1)

            def b_cross(i, m):
                u = m % 2
                pe.wait_ge(s["prod_ready"], grp(i, m, Q, Q))
                pe.wait_ge(s["bh_ready"], grp(i, m, NJ, NJ))
                for j in range(NJ):
                    mm = pe.matmul(bank(u, 0)[32 * j:32 * j + 32, :], decay_p[:], bh[u][:, j, :],
                                   start=True, stop=True)
                mm.then_inc(s["cross_ps"], 1)

            def b_crossT(i, m):
                u = m % 2
                pe.wait_ge(s["cross_ready"], grp(i, m, 1, 1))
                turned(bank(u, 1), crn[u], "crossT_ps")

            def b_gate(i, m):
                u = m % 2
                pe.wait_ge(s["temporal_ready"], grp(i, m, 1, 1))
                pe.matmul(bank(u, 2), wt["wtemp"], temporalT[u], start=True, stop=True).then_inc(s["temp_ps"], 1)

            def b_out(i, m):
                u = m % 2
                if at_start(i, m, 1):
                    pe.wait_ge(s["vec_step"], vec("w_out"))
                pe.wait_ge(s["mixed_ready"], grp(i, m, 1, 1))
                four(bank(u, 3), lambda cs: sg[u][:, cs], lambda cs: wt["wout"], "out_ps")

            def c_x1T(i, m):
                u = m % 2
                pe.wait_ge(s["x1_ready"], grp(i, m, 1, 1))
                pe.wait_ge(s["h1_ready"], (G if isinstance(i, int) and 2 * i + m > G - 3 else grp(i, m, 1, 3)))
                pe.wait_ge(s["centred"], grp(i, m, GB, GB))
                turned(bank(u, 3), x1g[u], "x1T_ps")

            def c_q(i, m):
                u = m % 2
                pe.wait_ge(s["gn_ready"], (G if isinstance(i, int) and 2 * i + m > G - 3 else grp(i, m, 1, 3)))
                pe.wait_ge(s["temp_tanh"], grp(i, m, 1, 1))
                pe.wait_ge(s["x1T_ready"], grp(i, m, 1, 1))
                pe.matmul(bank(u, 2), wt["wq"], x1T, start=True, stop=True).then_inc(s["q_ps"], 1)

            def c_k(i, m):
                u = m % 2
                pe.matmul(bank(u, 3), wt["wk"], x1T, start=True, stop=True).then_inc(s["k_ps"], 1)

            def c_qk(i, m):
                c_q(i, m)
                c_k(i, m)

            def c_v(i, m):
                u = m % 2
                pe.wait_ge(s["qk_f_ready"], grp(i, m, 2, 1))
                four(bank(u, 2), lambda cs: x1T[:, cs], lambda cs: wt["wv"], "v_ps")

            def front(i, m):
                f_x(i, m)
                f_soma(i, m)
                pe.wait_ge(s["vec_step"], vec("blend_4"))
                pe.transpose(bank(1, 0)[:, 0:P], bl_4, ident).then_inc(s["blend_turned"], 1)
                f_context(i, m)
                f_hidden(i, m)
                f_gate(i, m)
                f_modulation(i, m)
                f_modulation_n(i, m)
                f_gated(i, m)
                f_lags(i, m, range(Q))

            def step(i, m):
                f_x(i, m + 1)
                f_context(i, m + 1)
                b_states(i, m, range(0, 2))
                f_soma(i, m + 1)
                f_gate(i, m + 1)
                f_hidden(i, m + 1)
                b_states(i, m, range(2, NJ))
                f_modulation(i, m + 1)
                if not at_start(i, m, 1):
                    c_x1T(i, m - 1)
                f_gated(i, m + 1)
                b_cross(i, m)
                f_modulation_n(i, m + 1)
                if not at_start(i, m, 1):
                    c_q(i, m - 1)
                b_crossT(i, m)
                if not at_start(i, m, 1):
                    c_k(i, m - 1)
                f_lags(i, m + 1, range(0, 2))
                b_gate(i, m)
                f_lags(i, m + 1, range(2, 4))
                if not at_start(i, m, 1):
                    c_v(i, m - 1)
                f_lags(i, m + 1, range(4, 6))
                b_out(i, m)
                f_lags(i, m + 1, range(6, Q))
                if at_start(i, m, 1):
                    pe.wait_ge(s["vec_step"], vec(f"hot{K_SPARSE - 1}"))
                    for j in range(K_SPARSE):
                        mm = pe.matmul(bank(1, 3)[:, 0:P], ident_b[:], one_hot[:, j, :],
                                       start=(j == 0), stop=(j == K_SPARSE - 1))
                    mm.then_inc(s["counts_ps"], 1)

            def end():
                b_states(LAST, 1, range(NJ))
                b_cross(LAST, 1)
                scores(0, 0, 0)
                b_crossT(LAST, 1)
                scores(0, 0, 1)
                b_gate(LAST, 1)
                c_x1T(LAST, 0)
                scores(0, 0, 2)
                b_out(LAST, 1)
                c_qk(LAST, 0)
                scores(0, 0, 3)
                c_v(LAST, 0)
                scores(0, 1, 0)

            def scores(i, n, z):
                u, b = n // GB % 2, n % GB
                if row_no(i, n) == 0 and z == 0:
                    pe.wait_ge(s["temporal_ready"], G - 1)
                if z == 0 and b == 0:
                    pe.wait_ge(s[f"stack_loaded{u}"], i * (16 * 4 * NT) + 16 * 4 * NT * (1 + n // NB2))
                c = NZ * n + z
                if isinstance(i, int) and NZ * NB2 * i + c < 2:
                    pass
                else:
                    pe.wait_ge(s["negt_ready"], i * (4 * NZ * NB2) + 4 * (c - 1))
                for k in range(4):
                    r0, tile = SLOT * (z % 2), 4 * (z // 2) + k
                    mm = pe.matmul(ps[0][:, c % 2, k * P:k * P + P],
                                   stack[u][0][r0:r0 + KR, tile, b * P:b * P + P],
                                   stack[u][1][r0:r0 + KR, tile, b * P:b * P + P], start=True, stop=True)
                mm.then_inc(s["score_ps"], 1)

            def turn(i, n, z):
                c = NZ * n + z
                pe.wait_ge(s["prob_ready"], quads(i, c + 1))
                if row_no(i, n) == 0 and z == 0:
                    pe.wait_ge(s["qk_f_ready"], 2 * (G - 1))
                    pe.wait_ge(s["v_stored"], G - 1)
                if not (isinstance(i, int) and NZ * NB2 * i + c < 2):
                    pe.wait_ge(s["probT_ready"], quads(i, c - 1))
                for k in range(4):
                    mm = pe.transpose(ps[0][:, 2 + c % 2, k * P:k * P + P], prob[c % 4][:, k * P:k * P + P], ident)
                mm.then_inc(s["probT_ps"], 1)

            def values(i, n, z):
                c = NZ * n + z
                pe.wait_ge(s["probT_ready"], quads(i, c + 1))
                if z == 0:
                    pe.wait_ge(s["v_copied"], i * NB2 + (n + 1))
                    if row_no(i, n) == 0:
                        pe.wait_ge(s["temporal_ready"], G)
                    if row_no(i, n) >= 2:
                        pe.wait_ge(s["oT_ready"], i * NB2 + (n - 1))
                for k in range(4):
                    mm = pe.matmul(ps[1][32 * k:32 * k + 32, n % 2, z * P:z * P + P], vx[n % 2][:, 4 * z + k, :],
                                   probT[c % 4][:, k * P:k * P + P], start=True, stop=True)
                mm.then_inc(s["pv_ps"], 1)

            def turn_o(i, n):
                if row_no(i, n) == 0:
                    pe.wait_ge(s["v_stored"], G)
                pe.wait_ge(s["oT_ready"], i * NB2 + (n + 1))
                if not (isinstance(i, int) and NB2 * i + n < 1):
                    pe.wait_ge(s["attn_ready"], i * NB2 + n)
                for z in range(NZ):
                    mm = pe.transpose(ps[1][:, 2, z * P:z * P + P], oT[n % 2][:, z * P:z * P + P], ident)
                mm.then_inc(s["on_ps"], 1)

            def turn_attn(i, n):
                if row_no(i, n) == 0:
                    pe.wait_ge(s["qk_f_ready"], 2 * G)
                pe.wait_ge(s["attn_ready"], i * NB2 + (n + 1))
                if row_no(i, n) >= 1:
                    pe.wait_ge(s["attnT_ready"], i * NB2 + n)
                    pe.wait_ge(s["y_ready"], i * NB2 + n)
                pe.transpose(ps[1][:, 3, 0:P], attn[n % 2], ident).then_inc(s["attnT_ps"], 1)

            def project(i, n):
                pe.wait_ge(s["attnT_ready"], i * NB2 + (n + 1))
                pe.matmul(ps[1][:, 3, P:2 * P], attnT[n % 2], wt["wo"], start=True, stop=True).then_inc(s["y_ps"], 1)

            closing = {(0, 2): c_x1T, (0, 3): c_qk, (1, 1): c_v}

            def row_step(i, n):
                for z in range(NZ):
                    if (row_no(i, n), z) in closing:
                        closing[row_no(i, n), z](LAST, 1)
                    turn(i, n, z)
                    row, quad = n + 1 + (z + 1) // NZ, (z + 1) % NZ
                    if row_no(i, row) < B:
                        scores(i, row, quad)
                    if z >= 2:
                        values(i, n, z - 2)
                    elif row_no(i, n) >= 1:
                        values(i, n - 1, NZ - 2 + z)
                    if z == 1 and row_no(i, n) >= 2:
                        turn_attn(i, n - 2)
                    if z == 3 and row_no(i, n) >= 1:
                        turn_o(i, n - 1)
                    if z == 3 and row_no(i, n) >= 2:
                        project(i, n - 2)

            pipeline(pe, front, step, end)
            over_rows(pe, row_step)
            i = B // NB2 - 1
            for z in (NZ - 2, NZ - 1):
                values(i, NB2 - 1, z)
            turn_attn(i, NB2 - 2)
            project(i, NB2 - 2)
            turn_o(i, NB2 - 1)
            turn_attn(i, NB2 - 1)
            project(i, NB2 - 1)

        @block.scalar
        def _(act):
            act.wait_ge(s["x1b_ready"], 1)
            act.activation(table_probe[:], minus_half[:, 0:1], ACT.Exp).then_inc(s["table_loaded"], 1)
            act.wait_ge(s["small_loaded"], 48)
            act.wait_ge(s["vec_step"], vec("neg_abs_tau"))
            act.activation(sp_b, sp_a, ACT.Exp).then_inc(s["act_step"], 1)
            act.wait_ge(s["act_step"], scal("exp_tau"))
            act.activation(sp_c, sp_b, ACT.Ln, bias=1.0).then_inc(s["act_step"], 1)

            def f_x(i, m):
                u = m % 2
                act.wait_ge(s["xT_ps"], grp(i, m, 1, 1))
                act.activation(xT[u], bank(u, 0), ACT.Copy).then_inc(s["xT_ready"], 1)

            def f_context(i, m):
                u = m % 2
                act.wait_ge(s["ctx_ps"], grp(i, m, 1, 1))
                act.activation(ctxT[u], bank(u, 1), ACT.Copy).then_inc(s["ctx_ready"], 1)

            def f_soma(i, m):
                u = m % 2
                act.wait_ge(s["soma_ps"], grp(i, m, 1, 1))
                act.activation(somaT[u], bank(u, 0), ACT.Gelu, bias=col["bsoma"]).then_inc(s["soma_ready"], 1)

            def f_gate(i, m):
                u = m % 2
                if at_start(i, m, 1):
                    act.wait_ge(s["vec_step"], vec("mod_bias"))
                act.wait_ge(s["wg_ps"], grp(i, m, 1, 1))
                act.activation(th[u], bank(u, 2), ACT.Tanh, bias=hb[:, 0:1], scale=0.5).then_inc(s["gate_tanh"], 1)

            def f_hidden(i, m):
                u = m % 2
                act.wait_ge(s["h1_ps"], grp(i, m, 1, 1))
                act.activation(h1T[u], bank(u, 3)[:, 0:P], ACT.Gelu, bias=col["bn1"]).then_inc(s["h1_ready"], 1)

            def f_modulation(i, m):
                u = m % 2
                act.wait_ge(s["modT_ps"], grp(i, m, 1, 1))
                act.activation(thd[u], bank(u, 1), ACT.Tanh, bias=hb[:, 2:3], scale=0.5).then_inc(s["modT_tanh"], 1)

            def f_modulation_n(i, m):
                u = m % 2
                act.wait_ge(s["modn_ps"], grp(i, m, 1, 1))
                act.activation(modn[u], bank(u, 1)[:, 0:P], ACT.Copy).then_inc(s["modn_ready"], 1)
                act.wait_ge(s["modT_ready"], grp(i, m, 1, 1))
                act.activation(mod_pb[u][64:96, :], modT[u][64:96, :], ACT.Copy).then_inc(s["mod_part1b"], 1)

            def f_gated(i, m):
                u = m % 2
                act.wait_ge(s["gn_ps"], grp(i, m, 1, 1))
                act.activation(gn[u], bank(u, 2), ACT.Copy).then_inc(s["gn_ready"], 1)

            def b_cross(i, m):
                u = m % 2
                act.wait_ge(s["cross_ps"], grp(i, m, 1, 1))
                act.activation(crn[u], bank(u, 0), ACT.Copy).then_inc(s["cross_ready"], 1)

            def b_gate(i, m):
                u = m % 2
                act.wait_ge(s["temp_ps"], grp(i, m, 1, 1))
                act.activation(tg[u], bank(u, 2), ACT.Tanh, bias=hb[:, 1:2], scale=0.5).then_inc(s["temp_tanh"], 1)

            def c_x1T(i, m):
                u = m % 2
                act.wait_ge(s["x1T_ps"], grp(i, m, 1, 1))
                if at_start(i, m, 1):
                    act.wait_ge(s["counts_ps"], 1)
                else:
                    act.wait_ge(s["v_ps"], grp(i, m, 1, 0))
                act.activation(x1T, bank(u, 3), ACT.Copy).then_inc(s["x1T_ready"], 1)

            def c_qk(i, m):
                u = m % 2
                for n, (done, args) in enumerate((("q_ps", dict(bias=hb[:, 3:4], scale=-SCALE)),
                                                  ("k_ps", dict(bias=hb[:, 4:5])))):
                    if not at_start(i, m, 1):
                        act.wait_ge(s["rest1_ready"], grp(i, m, 2, n - 1))
                    act.wait_ge(s[done], grp(i, m, 1, 1))
                    act.activation(qk_f[n], bank(u, 2 + n), ACT.Identity, **args).then_inc(s["qk_f_ready"], 1)
                for n, parts in enumerate((q_parts, k_parts)):
                    act.wait_ge(s["qk_f_ready"], grp(i, m, 2, n + 1))
                    act.activation(parts[:, 0, group_cols(i, m)], qk_f[n], ACT.Copy).then_inc(s["part1_ready"], 1)

            def front(i, m):
                f_x(i, m)
                act.wait_ge(s["const_loaded"], 16)
                act.wait_ge(s["vec_step"], vec("log_decay"))
                act.activation(exp_lt, c_sb[:, C_LT:C_LT + P], ACT.Exp, scale=lna[:, D + 1:D + 2])\
                    .then_inc(s["act_step"], 1)
                act.wait_ge(s["vec_step"], vec("blend_negmax"))
                act.activation(bl_e, bl, ACT.Exp, bias=bl_m).then_inc(s["act_step"], 1)
                act.activation(exp_p, c_sb[:, C_P:C_P + D], ACT.Exp, scale=lna[:, D:D + 1]).then_inc(s["act_step"], 1)
                act.activation(apow, c_sb[:, C_T:C_T + Q], ACT.Exp, scale=lna[:, D:D + 1]).then_inc(s["act_step"], 1)
                act.wait_ge(s["vec_step"], vec("decay_arg"))
                act.activation(exp_a, arg_a, ACT.Exp).then_inc(s["act_step"], 1)
                act.activation(lam, rows_sb[:, R_U:R_U + B], ACT.Exp, scale=-5.0).then_inc(s["act_step"], 1)
                f_soma(i, m)
                f_context(i, m)
                f_hidden(i, m)
                act.wait_ge(s["vec_step"], vec("w_lag"))
                act.activation(lag_b[96:128], w_lag[96:128], ACT.Copy).then_inc(s["act_step"], 1)
                f_gate(i, m)
                f_modulation(i, m)
                act.wait_ge(s["vec_step"], vec("w_rest"))
                for r0 in (32, 96):
                    act.activation(lag_a[r0:r0 + 32], w_rest[r0:r0 + 32], ACT.Copy).then_inc(s["act_step"], 1)
                f_modulation_n(i, m)
                f_gated(i, m)

            def step(i, m):
                f_x(i, m + 1)
                f_context(i, m + 1)
                f_soma(i, m + 1)
                f_gate(i, m + 1)
                f_hidden(i, m + 1)
                f_modulation(i, m + 1)
                if not at_start(i, m, 1):
                    c_x1T(i, m - 1)
                f_gated(i, m + 1)
                b_cross(i, m)
                f_modulation_n(i, m + 1)
                if not at_start(i, m, 1):
                    c_qk(i, m - 1)
                b_gate(i, m)
                if at_start(i, m, 2) and m == 1:
                    act.wait_ge(s["vec_step"], vec("cnt_one"))
                    act.activation(lncnt[:], cnt1[:], ACT.Ln).then_inc(s["lncnt_ready"], 1)

            def end():
                b_cross(LAST, 1)
                b_gate(LAST, 1)
                c_x1T(LAST, 0)
                exps(0, 0, 0)
                exps(0, 0, 1)
                c_qk(LAST, 0)
                exps(0, 0, 2)

            def exps(i, n, z):
                c = NZ * n + z
                if not (isinstance(i, int) and NZ * NB2 * i + c < 4):
                    act.wait_ge(s["probT_ps"], quads(i, c - 3))
                elif c == 0:
                    act.wait_ge(s["cross_ps"], G)
                act.wait_ge(s["shifted"], quads(i, c + 1))
                act.activation(prob[c % 4], neg_t[c % NT_RING], ACT.Exp, scale=-1.0).then_inc(s["prob_ready"], 1)

            def move(i, n, z):
                c = NZ * n + z
                act.wait_ge(s["probT_ps"], quads(i, c + 1))
                if not (isinstance(i, int) and NZ * NB2 * i + c < 4):
                    act.wait_ge(s["pv_ps"], quads(i, c - 3))
                act.activation(probT[c % 4], ps[0][:, 2 + c % 2, :], ACT.Copy).then_inc(s["probT_ready"], 1)

            def move_o(i, n):
                act.wait_ge(s["pv_ps"], i * (NZ * NB2) + NZ * (n + 1))
                act.activation(oT[n % 2], ps[1][:, n % 2, :], ACT.Copy).then_inc(s["oT_ready"], 1)

            def move_attn(i, n):
                act.wait_ge(s["attnT_ps"], i * NB2 + (n + 1))
                act.activation(attnT[n % 2], ps[1][:, 3, 0:P], ACT.Copy).then_inc(s["attnT_ready"], 1)

            closing = {(0, 2): c_x1T, (0, 3): c_qk}

            def row_step(i, n):
                for z in range(NZ):
                    if (row_no(i, n), z) in closing:
                        closing[row_no(i, n), z](LAST, 1)
                    move(i, n, z)
                    if z == 2 and row_no(i, n) >= 2:
                        move_attn(i, n - 2)
                    if z == 2 and row_no(i, n) >= 1:
                        move_o(i, n - 1)
                    row, quad = n + (z + 3) // NZ, (z + 3) % NZ
                    if row_no(i, row) < B:
                        exps(i, row, quad)

            pipeline(act, front, step, end)
            over_rows(act, row_step)
            move_o(B // NB2 - 1, NB2 - 1)
            move_attn(B // NB2 - 1, NB2 - 2)
            move_attn(B // NB2 - 1, NB2 - 1)

        @block.vector
        def _(dve):
            count = [0]

            def pro(name, ins, waited=True):
                count[0] += 1
                assert VEC_STEPS[count[0] - 1] == name, name
                ins.then_inc(s["vec_step"], 1)
                if waited:
                    dve.wait_ge(s["vec_step"], count[0])

            for n in range(2):
                dve.memset(mod_pb[n][0:64, :], 0.0).then_inc(s["half_set"], 1)
            dve.memset(lag_b[0:64], 0.0).then_inc(s["half_set"], 1)
            dve.memset(wn2_row[:], 0.0).then_inc(s["half_set"], 1)
            dve.wait_ge(s["small_loaded"], 48)
            dve.tensor_copy(tau34[:, 0:D], rows_sb[:, R_TAU:R_TAU + D]).then_inc(s["half_set"], 1)
            dve.tensor_copy(tau34[:, D:D + 1], col["tau4"]).then_inc(s["half_set"], 1)
            dve.tensor_copy(tau34[:, D + 1:D + 2], rows_sb[:, R_TAU + D:R_TAU + D + 1]).then_inc(s["half_set"], 1)
            dve.wait_ge(s["half_set"], 7)
            pro("neg_abs_tau", dve.scalar_tensor_tensor(sp_a, tau34[:], -1.0, tau34[:], ALU.mult, ALU.min))
            pro("neg_relu_tau", dve.tensor_scalar(sp_d, tau34[:], 0.0, -1.0, ALU.max, ALU.mult))
            pro("gate_biases", dve.tensor_scalar(hb[:, 0:2], cols_sb[:, 0:3:2], 0.5, None, ALU.mult))
            pro("mod_bias", dve.tensor_scalar(hb[:, 2:3], col["bmod"], 0.5, None, ALU.mult))
            pro("q_bias", dve.tensor_scalar(hb[:, 3:4], col["bq"], -SCALE, None, ALU.mult))
            pro("k_bias", dve.tensor_copy(hb[:, 4:5], col["bk"]))
            dve.wait_ge(s["wn2_loaded"], 16)
            for b in range(GB):
                rows_of = slice(b * D, b * D + D)
                pro(f"wn2_row{b}", dve.tensor_copy(wn2_row[rows_of, b, :], wn2_sb[rows_of, :]), waited=b == GB - 1)
            dve.wait_ge(s["act_step"], scal("softplus"))
            pro("log_decay", dve.tensor_tensor(lna, sp_d, sp_c, ALU.subtract))
            dve.wait_ge(s["act_step"], scal("lt"))
            pro("lt", dve.tensor_tensor(lt[:], exp_lt, c_sb[:, C_LTM:C_LTM + P], ALU.mult))
            pro("blend_max", dve.tensor_reduce(bl_s, bl, AX_X, ALU.max))
            pro("blend_negmax", dve.tensor_scalar(bl_m, bl_s, -1.0, None, ALU.mult))
            pro("decay_arg", dve.tensor_tensor(arg_a.rearrange("p (k d) -> p k d", d=D),
                                               c_sb[:, C_A:C_A + NCH * D].rearrange("p (k d) -> p k d", d=D),
                                               lna[:, 0:D].unsqueeze(1).broadcast_to([P, NCH, D]), ALU.mult))
            dve.wait_ge(s["act_step"], scal("exp_blend"))
            pro("blend_sum", dve.tensor_reduce(bl_s, bl_e, AX_X, ALU.add))
            pro("blend_recip", dve.reciprocal(bl_r, bl_s))
            pro("blend_4", dve.tensor_scalar(bl_4.rearrange("p (k d) -> p k d", d=D),
                                             bl_e.unsqueeze(1).broadcast_to([P, 4, D]), bl_r, 0.5,
                                             ALU.mult, ALU.mult))
            dve.wait_ge(s["blend_turned"], 1)
            pro("half_bw", dve.tensor_copy(half_bw[:], bank(1, 0)[:, 0:P]))
            dve.wait_ge(s["act_step"], scal("decay_a"))
            pro("decay_p", dve.tensor_tensor(decay_p[:], exp_p, c_sb[:, C_PM:C_PM + D], ALU.mult))
            pro("decay_a", dve.tensor_tensor(decay_a[:].rearrange("p k d -> p (k d)"), exp_a,
                                             c_sb[:, C_AM:C_AM + NCH * D], ALU.mult))
            pro("w_lag", dve.tensor_tensor(w_lag, half_bw[:].unsqueeze(1).broadcast_to([P, Q, P]),
                                           apow.unsqueeze(2).broadcast_to([P, Q, P]), ALU.mult))
            pro("w_a", dve.tensor_copy(lag_a[:], w_lag))
            pro("w_rest", dve.tensor_tensor(w_rest, w_lag, lag_a[:], ALU.subtract))
            pro("w_mid", dve.tensor_copy(w_mid[64:96], w_rest[64:96]))
            pro("w_b2", dve.tensor_tensor(lag_b[64:96], w_rest[64:96], w_mid[64:96], ALU.subtract))

            def neighbours():
                pro("key_no", dve.tensor_copy(key_no[:], c_sb[:, C_K:C_K + P]))
                pro("w_out", dve.tensor_scalar(wt["wout"], wt["wout"], 0.5, None, ALU.mult))
                dve.wait_ge(s["idx_loaded"], 32)
                pro("ident_b", dve.tensor_copy(ident_b[:], ident))
                pro("idx_f", dve.tensor_copy(idx_f, idx_i[:]))
                pro("mask_f", dve.tensor_copy(im_f, masks_sb[:, P:P + K_SPARSE]))
                pro("idx_plus", dve.scalar_tensor_tensor(idx_m[:], idx_f, 1.0, im_f, ALU.add, ALU.mult))
                pro("idx_masked", dve.tensor_scalar(idx_m[:], idx_m[:], -1.0, None, ALU.add))

            def one_hots(first, last):
                for j in range(first, last):
                    pro(f"hot{j}", dve.tensor_scalar(one_hot[:, j, :], key_no[:], idx_m[:, j:j + 1],
                                                     None, ALU.is_equal), waited=False)

            def late_tables():
                pro("not_prior", dve.tensor_scalar(not_prior[:], masks_sb[:, 0:P], -1.0, 1.0, ALU.mult, ALU.add),
                    waited=False)
                dve.wait_ge(s["act_step"], scal("exp_u"))
                pro("lam", dve.tensor_scalar(lam, lam, 10.0, None, ALU.mult))
                pro("use", dve.tensor_scalar(use_b[:], lam, 1.0, None, ALU.is_ge))
                pro("not_use", dve.tensor_scalar(not_use, use_b[:], -1.0, 1.0, ALU.mult, ALU.add))
                pro("dense_lam", dve.tensor_tensor(dense_lam[:], not_use, lam, ALU.mult))
                dve.wait_ge(s["counts_ps"], 1)
                pro("cnt_one", dve.tensor_scalar(cnt1[:], bank(1, 3)[:, 0:P], 1.0, None, ALU.max), waited=False)
                pro("cnt_none", dve.tensor_scalar(count_none[:], bank(1, 3)[:, 0:P], 0.0, BIG,
                                                  ALU.is_equal, ALU.mult))

            def row_of(ap, i, n):
                return ap[:, i * NB2 + n:i * NB2 + n + 1] if isinstance(i, int) else ap[:, bass.ds(i * NB2 + n, 1)]

            def bias_terms(i, n):
                if row_no(i, n) >= 1:
                    dve.wait_ge(s["bias_ready"], i * NB2 + n)
                dve.tensor_tensor(nbias[n % 2], neg_lc[:], row_of(use_b, i, n).broadcast_to([P, P]), ALU.mult)\
                    .then_inc(s["bias_a"], 1)
                dve.tensor_tensor(dtmp, not_prior[:], row_of(dense_lam, i, n).broadcast_to([P, P]), ALU.mult)\
                    .then_inc(s["bias_a"], 1)

            def bias_sum(i, n):
                dve.wait_ge(s["bias_a"], i * (2 * NB2) + 2 * (n + 1))
                dve.tensor_tensor(nbias[n % 2], nbias[n % 2], dtmp, ALU.add).then_inc(s["bias_ready"], 1)

            def chunks(ap, a, b):
                return ap.rearrange("p (n q) -> p n q", q=Q)[:, :, a:b]

            def packed(ap, lag):
                return ap[:, 0:(W // Q) * (Q - lag)].rearrange("p (n q) -> p n q", q=Q - lag)

            def f_gated(i, m):
                u = m % 2
                dve.wait_ge(s["xT_ready"], grp(i, m, 1, 1))
                dve.wait_ge(s["gate_tanh"], grp(i, m, 1, 1))
                dve.scalar_tensor_tensor(gT[u], th[u], 1.0, xT[u], ALU.add, ALU.mult).then_inc(s["gated_ready"], 1)

            def f_modulation(i, m):
                u = m % 2
                dve.wait_ge(s["modT_tanh"], grp(i, m, 1, 1))
                dve.tensor_scalar(modT[u], thd[u], 0.5, 1.0, ALU.mult, ALU.add).then_inc(s["modT_ready"], 1)
                dve.tensor_scalar(mod_pa[u][:], thd[u], 0.5, 1.0, ALU.mult, ALU.add).then_inc(s["mod_part1"], 1)
                dve.wait_ge(s["modT_ready"], grp(i, m, 1, 1))
                dve.wait_ge(s["mod_part1"], grp(i, m, 1, 1))
                dve.tensor_tensor(mod_rest[u], modT[u], mod_pa[u][:], ALU.subtract).then_inc(s["mod_rest_ready"], 1)
                dve.wait_ge(s["mod_rest_ready"], grp(i, m, 1, 1))
                dve.tensor_copy(mod_pa[u][64:128, :], mod_rest[u][64:128, :]).then_inc(s["mod_part2"], 1)
                dve.wait_ge(s["mod_part2"], grp(i, m, 1, 1))
                dve.tensor_tensor(mod_pb[u][96:128, :], mod_rest[u][96:128, :], mod_pa[u][96:128, :],
                                  ALU.subtract).then_inc(s["mod_part3"], 1)

            def f_lags(i, m, lags):
                u = m % 2
                for lag in lags:
                    dve.wait_ge(s["lag_ps"], grp(i, m, Q, lag + 1))
                    if lag == 0:
                        if not at_start(i, m, 2):
                            dve.wait_ge(s["x1_ready"], grp(i, m, 1, -1))
                        dve.tensor_tensor(acc[u], bank(u, 0), gT[u], ALU.mult).then_inc(s["prod_ready"], 1)
                        continue
                    if lag >= 3:
                        dve.wait_ge(s["lag_added"], grp(i, m, Q - 1, lag - 2))
                    dve.tensor_tensor(packed(prod[u][lag % 2], lag), chunks(bank(u, lag % 2), 0, Q - lag),
                                      chunks(gT[u], 0, Q - lag), ALU.mult).then_inc(s["prod_ready"], 1)

            def b_states(i, m, blocks):
                u = m % 2
                for j in blocks:
                    dve.wait_ge(s["state_ps"], grp(i, m, NJ, j + 1))
                    dve.tensor_tensor(by_row(bh[u][:, j, :]), by_row(bank(u, 2 + j % 2)), each_row(half_bw[:]),
                                      ALU.mult).then_inc(s["bh_ready"], 1)

            def b_temporal(i, m):
                u = m % 2
                dve.wait_ge(s["lag_added"], grp(i, m, Q - 1, Q - 1))
                dve.wait_ge(s["crossT_ps"], grp(i, m, 1, 1))
                dve.tensor_tensor(temporalT[u], bank(u, 1), acc[u], ALU.add).then_inc(s["temporal_ready"], 1)

            def b_mixed(i, m):
                u = m % 2
                dve.wait_ge(s["temp_tanh"], grp(i, m, 1, 1))
                dve.scalar_tensor_tensor(sg[u], tg[u], 1.0, somaT[u], ALU.add, ALU.mult)\
                    .then_inc(s["mixed_ready"], 1)

            def c_moments(i, m):
                u = m % 2
                dve.wait_ge(s["out_ps"], grp(i, m, 1, 1))
                for b in range(GB):
                    dve.bn_stats(stats[:, u, b, :], bank(u, 3)[:, b * P:b * P + P]).then_inc(s["stats_ready"], 1)
                dve.wait_ge(s["stats_ready"], grp(i, m, GB, GB))
                dve.sem_inc(s["aggr_begun"], 1)
                for b in range(GB):
                    dve.bn_aggr(moments[:, u, b, :], stats[:, u, b, :]).then_inc(s["moments_ready"], 1)
                dve.wait_ge(s["moments_ready"], grp(i, m, GB, GB))
                dve.tensor_scalar(vareps[:, u, :], moments[:, u, :, 1], 1e-5, None, ALU.add)\
                    .then_inc(s["vareps_ready"], 1)

            def c_centre(i, m):
                u = m % 2
                for b in range(GB):
                    cs = slice(b * P, b * P + P)
                    dve.scalar_tensor_tensor(ln[u][:, cs], bank(u, 3)[:, cs], moments[:, u, b, 0:1], gamma,
                                             ALU.subtract, ALU.mult).then_inc(s["centred"], 1)

            def c_residual(i, m):
                u = m % 2
                dve.wait_ge(s["rstd_ready"], grp(i, m, 1, 1))
                dve.wait_ge(s["xb_ready"], grp(i, m, 1, 1))
                dve.wait_ge(s["centred"], grp(i, m, GB, GB))
                if not at_start(i, m, 2):
                    dve.wait_ge(s["x1b_ready"], grp(i, m, 1, 0))
                for b in range(GB):
                    cs = slice(b * P, b * P + P)
                    ins = dve.scalar_tensor_tensor(x1g[u][:, cs], ln[u][:, cs], rstd[:, u, b:b + 1], xb[u][:, cs],
                                                   ALU.mult, ALU.add)
                ins.then_inc(s["x1_ready"], 1)

            def c_rest(i, m, n):
                dve.wait_ge(s["part1_ready"], grp(i, m, 2, n + 1))
                if not (n == 0 and at_start(i, m, 1)):
                    dve.wait_ge(s["part3_ready"], grp(i, m, 2, n))
                dve.tensor_tensor(rest, qk_f[n], (q_parts, k_parts)[n][:, 0, group_cols(i, m)], ALU.subtract)\
                    .then_inc(s["rest1_ready"], 1)

            def c_part2(i, m, n):
                dve.wait_ge(s["rest1_ready"], grp(i, m, 2, n + 1))
                dve.tensor_copy((q_parts, k_parts)[n][:, 1, group_cols(i, m)], rest).then_inc(s["part2_ready"], 1)

            def c_part3(i, m, n):
                parts, col_ = (q_parts, k_parts)[n], group_cols(i, m)
                dve.wait_ge(s["part2_ready"], grp(i, m, 2, n + 1))
                dve.tensor_tensor(parts[:, 2, col_], rest, parts[:, 1, col_], ALU.subtract)\
                    .then_inc(s["part3_ready"], 1)

            def c_split(i, m, n):
                c_rest(i, m, n)
                c_part2(i, m, n)
                c_part3(i, m, n)

            def c_values(i, m):
                u = m % 2
                dve.wait_ge(s["v_ps"], grp(i, m, 1, 1))
                dve.tensor_tensor(v_all[:, group_rows(i, m), :], by_row(bank(u, 2)), each_row(bv), ALU.add)\
                    .then_inc(s["v_stored"], 1)

            def front(i, m):
                f_gated(i, m)
                f_modulation(i, m)
                f_lags(i, m, range(Q))
                dve.wait_ge(s["act_step"], scal("w_a3"))

            def step(i, m):
                closes, counts = not at_start(i, m, 1), at_start(i, m, 1)
                b_states(i, m, range(0, 1))
                if closes:
                    c_residual(i, m - 1)
                b_states(i, m, range(1, 2))
                if counts:
                    neighbours()
                    one_hots(0, 8)
                f_gated(i, m + 1)
                b_states(i, m, range(2, NJ))
                if counts:
                    one_hots(8, 12)
                f_modulation(i, m + 1)
                b_temporal(i, m)
                if counts:
                    one_hots(12, 16)
                if not at_start(i, m, 2):
                    c_rest(i, m - 2, 1)
                f_lags(i, m + 1, range(0, 2))
                if counts:
                    one_hots(16, 20)
                if not at_start(i, m, 2):
                    c_part2(i, m - 2, 1)
                f_lags(i, m + 1, range(2, 3))
                if counts:
                    one_hots(20, 24)
                if not at_start(i, m, 2):
                    c_part3(i, m - 2, 1)
                f_lags(i, m + 1, range(3, 4))
                if counts:
                    one_hots(24, 28)
                b_mixed(i, m)
                f_lags(i, m + 1, range(4, 5))
                if counts:
                    one_hots(28, K_SPARSE)
                if closes:
                    c_values(i, m - 1)
                    c_rest(i, m - 1, 0)
                f_lags(i, m + 1, range(5, 6))
                if closes:
                    c_part2(i, m - 1, 0)
                    c_part3(i, m - 1, 0)
                f_lags(i, m + 1, range(6, 7))
                c_moments(i, m)
                f_lags(i, m + 1, range(7, Q))
                c_centre(i, m)
                if counts:
                    late_tables()
                if at_start(i, m, 2) and m == 1:
                    dve.wait_ge(s["lncnt_ready"], 1)
                    dve.tensor_tensor(neg_lc[:], count_none[:], lncnt[:], ALU.subtract).then_inc(s["neg_lc_ready"], 1)
                    dve.wait_ge(s["neg_lc_ready"], 1)
                    for n in range(2):
                        bias_terms(0, n)
                        bias_sum(0, n)

            def end():
                b_states(LAST, 1, range(NJ))
                c_residual(LAST, 0)
                logits(0, 0, 0)
                b_temporal(LAST, 1)
                c_split(LAST, -1, 1)
                logits(0, 0, 1)
                b_mixed(LAST, 1)
                logits(0, 0, 2)
                c_moments(LAST, 1)
                c_centre(LAST, 1)
                c_values(LAST, 0)
                logits(0, 0, 3)
                c_residual(LAST, 1)

            def logits(i, n, z):
                c = NZ * n + z
                if z == 0:
                    dve.wait_ge(s["bias_ready"], i * NB2 + (n + 1))
                if row_no(i, n) == 0 and z == 0:
                    dve.wait_ge(s["out_ps"], G - 1)
                if not (isinstance(i, int) and NZ * NB2 * i + c < NT_RING):
                    dve.wait_ge(s["prob_ready"], quads(i, c - NT_RING + 1))
                dve.wait_ge(s["score_ps"], quads(i, c + 1))
                dve.sem_inc(s["logits_begun"], 1)
                for k in range(4):
                    cs = slice(k * P, k * P + P)
                    h = 4 * z + k
                    dve.tensor_tensor_reduce(out=neg_t[c % NT_RING][:, cs], in0=ps[0][:, c % 2, cs], in1=nbias[n % 2],
                                             scale=1.0, scalar=3.0e38, op0=ALU.add, op1=ALU.min,
                                             accum_out=neg_max[:, n % 2, h:h + 1]).then_inc(s["negt_ready"], 1)

            def normalise(i, n):
                dve.wait_ge(s["on_ps"], i * NB2 + (n + 1))
                o = ps[1][:, 2, :].rearrange("p (h e) -> p h e", e=D)
                dve.reciprocal(rden[:, n % 2, :], o[:, :, DH]).then_inc(s["rden_ready"], 1)
                dve.wait_ge(s["rden_ready"], i * NB2 + (n + 1))
                dve.tensor_tensor(attn[n % 2].rearrange("p (h e) -> p h e", e=DH), o[:, :, 0:DH],
                                  rden[:, n % 2, :].unsqueeze(2).broadcast_to([P, H, DH]), ALU.mult)\
                    .then_inc(s["attn_ready"], 1)

            def result(i, n):
                dve.wait_ge(s["y_ps"], i * NB2 + (n + 1))
                if row_no(i, n) == 0:
                    dve.wait_ge(s["x1b_ready"], G + 1)
                u, b = n // GB % 2, n % GB
                if b == 0:
                    dve.wait_ge(s[f"y_stored{u}"], i * 16 + 16 * (n // NB2 + 1))
                dve.tensor_tensor(yout[u][:, b, :], ps[1][:, 3, P:2 * P], x1b_all[:, i * NB2 + n, :]
                                  if isinstance(i, int) else x1b_all[:, bass.ds(i * NB2 + n, 1), :]
                                  .rearrange("p a c -> p (a c)"), ALU.add).then_inc(s["y_ready"], 1)

            closing = {(1, 2): [(c_values, 1)]}
            for slot, *args in (((0, 1), 0, 0), ((0, 3), 0, 1), ((2, 1), 1, 0), ((2, 3), 1, 1)):
                closing.setdefault(slot, []).append((c_split, *args))

            def row_step(i, n):
                for z in range(NZ):
                    if row_no(i, n + 1) < B:
                        logits(i, n + 1, z)
                    if z == 0 and row_no(i, n) >= 2:
                        normalise(i, n - 2)
                    if z == 0 and row_no(i, n) >= 3:
                        result(i, n - 3)
                    if z == BIAS_AT and row_no(i, n + 2) < B:
                        bias_terms(i, n + 2)
                    if z == BIAS_AT + 1 and row_no(i, n + 2) < B:
                        bias_sum(i, n + 2)
                    for piece, *args in closing.get((row_no(i, n), z), ()):
                        piece(LAST, *args)

            pipeline(dve, front, step, end)
            over_rows(dve, row_step)
            i = B // NB2 - 1
            normalise(i, NB2 - 2)
            result(i, NB2 - 3)
            result(i, NB2 - 2)
            normalise(i, NB2 - 1)
            result(i, NB2 - 1)

        @block.gpsimd
        def _(pool):
            pool.memset(minus_half[:], -0.5).then_inc(s["x1b_ready"], 1)
            for n in range(2):
                pool.memset(vx[n], 0.0).then_inc(s["vx_zeroed"], 1)
            pool.wait_ge(s["vx_zeroed"], 2)
            for n in range(2):
                pool.memset(vx[n][:, :, DH:DH + 1], 1.0).then_inc(s["vx_zeroed"], 1)
            pool.wait_ge(s["x1b_ready"], 1)
            pool.wait_ge(s["vx_zeroed"], 4)
            pool.wait_ge(s["small_loaded"], 48)

            def f_inputs(i, m):
                u = m % 2
                if not at_start(i, m, 2):
                    pool.wait_ge(s["x1_ready"], grp(i, m, 1, -1))
                pool.wait_ge(s[f"x_loaded{u}"], i * 16 + 16 * (m // 2 + 1))
                pool.tensor_tensor(by_row(xb[u]), by_row(xn[u]), each_row(beta), ALU.add).then_inc(s["xb_ready"], 1)

            def f_decayed(i, m, rows_):
                u = m % 2
                pool.wait_ge(s["modn_ready"], grp(i, m, 1, 1))
                for b in rows_:
                    pool.tensor_tensor(mod_a[u][:, b * W:b * W + W].rearrange("p (k d) -> p k d", d=D), decay_a[:],
                                       modn[u][:, b * D:b * D + D].unsqueeze(1).broadcast_to([P, NCH, D]),
                                       ALU.mult).then_inc(s["mod_a_ready"], 1)

            def f_lags(i, m, lags):
                u = m % 2
                for lag in lags:
                    pool.wait_ge(s["prod_ready"], grp(i, m, Q, lag + 1))
                    if lag >= 2:
                        pool.wait_ge(s["lag_added"], grp(i, m, Q - 1, lag - 1))
                    a = acc[u].rearrange("p (n q) -> p n q", q=Q)[:, :, lag:Q]
                    pr_ = prod[u][lag % 2][:, 0:(W // Q) * (Q - lag)].rearrange("p (n q) -> p n q", q=Q - lag)
                    pool.tensor_tensor(a, a, pr_, ALU.add).then_inc(s["lag_added"], 1)

            def c_rstd(i, m):
                u = m % 2
                pool.wait_ge(s["vareps_ready"], grp(i, m, 1, 1))
                pool.tensor_tensor(rstd[:, u, :], vareps[:, u, :], minus_half[:], ALU.pow).then_inc(s["rstd_ready"], 1)

            def c_keep(i, m):
                u = m % 2
                pool.wait_ge(s["x1_ready"], grp(i, m, 1, 1))
                pool.tensor_tensor(x1b_all[:, group_rows(i, m), :], by_row(x1g[u]), each_row(bo), ALU.add)\
                    .then_inc(s["x1b_ready"], 1)

            def f_accumulate(i, m):
                f_decayed(i, m, range(0, 3))
                f_lags(i, m, range(1, 5))
                f_decayed(i, m, range(3, GB))
                f_lags(i, m, range(5, Q))

            def front(i, m):
                f_inputs(i, m)
                f_accumulate(i, m)

            def step(i, m):
                f_inputs(i, m + 1)
                if not at_start(i, m, 1):
                    c_keep(i, m - 1)
                f_accumulate(i, m + 1)
                c_rstd(i, m)
                if at_start(i, m, 3) and m == 2:
                    prepare_values(0, 0)

            def prepare_values(i, n):
                if row_no(i, n) == 0:
                    pool.wait_ge(s["v_stored"], 2)
                if row_no(i, n) == 2:
                    pool.wait_ge(s["v_stored"], G)
                if row_no(i, n) >= 2:
                    pool.wait_ge(s["pv_ps"], i * (NZ * NB2) + NZ * (n - 1))
                v = v_all[:, i * NB2 + n, :] if isinstance(i, int) else \
                    v_all[:, bass.ds(i * NB2 + n, 1), :].rearrange("p a c -> p (a c)")
                pool.tensor_copy(vx[n % 2][:, :, 0:DH], v.rearrange("p (h e) -> p h e", e=DH))\
                    .then_inc(s["v_copied"], 1)

            def shift(i, n, z):
                c = NZ * n + z
                pool.wait_ge(s["negt_ready"], i * (4 * NZ * NB2) + 4 * (c + 1))
                t4 = neg_t[c % NT_RING].rearrange("p (h k) -> p h k", h=4)
                pool.tensor_tensor(t4, t4, neg_max[:, n % 2, 4 * z:4 * z + 4].unsqueeze(2).broadcast_to([P, 4, P]),
                                   ALU.subtract).then_inc(s["shifted"], 1)

            def row_step(i, n):
                for z in range(NZ):
                    if row_no(i, n + 1) < B:
                        shift(i, n + 1, z)
                    if z == 1 and row_no(i, n + 1) < B:
                        prepare_values(i, n + 1)

            def end():
                shift(0, 0, 0)
                shift(0, 0, 1)
                c_keep(LAST, 0)
                c_rstd(LAST, 1)
                shift(0, 0, 2)
                shift(0, 0, 3)
                c_keep(LAST, 1)

            pipeline(pool, front, step, end)
            over_rows(pool, row_step)


_ORDER = ["x", "w", "wn2", "cols", "rows", "consts", "ident", "idx", "masks"]


def shape_constants():
    c = np.zeros((P, C_END), np.float32)
    r = np.arange(P)
    lag = r[None, :] - r[:, None]
    c[:, C_LT:C_LT + P] = np.maximum(lag, 0)
    c[:, C_LTM:C_LTM + P] = lag >= 0
    to_start = np.repeat(np.arange(NCH) * Q, D)[None, :] - r[:, None]
    c[:, C_A:C_A + NCH * D] = np.maximum(to_start, 0)
    c[:, C_AM:C_AM + NCH * D] = to_start > 0
    inside = np.arange(D)[None, :] - (r // D * Q)[:, None]
    c[:, C_P:C_P + D] = np.clip(inside, 0, Q)
    c[:, C_PM:C_PM + D] = (inside >= 0) & (inside < Q)
    c[:, C_T:C_T + Q] = np.arange(Q)[None, :]
    c[:, C_K:C_K + P] = r[None, :]
    return c


def kernel(x, condB_tauraws, cond_256, condB_bn2, cond_1024, itok_Sx32_0_1023, condB_uprev, mask_SxS_bk0,
           mask_Sx32_bk1, L0_cond_tau_ctx, L0_cond_Wg, L0_cond_bg, L0_cond_Wn1, L0_cond_bn1, L0_cond_Wsoma,
           L0_cond_bsoma, L0_cond_Wtemp, L0_cond_btemp, L0_cond_Wout, L0_cond_gamma, L0_cond_beta, L1_cond_Wq,
           L1_cond_bq, L1_cond_Wk, L1_cond_bk, L1_cond_Wv, L1_cond_bv, L1_cond_Wo, L1_cond_bo):
    import concourse.bacc as bacc
    from concourse.bass_utils import run_bass_kernel_spmd

    def arr(a):
        return np.asarray(a)

    order = np.arange(P).reshape(NZ // 2, 2, 4, DH).transpose(1, 3, 0, 2).reshape(P)
    wg = arr(L0_cond_Wg).T
    weights = [wg[0:P], wg[P:2 * P], arr(L0_cond_Wsoma).T, arr(L0_cond_Wtemp).T, arr(L0_cond_Wout).T,
               arr(L1_cond_Wq)[order].T, arr(L1_cond_Wk)[order].T, arr(L1_cond_Wv).T, arr(L1_cond_Wo).T]
    taus = arr(condB_tauraws)
    four = P // D
    bn2 = np.tile(arr(condB_bn2), four)
    columns = {"bg": L0_cond_bg, "bsoma": L0_cond_bsoma, "btemp": L0_cond_btemp, "bq": arr(L1_cond_bq)[order],
               "bk": arr(L1_cond_bk)[order], "bmod": bn2, "bn1": np.tile(arr(L0_cond_bn1), four),
               "tau4": np.tile(taus, four)}
    arrays = {
        "x": arr(x),
        "w": np.stack(weights, axis=1),
        "wn2": np.tile(arr(cond_256).T, (four, four)),
        "cols": np.concatenate([np.stack([arr(columns[n]) for n in COLS], axis=1), arr(L0_cond_Wn1).T,
                                arr(cond_1024).T], axis=1),
        "rows": np.concatenate([arr(L0_cond_gamma), arr(L0_cond_beta), arr(L1_cond_bo), arr(L1_cond_bv), taus,
                                arr(L0_cond_tau_ctx).reshape(1), arr(condB_uprev)])[None, :],
        "consts": shape_constants(),
        "ident": np.eye(P, dtype=np.float32),
        "idx": arr(itok_Sx32_0_1023),
        "masks": np.concatenate([arr(mask_SxS_bk0), arr(mask_Sx32_bk1)], axis=1),
    }
    nc = bacc.Bacc("TRN2", target_bir_lowering=False, num_devices=1)
    ins, args = {}, []
    for name in _ORDER:
        a = np.ascontiguousarray(arrays[name])
        ins[f"in_{name}"] = a
        args.append(nc.dram_tensor(f"in_{name}", a.shape, mybir.dt.from_np(a.dtype), kind="ExternalInput").ap())
    out = nc.dram_tensor("out", (B, P, P), F32, kind="ExternalOutput").ap()
    build(nc, *args, out)
    return run_bass_kernel_spmd(nc, [ins], core_ids=[0]).results[0]["out"]
```
